# Optimizing a Trainium2 kernel written in Bass

```python
import numpy as np
import jax
import jax.numpy as jnp

def _softmax(x, axis=-1):
    return jax.nn.softmax(x, axis=axis)

def _gelu(x):
    return jax.nn.gelu(x, approximate=True)

def _silu(x):
    return jax.nn.silu(x)

def _sigmoid(x):
    return jax.nn.sigmoid(x)

def _layernorm(x, axis=-1, eps=1e-05):
    m = jnp.mean(x, axis=axis, keepdims=True)
    v = jnp.var(x, axis=axis, keepdims=True)
    return (x - m) / jnp.sqrt(v + eps)

def _scatter_add(tgt, idx, src, axis=0):
    return tgt.at[idx].add(src)

def _segment_sum(src, seg, n):
    return jax.ops.segment_sum(src, seg, n)
kernel_name = 'mk_hybrid_d1_jaxref_r8_7645d6'

def setup_inputs(seed: int=0):
    np.random.seed(seed)
    _w = jnp.asarray

    def _L0_attn_a_setup():
        import jax, jax.numpy as jnp
        import numpy as np
        B, N, DM, H = (1, 256, 128, 16)
        CURV = 1.0
        key = jax.random.key(seed)
        ks = jax.random.split(key, 5)
        s = 1.0 / np.sqrt(DM)
        x = jax.random.normal(ks[0], (B, N, DM), dtype=jnp.float32)
        Wq = jax.random.uniform(ks[1], (DM, DM), jnp.float32, -s, s)
        Wk = jax.random.uniform(ks[2], (DM, DM), jnp.float32, -s, s)
        Wv = jax.random.uniform(ks[3], (DM, DM), jnp.float32, -s, s)
        Wo = jax.random.uniform(ks[4], (DM, DM), jnp.float32, -s, s)
        return {'x': x, 'Wq': Wq, 'Wk': Wk, 'Wv': Wv, 'Wo': Wo}
    _L0_attn_a_in = _L0_attn_a_setup()

    def _L0_attn_b_setup():
        import jax, jax.numpy as jnp
        import numpy as np
        DIM = 128
        NHEAD = 16
        HEAD_DIM = DIM // NHEAD

        def _rotate_half(t):
            h = t.shape[-1] // 2
            return jnp.concatenate([-t[..., h:], t[..., :h]], axis=-1)
        key = jax.random.key(seed)
        ks = jax.random.split(key, 5)
        B, N = (4, 256)
        return {'x': jax.random.normal(ks[0], (B, N, DIM), dtype=jnp.float32), 'qkv_w': jax.random.normal(ks[1], (3 * DIM, DIM), dtype=jnp.float32) * 0.02, 'qkv_b': jax.random.normal(ks[2], (3 * DIM,), dtype=jnp.float32) * 0.02, 'proj_w': jax.random.normal(ks[3], (DIM, DIM), dtype=jnp.float32) * 0.02, 'proj_b': jax.random.normal(ks[4], (DIM,), dtype=jnp.float32) * 0.02}
    _L0_attn_b_in = _L0_attn_b_setup()

    def _L0_ffn_setup():
        import jax, jax.numpy as jnp
        import numpy as np
        H = 128
        I = 64
        E = 64
        G = 8
        TOPK_GROUP = 4
        K = 8
        I_SH = 128
        SCALE = 2.5

        def _route(x, router_w, e_bias):
            T = x.shape[0]
            scores = jax.nn.sigmoid(x.astype(jnp.float32) @ router_w.T.astype(jnp.float32))
            sfc = jax.lax.stop_gradient(scores) + e_bias[None, :]
            group_scores = jax.lax.top_k(sfc.reshape(T, G, E // G), 2)[0].sum(-1)
            _, gidx = jax.lax.top_k(group_scores, TOPK_GROUP)
            gmask = jax.nn.one_hot(gidx, G, dtype=sfc.dtype).sum(1)
            smask = jnp.repeat(gmask, E // G, axis=1)
            masked = jnp.where(smask > 0, sfc, 0.0)
            _, topk_idx = jax.lax.top_k(masked, K)
            w = jnp.take_along_axis(scores, topk_idx, axis=1)
            w = w / (w.sum(-1, keepdims=True) + 1e-20)
            return (topk_idx, w * SCALE)
        key = jax.random.key(seed)
        ks = jax.random.split(key, 9)
        s = 0.02
        return {'hidden_states': jax.random.normal(ks[0], (2, 128, H), jnp.float32), 'router_w': jax.random.normal(ks[1], (E, H), jnp.float32) * s, 'e_bias': jnp.zeros((E,), jnp.float32), 'Wg': jax.random.normal(ks[2], (E, H, I), jnp.float32) * s, 'Wu': jax.random.normal(ks[3], (E, H, I), jnp.float32) * s, 'Wd': jax.random.normal(ks[4], (E, I, H), jnp.float32) * s, 'SWg': jax.random.normal(ks[5], (H, I_SH), jnp.float32) * s, 'SWu': jax.random.normal(ks[6], (H, I_SH), jnp.float32) * s, 'SWd': jax.random.normal(ks[7], (I_SH, H), jnp.float32) * s}
    _L0_ffn_in = _L0_ffn_setup()
    _d = {'L0_attn_a_x': _L0_attn_a_in['x'], 'L0_attn_a_Wq': _L0_attn_a_in['Wq'], 'L0_attn_a_Wk': _L0_attn_a_in['Wk'], 'L0_attn_a_Wv': _L0_attn_a_in['Wv'], 'L0_attn_a_Wo': _L0_attn_a_in['Wo'], 'L0_attn_b_qkv_w': _L0_attn_b_in['qkv_w'], 'L0_attn_b_qkv_b': _L0_attn_b_in['qkv_b'], 'L0_attn_b_proj_w': _L0_attn_b_in['proj_w'], 'L0_attn_b_proj_b': _L0_attn_b_in['proj_b'], 'L0_ffn_router_w': _L0_ffn_in['router_w'], 'L0_ffn_e_bias': _L0_ffn_in['e_bias'], 'L0_ffn_Wg': _L0_ffn_in['Wg'], 'L0_ffn_Wu': _L0_ffn_in['Wu'], 'L0_ffn_Wd': _L0_ffn_in['Wd'], 'L0_ffn_SWg': _L0_ffn_in['SWg'], 'L0_ffn_SWu': _L0_ffn_in['SWu'], 'L0_ffn_SWd': _L0_ffn_in['SWd']}
    _x0 = _d['L0_attn_a_x']
    _d['L0_attn_a_x'] = jax.random.normal(jax.random.fold_in(jax.random.key(seed), 1), (8, 256, 128), dtype=_x0.dtype)
    del _x0
    return _d

def reference(L0_attn_a_x, L0_attn_a_Wq, L0_attn_a_Wk, L0_attn_a_Wv, L0_attn_a_Wo, L0_attn_b_qkv_w, L0_attn_b_qkv_b, L0_attn_b_proj_w, L0_attn_b_proj_b, L0_ffn_router_w, L0_ffn_e_bias, L0_ffn_Wg, L0_ffn_Wu, L0_ffn_Wd, L0_ffn_SWg, L0_ffn_SWu, L0_ffn_SWd):

    def _L0_attn_a_ref(x, Wq, Wk, Wv, Wo):
        import jax, jax.numpy as jnp
        import numpy as np
        B, N, DM, H = (1, 256, 128, 16)
        CURV = 1.0
        b, n, d = x.shape
        hd = d // H

        def split_heads(t):
            return t.reshape(b, n, H, hd).transpose(0, 2, 1, 3)
        q = split_heads(x @ Wq.T)
        k = split_heads(x @ Wk.T)
        v = split_heads(x @ Wv.T)
        q_norm_sq = jnp.sum(q * q, axis=-1, keepdims=True)
        k_norm_sq = jnp.sum(k * k, axis=-1)[:, :, None, :]
        qk = jnp.einsum('bhnd,bhmd->bhnm', q, k)
        diff_sq = jnp.maximum(q_norm_sq + k_norm_sq - 2.0 * qk, 0.0)
        denom = jnp.maximum((1.0 - CURV * q_norm_sq) * (1.0 - CURV * k_norm_sq), 1e-06)
        cosh_arg = jnp.maximum(1.0 + 2.0 * CURV * diff_sq / denom, 1.0)
        distance = jnp.where(cosh_arg > 1.0, jnp.arccosh(jnp.maximum(cosh_arg, 1.0 + 1e-12)), 0.0)
        attn = jax.nn.softmax(-distance, axis=-1)
        out = jnp.einsum('bhnm,bhmd->bhnd', attn, v)
        out = out.transpose(0, 2, 1, 3).reshape(b, n, d)
        return out @ Wo.T

    def _L0_attn_b_ref(x, qkv_w, qkv_b, proj_w, proj_b):
        import jax, jax.numpy as jnp
        import numpy as np
        DIM = 128
        NHEAD = 16
        HEAD_DIM = DIM // NHEAD

        def _rotate_half(t):
            h = t.shape[-1] // 2
            return jnp.concatenate([-t[..., h:], t[..., :h]], axis=-1)
        B, N, D = x.shape
        H, hd = (NHEAD, HEAD_DIM)
        qkv = x @ qkv_w.T + qkv_b
        qkv = jnp.transpose(qkv.reshape(B, N, 3, H, hd), (2, 0, 3, 1, 4))
        q, k, v = (qkv[0], qkv[1], qkv[2])
        inv_freq = 1.0 / 10000.0 ** (jnp.arange(0, hd, 2, dtype=x.dtype) / hd)
        pos = jnp.arange(N, dtype=x.dtype)
        freqs = pos[:, None] * inv_freq[None, :]
        emb = jnp.concatenate([freqs, freqs], axis=-1)
        cos = jnp.cos(emb)[None, None, None]
        sin = jnp.sin(emb)[None, None, None]
        q = q * cos + _rotate_half(q) * sin
        k = k * cos + _rotate_half(k) * sin
        scale = hd ** (-0.5)
        attn = jnp.einsum('abhqd,abhkd->abhqk', q, k) * scale
        attn = jax.nn.softmax(attn, axis=-1)
        out = jnp.einsum('abhqk,bhkd->abhqd', attn, v)
        out = jnp.swapaxes(out, 1, 2).reshape(B, N, D)
        out = out @ proj_w.T + proj_b
        return out

    def _L0_ffn_ref(hidden_states, router_w, e_bias, Wg, Wu, Wd, SWg, SWu, SWd):
        import jax, jax.numpy as jnp
        import numpy as np
        H = 128
        I = 64
        E = 64
        G = 8
        TOPK_GROUP = 4
        K = 8
        I_SH = 128
        SCALE = 2.5

        def _route(x, router_w, e_bias):
            T = x.shape[0]
            scores = jax.nn.sigmoid(x.astype(jnp.float32) @ router_w.T.astype(jnp.float32))
            sfc = jax.lax.stop_gradient(scores) + e_bias[None, :]
            group_scores = jax.lax.top_k(sfc.reshape(T, G, E // G), 2)[0].sum(-1)
            _, gidx = jax.lax.top_k(group_scores, TOPK_GROUP)
            gmask = jax.nn.one_hot(gidx, G, dtype=sfc.dtype).sum(1)
            smask = jnp.repeat(gmask, E // G, axis=1)
            masked = jnp.where(smask > 0, sfc, 0.0)
            _, topk_idx = jax.lax.top_k(masked, K)
            w = jnp.take_along_axis(scores, topk_idx, axis=1)
            w = w / (w.sum(-1, keepdims=True) + 1e-20)
            return (topk_idx, w * SCALE)
        orig_shape = hidden_states.shape
        x = hidden_states.reshape(-1, orig_shape[-1])
        T = x.shape[0]
        topk_idx, topk_w = _route(x, router_w, e_bias)
        coef = jnp.zeros((T, E), topk_w.dtype).at[jnp.arange(T)[:, None], topk_idx].add(topk_w)
        g = jnp.einsum('th,ehi->tei', x, Wg)
        u = jnp.einsum('th,ehi->tei', x, Wu)
        h = jax.nn.silu(g) * u * coef[:, :, None]
        moe_out = jnp.einsum('tei,eih->th', h, Wd)
        shared = jax.nn.silu(x @ SWg) * (x @ SWu) @ SWd
        return (moe_out + shared).reshape(orig_shape)
    x = L0_attn_a_x
    x = x + _L0_attn_a_ref(_layernorm(x, axis=-1), L0_attn_a_Wq, L0_attn_a_Wk, L0_attn_a_Wv, L0_attn_a_Wo)
    x = x + _L0_ffn_ref(_layernorm(x, axis=-1), L0_ffn_router_w, L0_ffn_e_bias, L0_ffn_Wg, L0_ffn_Wu, L0_ffn_Wd, L0_ffn_SWg, L0_ffn_SWu, L0_ffn_SWd)
    x = x + _L0_attn_b_ref(_layernorm(x, axis=-1), L0_attn_b_qkv_w, L0_attn_b_qkv_b, L0_attn_b_proj_w, L0_attn_b_proj_b)
    x = x + _L0_ffn_ref(_layernorm(x, axis=-1), L0_ffn_router_w, L0_ffn_e_bias, L0_ffn_Wg, L0_ffn_Wu, L0_ffn_Wd, L0_ffn_SWg, L0_ffn_SWu, L0_ffn_SWd)
    return x

_drawn_inputs = setup_inputs


def setup_inputs(seed=0):
    import zlib

    import numpy as np

    out = dict(_drawn_inputs(seed))
    spreads = {'L0_ffn_e_bias': (0.0, 0.8)}
    factors = {'L0_attn_b_qkv_w': 8.0,
     'L0_attn_b_qkv_b': 8.0,
     'L0_attn_b_proj_w': 8.0,
     'L0_attn_b_proj_b': 2.773,
     'L0_ffn_router_w': 8.0,
     'L0_ffn_Wg': 7.774,
     'L0_ffn_Wu': 7.687,
     'L0_ffn_Wd': 7.728,
     'L0_ffn_SWg': 4.85,
     'L0_ffn_SWu': 4.826,
     'L0_ffn_SWd': 4.803}
    for name, (base, spread) in spreads.items():
        noise = np.random.default_rng([zlib.crc32(name.encode()), seed]).standard_normal(out[name].shape)
        drawn = base * np.exp(spread * noise) if base else spread * noise
        out[name] = jnp.asarray(drawn.astype(out[name].dtype))
    for name, factor in factors.items():
        out[name] = (out[name] * factor).astype(out[name].dtype)
    return out
```

```python
from contextlib import ExitStack

import concourse.bass as bass
from concourse import mybir

F32 = mybir.dt.float32
F32R = mybir.dt.float32r
ALU = mybir.AluOpType
ACT = mybir.ActivationFunctionType
AX_X = mybir.AxisListType.X

P = 128
B, N = 8, 256
T = B * N
TILES = T // P
H, HD = 16, 8
E, I = 64, 64
PAIRS = E // 2
GROUPS = 4
GT = T // GROUPS
GTILES = GT // P
UNITS = H // 2
CHUNKS = H // 4
MT = N // P
UC = 2 * MT * N
VW = 32
VB = H * VW + H
KA = 4 * HD + 4
KB = 4 * HD
BIG = float(2 ** 100)
FF_TOK = 512
FF_STEPS = T // FF_TOK
SCALE_B = HD ** -0.5
LOADS = (2 * 8 + 4 + 2, 2 * 8 + 1)
CR_YD, CR_WS, CR_EV, CR_OS, CR_OP, CR_GRP, CR_SCR, CR_HL = FF_STEPS, 1, 2, 16, 1, 1, 16, 2
DVE_A = 4 + 1 + 2 + 1 + 2 + GTILES + 4 + 2
DVE_B = 4 + 1 + 6 + 4 + GTILES
DVE_F0 = 1 + 1 + 4 + 1 + 2 + 1 + 8 * GTILES + 1 + 2 * GTILES + 3 + 2 * GTILES + 4 + 3
E_A = (H // 4) * B
ROUTE_SCALE = 2.5

C_ID, C_HS, C_ROT, C_COS, C_SIN, C_END = 0, 128, 144, 272, 784, 1296


class Steps:

    def __init__(self, eng, sem):
        self.eng, self.sem, self.n, self.off = eng, sem, 0, 0

    def do(self, ins):
        ins.then_inc(self.sem, 1)
        self.n += 1

    def sync(self):
        self.eng.wait_ge(self.sem, self.off + self.n)

    def sync_apart(self, mark):
        self.sync()
        self.eng.sem_inc(mark, 1)

    def enter(self, i, per):
        self.start, self.per, self.off = self.n, per, i * per

    def leave(self, trips):
        assert self.n - self.start == self.per, (self.n - self.start, self.per)
        self.n, self.off = self.start + trips * self.per, 0


def hybrid(nc, x, consts, selh, wA, wB, bqk, brow, rwT, wexp, out):
    ctx = ExitStack()

    def sem(name):
        return ctx.enter_context(nc.semaphore(name))

    def dram(name, shape, dt):
        return nc.dram_tensor(name, shape, dt, kind="Internal").ap()

    q_d = dram("q_split", [2, P, T], F32)
    k_d = dram("k_split", [2, P, T], F32)
    qn_d = dram("q_norm_split", [2, H, T], F32)
    kn_d = dram("k_norm_split", [2, H, T], F32)
    a_d = dram("one_minus_q_norm", [H, T], F32)
    vb_d = dram("v_and_b", [T, VB], F32)
    o_d = dram("attn_unnormalised", [B, P, 4 * N], F32)

    with ctx:
        def keep(name, shape, dt=F32):
            return ctx.enter_context(nc.sbuf_tensor(name, shape, dt))

        X = keep("X", [P, TILES, P])
        cst = keep("cst", [P, C_END])
        wa = keep("wa", [P, 4 * P])
        wb = keep("wb", [P, 4 * P])
        bqk_s = keep("bqk_s", [P, 2])
        bv_s = keep("bv_s", [P, P])
        pb_s = keep("pb_s", [P, P])
        eb_s = keep("eb_s", [P, E])
        rw_s = keep("rw_s", [P, E])
        eps_s = keep("eps_s", [P, 1])
        stats = keep("stats", [P, GTILES, 6])
        mv = keep("mv", [P, GTILES, 2])
        std = keep("std", [P, GTILES])
        rstd = keep("rstd", [P, GTILES])
        ident = cst[:, C_ID:C_ID + P]
        HS = cst[:, C_HS:C_HS + H]
        ROT = cst[:, C_ROT:C_ROT + P]

        ps = ctx.enter_context(nc.psum_tensor("ps", [P, 8 * 512], F32))

        def bank(n, k=1):
            return ps[:, 512 * n:512 * (n + k)]

        with ExitStack() as pre:
            def sb(name, shape, dt=F32):
                return pre.enter_context(nc.sbuf_tensor(name, shape, dt))
            xn = sb("xn", [P, GTILES, P])
            xT = sb("xT", [P, GT])
            sqq = sb("sqq", [P, GT])
            sqk = sb("sqk", [P, GT])
            k2 = sb("k2", [P, GT])
            q2 = sb("q2", [P, GT])
            rt = sb("rt", [P, GT])
            qh = sb("qh", [P, GT], F32R)
            ql = sb("ql", [P, GT], F32R)
            kh = sb("kh", [P, GT], F32R)
            kl = sb("kl", [P, GT], F32R)
            qnh = sb("qnh", [H, GT], F32R)
            qnl = sb("qnl", [H, GT], F32R)
            knh = sb("knh", [H, GT], F32R)
            knl = sb("knl", [H, GT], F32R)
            arow = sb("arow", [H, GT])
            vb = sb("vb", [P, GTILES, VB])
        with ExitStack() as att:
            def sb(name, shape, dt=F32):
                return att.enter_context(nc.sbuf_tensor(name, shape, dt))
            qst = [sb(f"qst{s}", [P, UNITS, N], F32R) for s in range(2)]
            kst = [sb(f"kst{s}", [P, UNITS, N], F32R) for s in range(2)]
            vbs = [sb(f"vbs{s}", [P, MT, VB]) for s in range(2)]
            osb = [sb(f"osb{s}", [P, 4 * N]) for s in range(2)]
            with ExitStack() as a_only:
                abc = [a_only.enter_context(nc.sbuf_tensor(f"abc{s}", [P, H, N], F32)) for s in range(2)]
                Nt = a_only.enter_context(nc.sbuf_tensor("Nt", [P, CHUNKS, 2 * UC], F32))
                St = a_only.enter_context(nc.sbuf_tensor("St", [P, CHUNKS, 2 * UC], F32))
                Dt = a_only.enter_context(nc.sbuf_tensor("Dt", [P, CHUNKS, 2 * UC], F32))
            Wt = sb("Wt", [P, CHUNKS, 2 * UC])
            selh_f = sb("selh_f", [P, H * P])
            selh_r = sb("selh_r", [P, H * P], F32R)
            mx = sb("mx", [P, MT, H])
            mxh_r = sb("mxh_r", [P, MT, H], F32R)
            mxs = sb("mxs", [P, MT, 2 * H])
            mxT = sb("mxT", [P, N], F32R)
        with ExitStack() as ffn:
            def sb(name, shape, dt=F32):
                return ffn.enter_context(nc.sbuf_tensor(name, shape, dt))
            xh = sb("xh", [P, T], F32R)
            xl = sb("xl", [P, T], F32R)
            cs = sb("cs", [P, T], F32R)
            with ExitStack() as rtr:
                def sr(name, shape, dt=F32):
                    return rtr.enter_context(nc.sbuf_tensor(name, shape, dt))
                f_xn = sr("f_xn", [P, GTILES, P])
                f_xT = sr("f_xT", [P, GT])
                ou = sr("ou", [P, 2, 4 * N])
                rden = sr("rden", [P, GTILES, H])
                otok = sr("otok", [P, GTILES, P])
                oT = sr("oT", [P, GT])
                sc = sr("sc", [P, GTILES, E])
                sfc = sr("sfc", [P, GTILES, E])
                m8 = sr("m8", [P, GTILES, 8, 8])
                gs = sr("gs", [P, GTILES, 12])
                g8 = sr("g8", [P, GTILES, 8])
                gr = sr("gr", [P, GTILES, 12])
                gm = sr("gm", [P, GTILES, 8])
                mk = sr("mk", [P, GTILES, E])
                k8 = sr("k8", [P, GTILES, 8])
                mr = sr("mr", [P, GTILES, E])
                wsel = sr("wsel", [P, GTILES, E])
                wsum = sr("wsum", [P, GTILES])
                wrec = sr("wrec", [P, GTILES])
                coef = sr("coef", [P, GTILES, 2 * E])
                chi = sr("chi", [P, GT], F32R)
            wraw = [sb(f"wraw{s}", [P, 4 * P]) for s in range(2)]
            whi = [sb(f"whi{s}", [P, 4 * P], F32R) for s in range(2)]
            wlo = [sb(f"wlo{s}", [P, 3 * P], F32R) for s in range(2)]
            sg = [sb(f"sg{s}", [P, FF_TOK]) for s in range(2)]
            h1 = [sb(f"h1{s}", [P, FF_TOK]) for s in range(2)]
            hf = [sb(f"hf{s}", [P, FF_TOK]) for s in range(2)]
            hh = [sb(f"hh{s}", [P, FF_TOK], F32R) for s in range(4)]
            hl = [sb(f"hl{s}", [P, FF_TOK], F32R) for s in range(4)]
            zr = sb("zr", [P, FF_TOK], F32R)
            yT = sb("yT", [P, T])

        s_in = sem("inputs_loaded")
        s_out = sem("output_stored")
        s_phase = sem("phase_done")
        s_mark = sem("wait_carrier")
        s_eps = sem("eps_ready")
        s_stat = sem("stats_ready")
        s_std = sem("std_ready")
        s_xn = sem("xn_ready")
        s_xnT = sem("xnT_in_psum")
        s_xT = sem("xT_ready")
        s_qkv = sem("qkv_in_psum")
        s_sq = sem("squares_ready")
        s_nrm = sem("norms_in_psum")
        s_rot = sem("rotated_in_psum")
        s_spl = sem("splits_ready")
        s_scr = sem("scratch_stored")
        s_ou = sem("unnormalised_loaded")
        s_oP = sem("o_token_major_in_psum")
        s_on = sem("o_normalised")
        s_oT = sem("oT_in_psum")
        s_oTs = sem("oT_ready")
        s_wo = sem("projection_in_psum")
        s_lg = sem("logits_in_psum")
        s_sc = sem("scores_ready")
        s_cf = sem("coef_ready")
        s_cT = sem("coefT_in_psum")
        s_grp = sem("group_used")
        s_init = sem("stack_constants_ready")
        s_sel = sem("selector_loaded")
        s_ld = [sem(f"sample_loaded{s}") for s in range(2)]
        s_s = sem("diff_in_psum")
        s_fr = sem("diff_read")
        s_rt = sem("roots_ready")
        s_y = sem("root_sum_ready")
        s_e = sem("inverse_square_ready")
        s_w = sem("weights_ready")
        s_pv = sem("pv_in_psum")
        s_ev = sem("pv_copied")
        s_os = [sem(f"o_stored{s}") for s in range(2)]
        s_s1 = sem("b_scores_in_psum")
        s_mx = sem("b_unit_max_read")
        s_ms = sem("b_max_split_ready")
        s_mT = sem("b_maxT_in_psum")
        s_mr = sem("b_maxT_ready")
        s_s2 = sem("b_shifted_in_psum")
        s_wl = [sem(f"expert_weights_loaded{s}") for s in range(2)]
        s_ws = sem("expert_weights_split")
        s_z = sem("zero_ready")
        s_g = sem("gate_in_psum")
        s_u = sem("up_in_psum")
        s_c = sem("coef_in_psum")
        s_sg = sem("silu_ready")
        s_h1 = sem("gate_up_ready")
        s_h = sem("h_ready")
        s_hh = sem("h_hi_ready")
        s_hl = sem("h_lo_ready")
        s_yd = sem("down_done")
        s_yT = sem("yT_ready")
        s_yP = sem("y_token_major_in_psum")
        s_res = sem("residual_added")
        s_dve = sem("dve_steps")
        s_act = sem("act_steps")
        s_pool = sem("pool_steps")

        block = ctx.enter_context(nc.Block())

        def meet(eng, n):
            eng.sem_inc(s_phase, 1)
            eng.wait_ge(s_phase, 5 * n)

        def lap(stage, i):
            return i + (GROUPS * stage + 1)

        def samples(eng, step):
            with eng.Fori(0, B // 2 - 1) as i:
                step(i, 0, False)
                step(i, 1, False)
            step(B // 2 - 1, 0, False)
            step(B // 2 - 1, 1, True)

        def after(i, slot, per, k, base=0):
            return i * (2 * per) + (slot * per + k + base)

        @block.sync
        def _(sp):
            sp.dma_start(X[:, :, :], x.rearrange("b (m p) d -> p (b m) d", p=P)).then_inc(s_in, 16)
            sp.dma_start(cst[:, :], consts).then_inc(s_in, 16)
            sp.dma_start(wa[:, :], wA).then_inc(s_in, 16)
            sp.dma_start(wb[:, :], wB).then_inc(s_in, 16)
            sp.dma_start(bqk_s[:, :], bqk).then_inc(s_in, 16)
            sp.dma_start(bv_s[:, :], brow[0:1, 0:P].broadcast_to([P, P])).then_inc(s_in, 16)
            sp.dma_start(pb_s[:, :], brow[0:1, P:2 * P].broadcast_to([P, P])).then_inc(s_in, 16)
            sp.dma_start(eb_s[:, :], brow[0:1, 2 * P:2 * P + E].broadcast_to([P, E])).then_inc(s_in, 16)
            sp.dma_start(rw_s[:, :], rwT).then_inc(s_in, 16)
            sp.wait_ge(s_in, 16 * 9)

            def store_splits(stage, i):
                at = bass.ds(i * GT, GT)
                sp.wait_ge(s_spl, lap(stage, i))
                todo = [(q_d[0, :, at], qh[:, :].bitcast(F32)), (q_d[1, :, at], ql[:, :].bitcast(F32)),
                        (k_d[0, :, at], kh[:, :].bitcast(F32)), (k_d[1, :, at], kl[:, :].bitcast(F32)),
                        (vb_d[at, :].rearrange("(t p) c -> p t c", p=P), vb[:, :, :])]
                if stage == 0:
                    todo += [(qn_d[0, :, at], qnh[:, :].bitcast(F32)), (qn_d[1, :, at], qnl[:, :].bitcast(F32)),
                             (kn_d[0, :, at], knh[:, :].bitcast(F32)), (kn_d[1, :, at], knl[:, :].bitcast(F32)),
                             (a_d[:, at], arow[:, :])]
                for to, of in todo:
                    sp.dma_start(to, of).then_inc(s_scr, 16)
                return 16 * len(todo)

            def load_sample(i, slot, phase):
                at = bass.ds(i * (2 * N) + slot * N, N)
                for g in range(2):
                    for r in range(4):
                        row = 64 * g + HD * r
                        for to, of, role in ((qst, q_d, r // 2), (kst, k_d, r % 2)):
                            src = of[role, :, at].rearrange("(t g j) n -> g j t n", g=2, j=HD)[g]
                            sp.dma_start(to[slot][row:row + HD, :, :].bitcast(F32), src).then_inc(s_ld[slot], 16)
                    if phase == 0:
                        for to, of, row in ((qst, qn_d, 64 * g + 32), (kst, kn_d, 64 * g + 34)):
                            src = of[:, :, at].rearrange("r (t g) n -> g r t n", g=2)[g]
                            sp.dma_start(to[slot][row:row + 2, :, :].bitcast(F32), src).then_inc(s_ld[slot], 16)
                if phase == 0:
                    sp.dma_start(abc[slot][:, :, :], a_d[:, at].partition_broadcast(P)).then_inc(s_ld[slot], 16)
                sp.dma_start(vbs[slot][:, :, :], vb_d[at, :].rearrange("(m p) c -> p m c", p=P)).then_inc(s_ld[slot], 16)

            def sample_phase(phase):
                base = 4 * B * phase
                if phase == 0:
                    sp.wait_ge(s_init, 1)
                else:
                    for g in range(2):
                        sp.dma_start(selh_f[64 * g:64 * g + 2 * H, :], selh).then_inc(s_sel, 16)
                load_sample(0, 0, phase)
                load_sample(0, 1, phase)

                def step(i, slot, last):
                    if not (isinstance(i, int)):
                        sp.wait_ge(s_pv, after(i, slot, CHUNKS, CHUNKS, base))
                        load_sample(i + 1, slot, phase)
                    sp.wait_ge(s_ev, after(i, slot, 1, 1, B * phase + CR_EV))
                    sp.dma_start(o_d[bass.ds(i * 2 + slot, 1), :, :].rearrange("a p n -> p (a n)"),
                                 osb[slot][:, :]).then_inc(s_os[slot], 16)
                samples(sp, step)
                for s in range(2):
                    sp.wait_ge(s_os[s], 16 * (B // 2) * (phase + 1) + CR_OS)

            def experts_phase(f):
                base = (PAIRS + 1) * f
                sp.dma_start(wraw[1][:, :], wexp[PAIRS]).then_inc(s_wl[1], 16)
                with sp.Fori(0, PAIRS // 2) as i:
                    for s in range(2):
                        sp.wait_ge(s_ws, i * 2 + (base + s + CR_WS))
                        sp.dma_start(wraw[s][:, :], wexp[bass.ds(i * 2 + s, 1), :, :].rearrange("a p n -> p (a n)")
                                     ).then_inc(s_wl[s], 16)

            def prepare_f(f):
                with sp.Fori(0, GROUPS) as i:
                    sp.wait_ge(s_oP, i + (GROUPS * f + CR_OP))
                    if f == 0:
                        to, of = ou[:, :, :], o_d[bass.ds(i * 2, 2), :, :].rearrange("a p n -> p a n")
                    else:
                        to = ou[:, :, :].rearrange("p a n -> p (a n)").rearrange("p (b n) -> p b n", n=N)
                        of = o_d[:, :, bass.ds(i * N, N)].rearrange("b p n -> p b n")
                    sp.dma_start(to, of).then_inc(s_ou, 16)

            sp.sem_inc(s_scr, CR_SCR)
            for s in range(2):
                sp.sem_inc(s_os[s], CR_OS)
            with sp.Fori(0, GROUPS) as i:
                per = store_splits(0, i)
                sp.wait_ge(s_scr, i * per + (per + CR_SCR))
                sp.sem_inc(s_mark, 1)
            done_a = GROUPS * per
            meet(sp, 1)
            sample_phase(0)
            meet(sp, 2)
            prepare_f(0)
            meet(sp, 3)
            experts_phase(0)
            meet(sp, 4)
            with sp.Fori(0, GROUPS) as i:
                per = store_splits(1, i)
                sp.wait_ge(s_scr, i * per + (per + done_a + CR_SCR))
                sp.sem_inc(s_mark, 1)
            meet(sp, 5)
            sample_phase(1)
            meet(sp, 6)
            prepare_f(1)
            meet(sp, 7)
            experts_phase(1)
            sp.wait_ge(s_res, 2 * FF_STEPS)
            sp.dma_start(out.rearrange("b (m p) d -> p (b m) d", p=P), X[:, :, :]).then_inc(s_out, 16)
            sp.wait_ge(s_out, 16)

        @block.tensor
        def _(pe):
            def mm(o, l, r, start=True, stop=True, **kw):
                return pe.matmul(o, l, r, start=start, stop=stop, **kw)

            def norm_transposed(stage, i, xn_):
                pe.wait_ge(s_xn, lap(stage, i))
                for j in range(GTILES):
                    last = pe.transpose(bank(0)[:, j * P:(j + 1) * P], xn_[:, j, :], ident)
                last.then_inc(s_xnT, 1)
                pe.wait_ge(s_xT, lap(stage, i))

            def prepare_qkv(k, i):
                w = (wa, wb)[k]
                norm_transposed(2 * k, i, xn)
                mm(bank(1), w[:, 0:P], xT[:, :])
                mm(bank(2), w[:, P:2 * P], xT[:, :])
                for j in range(GTILES):
                    last = mm(bank(3)[:, j * P:(j + 1) * P], xT[:, j * P:(j + 1) * P], w[:, 2 * P:3 * P])
                last.then_inc(s_qkv, 1)
                pe.wait_ge(s_sq, lap(k, i))
                if k == 0:
                    mm(bank(4)[0:H, :], HS, sqq[:, :])
                    mm(bank(5)[0:H, :], HS, sqk[:, :])
                    for j in range(GTILES):
                        last = mm(bank(6)[:, j * H:(j + 1) * H], sqk[:, j * P:(j + 1) * P], HS)
                    last.then_inc(s_nrm, 1)
                else:
                    mm(bank(4), ROT, sqq[:, :])
                    mm(bank(5), ROT, sqk[:, :]).then_inc(s_rot, 1)

            def pv(i, slot, c, wt, phase):
                if phase == 0:
                    b0 = 4 + 2 * slot
                    pe.wait_ge(s_w, after(i, slot, CHUNKS, c + 1))
                    pe.wait_ge(s_ev, after(i, slot, 1, CR_EV - 1))
                else:
                    b0 = 6
                    pe.wait_ge(s_e, after(i, slot, UNITS, 2 * c + 2, E_A))
                    pe.wait_ge(s_ev, after(i, slot, 1, 0, B + CR_EV))
                for mt in range(MT):
                    for g in range(4):
                        h = 4 * c + g
                        col = (g * MT + mt) * N
                        last = mm(ps[32 * g:32 * g + VW, 512 * b0 + c * N:512 * b0 + (c + 1) * N],
                                  vbs[slot][:, mt, h * VW:(h + 1) * VW], wt[:, c, col:col + N],
                                  start=(mt == 0), stop=(mt == MT - 1), tile_position=(0, 32 * g))
                last.then_inc(s_pv, 1)

            def a_scores(i, slot, u):
                b0 = 2 * (u % 2)
                for g in range(2):
                    for mt in range(MT):
                        col = 512 * b0 + (g * MT + mt) * N
                        last = mm(ps[:, col:col + N], kst[slot][64 * g:64 * g + KA, u, mt * P:(mt + 1) * P],
                                  qst[slot][64 * g:64 * g + KA, u, :])
                last.then_inc(s_s, 1)

            def samples_a():
                pe.wait_ge(s_ld[0], 16 * LOADS[0])
                for u in range(UNITS):
                    if u >= 2:
                        pe.wait_ge(s_fr, u - 1)
                    a_scores(0, 0, u)

                def step(i, slot, last):
                    ni, ns = (i, 1) if slot == 0 else (i + 1, 0)
                    if not last:
                        pe.wait_ge(s_ld[ns], ni * (16 * LOADS[0]) + 16 * LOADS[0])
                    for c in range(CHUNKS):
                        pv(i, slot, c, St, 0)
                        if not last:
                            for u in (2 * c, 2 * c + 1):
                                pe.wait_ge(s_fr, after(i, slot, UNITS, UNITS + u - 1))
                                a_scores(ni, ns, u)
                samples(pe, step)
                pe.wait_ge(s_pv, CHUNKS * B)

            def b_scores(i, slot, u):
                for g in range(2):
                    for nt in range(MT):
                        col = 512 * 4 + (g * MT + nt) * N
                        last = mm(ps[:, col:col + N], qst[slot][64 * g:64 * g + KB, u, nt * P:(nt + 1) * P],
                                  kst[slot][64 * g:64 * g + KB, u, :])
                last.then_inc(s_s1, 1)

            def b_shifted(i, slot, u):
                b0 = 2 * (u % 2)
                for g in range(2):
                    h = 2 * u + g
                    for mt in range(MT):
                        col = 512 * b0 + (g * MT + mt) * N
                        mm(ps[:, col:col + N], kst[slot][64 * g:64 * g + KB, u, mt * P:(mt + 1) * P],
                           qst[slot][64 * g:64 * g + KB, u, :], start=True, stop=False)
                        last = mm(ps[:, col:col + N], selh_r[64 * g:64 * g + 2 * H, h * P:(h + 1) * P],
                                  mxT[64 * g:64 * g + 2 * H, :],
                                  start=False, stop=True)
                last.then_inc(s_s2, 1)

            def samples_b():
                base1 = UNITS * B
                l0 = 16 * LOADS[0] * (B // 2)
                pe.wait_ge(s_ld[0], l0 + 16 * LOADS[1])
                for u in range(UNITS):
                    if u >= 1:
                        pe.wait_ge(s_mx, u)
                    b_scores(0, 0, u)

                def step(i, slot, last):
                    ni, ns = (i, 1) if slot == 0 else (i + 1, 0)
                    pe.wait_ge(s_ms, after(i, slot, 1, 1))
                    for nt in range(MT):
                        tr = pe.transpose(ps[0:2 * H, 512 * 4 + nt * P:512 * 4 + (nt + 1) * P], mxs[:, nt, :], ident)
                    tr.then_inc(s_mT, 1)
                    pe.wait_ge(s_mr, after(i, slot, 1, 1))
                    if not last:
                        pe.wait_ge(s_ld[ns], ni * (16 * LOADS[1]) + (16 * LOADS[1] + l0))
                    for u in range(UNITS):
                        pe.wait_ge(s_e, after(i, slot, UNITS, u - 1, E_A))
                        b_shifted(i, slot, u)
                        if not last:
                            if u >= 1:
                                pe.wait_ge(s_mx, after(i, slot, UNITS, UNITS + u))
                            b_scores(ni, ns, u)
                        if u % 2 == 1 and u >= 3:
                            pv(i, slot, u // 2 - 1, Wt, 1)
                    pv(i, slot, CHUNKS - 1, Wt, 1)
                samples(pe, step)
                pe.wait_ge(s_pv, 2 * CHUNKS * B)

            def prepare_f(f, i):
                pe.wait_ge(s_grp, i + (GROUPS * f + CR_GRP))
                pe.wait_ge(s_ou, i * 16 + (16 * GROUPS * f + 16))
                if f == 0:
                    for b2 in range(2):
                        for nt in range(MT):
                            for hg in range(CHUNKS):
                                col = 512 * (2 * b2 + nt) + hg * P
                                last = pe.transpose(ps[:, col:col + P],
                                                    ou[:, b2, hg * N + nt * P:hg * N + (nt + 1) * P], ident)
                else:
                    by16 = ou[:, :, :].rearrange("p a n -> p (a n)").rearrange("p (r l) -> p l r", l=P // HD)
                    for low in range(P // HD):
                        last = pe.transpose(ps[:, low * P:(low + 1) * P], by16[:, low, :], ident)
                last.then_inc(s_oP, 1)
                pe.wait_ge(s_on, lap(f, i))
                for j in range(GTILES):
                    last = pe.transpose(bank(4)[:, j * P:(j + 1) * P], otok[:, j, :], ident)
                last.then_inc(s_oT, 1)
                pe.wait_ge(s_oTs, lap(f, i))
                for j in range(GTILES):
                    last = mm(bank(5)[:, j * P:(j + 1) * P], oT[:, j * P:(j + 1) * P], (wa, wb)[f][:, 3 * P:4 * P])
                last.then_inc(s_wo, 1)
                norm_transposed(2 * f + 1, i, f_xn)
                for j in range(GTILES):
                    last = mm(bank(1)[:, j * E:(j + 1) * E], f_xT[:, j * P:(j + 1) * P], rw_s[:, :])
                last.then_inc(s_lg, 1)
                pe.wait_ge(s_cf, lap(f, i))
                for j in range(GTILES):
                    last = pe.transpose(bank(2)[:, j * P:(j + 1) * P], coef[:, j, :], ident)
                last.then_inc(s_cT, 1)

            def experts(f):
                s0 = (PAIRS + 1) * FF_STEPS * f
                w0 = (PAIRS + 1) * f

                def y(n, slot, chunk):
                    pe.wait_ge(s_hl, n + CR_HL)
                    hi, lo = hh[chunk], hl[chunk]
                    for k, (l, r) in enumerate(((whi[slot], hi), (whi[slot], lo), (wlo[slot], hi))):
                        last = mm(bank(chunk), l[:, 2 * P:3 * P], r[:, :], start=False, stop=False,
                                  skip_group_check=True)
                    last.then_inc(s_yd, 1)

                def gate_up(n, slot, chunk, first, shared):
                    cols = slice(chunk * FF_TOK, (chunk + 1) * FF_TOK)
                    hi, lo = whi[slot], wlo[slot]
                    if not first:
                        pe.wait_ge(s_sg, n)
                    for k, (l, r) in enumerate(((hi, xh), (hi, xl), (lo, xh))):
                        last = mm(bank(4), l[:, 0:P], r[:, cols], start=(k == 0), stop=(k == 2))
                    last.then_inc(s_g, 1)
                    if not first:
                        pe.wait_ge(s_h1, n)
                    for k, (l, r) in enumerate(((hi, xh), (hi, xl), (lo, xh))):
                        last = mm(bank(5), l[:, P:2 * P], r[:, cols], start=(k == 0), stop=(k == 2))
                    last.then_inc(s_u, 1)
                    if not first:
                        pe.wait_ge(s_h, n)
                    if not shared:
                        mm(bank(6), hi[:, 3 * P:4 * P], cs[:, cols]).then_inc(s_c, 1)

                pe.wait_ge(s_z, f + 1)
                for c in range(FF_STEPS):
                    mm(bank(c), zr[:, 0:P], zr[:, :], start=True, stop=False, skip_group_check=True)
                pe.wait_ge(s_ws, w0 + 1 + CR_WS)
                for c in range(FF_STEPS):
                    gate_up(s0 + c, 1, c, c == 0, True)
                    if c >= 2:
                        y(s0 + c - 1, 1, c - 2)
                with pe.Fori(0, PAIRS // 2) as i:
                    for s in range(2):
                        pe.wait_ge(s_ws, i * 2 + (w0 + 2 + s + CR_WS))
                        for c in range(FF_STEPS):
                            n = i * (2 * FF_STEPS) + (s0 + (s + 1) * FF_STEPS + c)
                            gate_up(n, s, c, False, False)
                            y(n - 1, s if c >= 2 else 1 - s, (c - 2) % FF_STEPS)
                end = s0 + (PAIRS + 1) * FF_STEPS
                y(end - 1, 1, FF_STEPS - 2)
                y(end, 1, FF_STEPS - 1)
                for c in range(FF_STEPS):
                    pe.wait_ge(s_yT, FF_STEPS * f + c + 1)
                    for j in range(GTILES):
                        last = pe.transpose(bank(4 + c)[:, j * P:(j + 1) * P],
                                            yT[:, (c * GTILES + j) * P:(c * GTILES + j + 1) * P], ident)
                    last.then_inc(s_yP, 1)
                pe.wait_ge(s_yP, FF_STEPS * (f + 1))

            pe.sem_inc(s_yd, CR_YD)
            pe.sem_inc(s_oP, CR_OP)
            pe.wait_ge(s_in, 16 * 9)
            with pe.Fori(0, GROUPS) as i:
                prepare_qkv(0, i)
            pe.wait_ge(s_nrm, GROUPS)
            meet(pe, 1)
            samples_a()
            meet(pe, 2)
            with pe.Fori(0, GROUPS) as i:
                prepare_f(0, i)
            pe.wait_ge(s_cT, GROUPS)
            meet(pe, 3)
            experts(0)
            meet(pe, 4)
            with pe.Fori(0, GROUPS) as i:
                prepare_qkv(1, i)
            pe.wait_ge(s_rot, GROUPS)
            meet(pe, 5)
            samples_b()
            meet(pe, 6)
            with pe.Fori(0, GROUPS) as i:
                prepare_f(1, i)
            pe.wait_ge(s_cT, 2 * GROUPS)
            meet(pe, 7)
            experts(1)

        @block.scalar
        def _(act):
            st = Steps(act, s_act)

            def norm(stage, i, xT_):
                act.wait_ge(s_stat, lap(stage, i))
                act.activation(std[:, :], mv[:, :, 1], ACT.Sqrt, bias=eps_s[:, 0:1]).then_inc(s_std, 1)
                act.wait_ge(s_xnT, lap(stage, i))
                act.activation(xT_[:, :], bank(0), ACT.Copy).then_inc(s_xT, 1)

            def prepare_qkv(k, i):
                norm(2 * k, i, xT)
                act.wait_ge(s_qkv, lap(k, i))
                if k == 0:
                    act.activation(sqq[:, :], bank(1), ACT.Square)
                    act.activation(sqk[:, :], bank(2), ACT.Square).then_inc(s_sq, 1)
                else:
                    act.activation(sqq[:, :], bank(1), ACT.Identity, bias=bqk_s[:, 0:1])
                    act.activation(sqk[:, :], bank(2), ACT.Identity, bias=bqk_s[:, 1:2]).then_inc(s_sq, 1)

            def samples_a():
                def step(i, slot, last):
                    for c in range(CHUNKS):
                        act.wait_ge(s_fr, after(i, slot, UNITS, 2 * c + 2))
                        act.activation(Nt[:, c, :], Nt[:, c, :], ACT.Sqrt)
                        act.activation(St[:, c, :], St[:, c, :], ACT.Sqrt).then_inc(s_rt, 1)
                    for c in range(CHUNKS):
                        act.wait_ge(s_y, after(i, slot, CHUNKS, c + 1))
                        st.do(act.activation(Nt[:, c, :], Nt[:, c, :], ACT.Ln))
                        st.sync()
                        act.activation(Nt[:, c, :], Nt[:, c, :], ACT.Exp, scale=-2.0).then_inc(s_e, 1)
                with act.Fori(0, B // 2 - 1) as i:
                    st.enter(i, 2 * CHUNKS)
                    step(i, 0, False)
                    step(i, 1, False)
                st.leave(B // 2 - 1)
                step(B // 2 - 1, 0, False)
                step(B // 2 - 1, 1, True)
                act.wait_ge(s_e, CHUNKS * B)

            def samples_b():
                def step(i, slot, last):
                    for u in range(UNITS):
                        b0 = 2 * (u % 2)
                        act.wait_ge(s_s2, after(i, slot, UNITS, u + 1))
                        act.wait_ge(s_pv, after(i, slot, CHUNKS, u // 2 + 1 - CHUNKS, CHUNKS * B))
                        act.activation(Wt[:, u // 2, (u % 2) * UC:(u % 2 + 1) * UC],
                                       ps[:, 512 * b0:512 * b0 + UC], ACT.Exp, scale=SCALE_B).then_inc(s_e, 1)
                samples(act, step)
                act.wait_ge(s_e, E_A + UNITS * B)

            def prepare_f(f, i):
                act.wait_ge(s_oT, lap(f, i))
                act.activation(oT[:, :], bank(4), ACT.Copy).then_inc(s_oTs, 1)
                norm(2 * f + 1, i, f_xT)
                act.wait_ge(s_lg, lap(f, i))
                act.activation(sc[:, :, :].rearrange("p t e -> p (t e)"), bank(1)[:, 0:GTILES * E],
                               ACT.Sigmoid).then_inc(s_sc, 1)

            def experts(f):
                s0 = (PAIRS + 1) * FF_STEPS * f

                def silu(n, c, sg_used):
                    act.wait_ge(s_g, n + 1)
                    if sg_used is not None:
                        act.wait_ge(s_h1, sg_used)
                    act.activation(sg[c % 2][:, :], bank(4), ACT.Silu).then_inc(s_sg, 1)

                def high(n, c):
                    act.wait_ge(s_h, n)
                    act.wait_ge(s_yd, n - FF_STEPS + CR_YD)
                    act.activation(hh[c][:, :], hf[c % 2][:, :], ACT.Copy).then_inc(s_hh, 1)

                for c in range(FF_STEPS):
                    silu(s0 + c, c, s0 + c - 1 if s0 + c >= 2 else None)
                    if c >= 1:
                        high(s0 + c, c - 1)
                with act.Fori(0, PAIRS // 2) as i:
                    for s in range(2):
                        for c in range(FF_STEPS):
                            n = i * (2 * FF_STEPS) + (s0 + (s + 1) * FF_STEPS + c)
                            silu(n, c, n - 1)
                            high(n, (c - 1) % FF_STEPS)
                end = s0 + (PAIRS + 1) * FF_STEPS
                high(end, FF_STEPS - 1)
                for c in range(FF_STEPS):
                    act.wait_ge(s_yd, end - (FF_STEPS - 1 - c) + CR_YD)
                    act.activation(yT[:, c * FF_TOK:(c + 1) * FF_TOK], bank(c), ACT.Copy).then_inc(s_yT, 1)
                act.wait_ge(s_yT, FF_STEPS * (f + 1))

            act.wait_ge(s_in, 16 * 9)
            act.wait_ge(s_eps, 1)
            with act.Fori(0, GROUPS) as i:
                prepare_qkv(0, i)
            act.wait_ge(s_sq, GROUPS)
            meet(act, 1)
            samples_a()
            meet(act, 2)
            with act.Fori(0, GROUPS) as i:
                prepare_f(0, i)
            act.wait_ge(s_sc, GROUPS)
            meet(act, 3)
            experts(0)
            meet(act, 4)
            with act.Fori(0, GROUPS) as i:
                prepare_qkv(1, i)
            act.wait_ge(s_sq, 2 * GROUPS)
            meet(act, 5)
            samples_b()
            meet(act, 6)
            with act.Fori(0, GROUPS) as i:
                prepare_f(1, i)
            act.wait_ge(s_sc, 2 * GROUPS)
            meet(act, 7)
            experts(1)

        @block.gpsimd
        def _(pool):
            def samples_a():
                def step(i, slot, last):
                    for c in range(CHUNKS):
                        pool.wait_ge(s_e, after(i, slot, CHUNKS, c + 1))
                        pool.tensor_tensor(St[:, c, :], Dt[:, c, :], Nt[:, c, :], ALU.mult).then_inc(s_w, 1)
                samples(pool, step)
                pool.wait_ge(s_w, CHUNKS * B)

            def split(slot, n, loaded):
                pool.wait_ge(s_wl[slot], loaded)
                pool.sem_inc(s_mark, 1)
                pool.tensor_copy(whi[slot][:, :], wraw[slot][:, :]).then_inc(s_pool, 1)
                pool.wait_ge(s_pool, n)
                pool.tensor_tensor(wlo[slot][:, :], wraw[slot][:, 0:3 * P], whi[slot][:, 0:3 * P],
                                   ALU.subtract).then_inc(s_ws, 1)

            def experts(f):
                w0 = (PAIRS + 1) * f
                s0 = (PAIRS + 1) * FF_STEPS * f
                loads = ((PAIRS // 2) * f, (PAIRS // 2 + 1) * f + 1)
                split(1, w0 + 1, 16 * loads[1])
                with pool.Fori(0, PAIRS // 2) as i:
                    for s in range(2):
                        pool.wait_ge(s_yd, i * (2 * FF_STEPS) + (s0 + s * FF_STEPS + CR_YD))
                        split(s, i * 2 + (w0 + 2 + s), i * 16 + 16 * (loads[s] + 1))
                pool.wait_ge(s_ws, w0 + PAIRS + 1 + CR_WS)

            pool.sem_inc(s_ws, CR_WS)
            meet(pool, 1)
            samples_a()
            meet(pool, 2)
            meet(pool, 3)
            experts(0)
            meet(pool, 4)
            meet(pool, 5)
            meet(pool, 6)
            meet(pool, 7)
            experts(1)

        @block.vector
        def _(dve):
            st = Steps(dve, s_dve)

            def tile(i, j):
                return X[:, bass.ds(i * GTILES + j, 1), :].rearrange("p a d -> p (a d)")

            def norm(stage, i, xn_):
                dve.sem_inc(s_mark, 1)
                for j in range(GTILES):
                    st.do(dve.bn_stats(stats[:, j, :], tile(i, j)))
                st.sync_apart(s_mark)
                for j in range(GTILES):
                    last = dve.bn_aggr(mv[:, j, :], stats[:, j, :])
                last.then_inc(s_stat, 1)
                dve.wait_ge(s_std, lap(stage, i))
                st.do(dve.reciprocal(rstd[:, :], std[:, :]))
                st.sync()
                for j in range(GTILES):
                    last = dve.tensor_scalar(xn_[:, j, :], tile(i, j), mv[:, j, 0:1], rstd[:, j:j + 1],
                                             ALU.subtract, ALU.mult)
                last.then_inc(s_xn, 1)

            def split(hi, lo, of):
                st.do(dve.tensor_copy(hi, of))
                st.sync()
                st.do(dve.tensor_tensor(lo, of, hi, ALU.subtract))

            def init_v():
                st.do(dve.memset(vb[:, :, :], 0.0))
                st.sync()
                heads = vb[:, :, 0:H * VW].rearrange("p t (h c) -> p t h c", c=VW)
                st.do(dve.memset(heads[:, :, :, HD:HD + 1], 1.0))
                st.sync()

            def v_columns(k):
                for j in range(GTILES):
                    o = vb[:, j, 0:H * VW].rearrange("p (h c) -> p h c", c=VW)[:, :, 0:HD]
                    v = bank(3)[:, j * P:(j + 1) * P].rearrange("p (h c) -> p h c", c=HD)
                    if k == 0:
                        st.do(dve.tensor_copy(o, v))
                    else:
                        st.do(dve.tensor_tensor(o, v, bv_s[:, :].rearrange("p (h c) -> p h c", c=HD), ALU.add))

            def prepare_a(i):
                norm(0, i, xn)
                dve.wait_ge(s_sq, lap(0, i))
                dve.wait_ge(s_scr, i * (16 * 10) + CR_SCR)
                split(qh[:, :], ql[:, :], bank(1))
                st.do(dve.tensor_scalar(k2[:, :], bank(2), -2.0, None, ALU.mult))
                st.sync()
                split(kh[:, :], kl[:, :], k2[:, :])
                v_columns(0)
                dve.wait_ge(s_nrm, lap(0, i))
                split(qnh[:, :], qnl[:, :], bank(4)[0:H, :])
                split(knh[:, :], knl[:, :], bank(5)[0:H, :])
                st.do(dve.tensor_scalar(arow[:, :], bank(4)[0:H, :], -1.0, 1.0, ALU.mult, ALU.add))
                st.do(dve.tensor_scalar(vb[:, :, H * VW:VB],
                                        bank(6)[:, 0:GTILES * H].rearrange("p (t h) -> p t h", h=H),
                                        -1.0, 1.0, ALU.mult, ALU.add))
                st.sync()
                dve.sem_inc(s_spl, 1)

            def prepare_b(i):
                norm(2, i, xn)
                dve.wait_ge(s_rot, lap(0, i))
                dve.wait_ge(s_scr, i * (16 * 5) + (GROUPS * 16 * 10 + CR_SCR))
                for raw, b, o in ((sqq, 4, q2), (sqk, 5, k2)):
                    st.do(dve.tensor_tensor(rt[:, :], bank(b), cst[:, C_SIN:C_SIN + GT], ALU.mult))
                    st.do(dve.tensor_tensor(o[:, :], raw[:, :], cst[:, C_COS:C_COS + GT], ALU.mult))
                    st.sync()
                    st.do(dve.tensor_tensor(o[:, :], o[:, :], rt[:, :], ALU.add))
                    st.sync()
                split(qh[:, :], ql[:, :], q2[:, :])
                split(kh[:, :], kl[:, :], k2[:, :])
                v_columns(1)
                st.sync()
                dve.sem_inc(s_spl, 1)

            def samples_a():
                def front(i, slot, c, first=False):
                    if not first:
                        dve.wait_ge(s_w, after(i, slot, CHUNKS, c + 1 - CHUNKS))
                    if c == 0:
                        dve.wait_ge(s_ld[slot], i * (16 * LOADS[0]) + 16 * LOADS[0])
                    for u in (2 * c, 2 * c + 1):
                        for g in range(2):
                            for mt in range(MT):
                                col = ((u % 2) * 2 * MT + g * MT + mt) * N
                                h = 2 * u + g
                                st.do(dve.tensor_scalar(Dt[:, c, col:col + N], abc[slot][:, h, :],
                                                        vbs[slot][:, mt, H * VW + h:H * VW + h + 1], 1e-6,
                                                        ALU.mult, ALU.max))
                    st.sync()
                    if not first:
                        dve.wait_ge(s_pv, after(i, slot, CHUNKS, c + 1 - CHUNKS))
                    for u in (2 * c, 2 * c + 1):
                        dve.wait_ge(s_s, after(i, slot, UNITS, u + 1))
                        b0 = 512 * 2 * (u % 2)
                        at = slice((u % 2) * UC, (u % 2 + 1) * UC)
                        dve.tensor_scalar(Nt[:, c, at], ps[:, b0:b0 + UC], 0.0, None, ALU.max)
                        dve.scalar_tensor_tensor(St[:, c, at], ps[:, b0:b0 + UC], 0.0, Dt[:, c, at],
                                                 ALU.max, ALU.add).then_inc(s_fr, 1)

                def step(i, slot, last):
                    for c in range(CHUNKS):
                        dve.wait_ge(s_rt, after(i, slot, CHUNKS, c + 1))
                        dve.tensor_tensor(Nt[:, c, :], Nt[:, c, :], St[:, c, :], ALU.add).then_inc(s_y, 1)
                    ni, ns = (i, 1) if slot == 0 else (i + 1, 0)
                    if not last:
                        for c in range(CHUNKS):
                            front(ni, ns, c)
                    dve.wait_ge(s_pv, after(i, slot, CHUNKS, CHUNKS))
                    dve.wait_ge(s_os[slot], i * 16 + CR_OS)
                    b0 = 512 * (4 + 2 * slot)
                    dve.tensor_copy(osb[slot][:, :], ps[:, b0:b0 + 2 * 512]).then_inc(s_ev, 1)

                for s in range(2):
                    st.do(dve.memset(qst[s][:, :, :].bitcast(F32), 1.0))
                    st.do(dve.memset(kst[s][:, :, :].bitcast(F32), 1.0))
                st.sync()
                dve.sem_inc(s_init, 1)
                for c in range(CHUNKS):
                    front(0, 0, c, first=True)
                with dve.Fori(0, B // 2 - 1) as i:
                    st.enter(i, 2 * UNITS * 2 * MT)
                    step(i, 0, False)
                    step(i, 1, False)
                st.leave(B // 2 - 1)
                step(B // 2 - 1, 0, False)
                step(B // 2 - 1, 1, True)
                dve.wait_ge(s_ev, B + CR_EV)

            def samples_b():
                def unit_max(u, count):
                    dve.wait_ge(s_s1, count)
                    dve.tensor_reduce(mx[:, :, 2 * u:2 * u + 2].rearrange("p t g -> p g t"),
                                      ps[:, 512 * 4:512 * 4 + UC].rearrange("p (g t m) -> p g t m", g=2, t=MT),
                                      AX_X, ALU.max).then_inc(s_mx, 1)

                def split_max(count):
                    dve.wait_ge(s_mx, count)
                    st.do(dve.tensor_copy(mxh_r[:, :, :], mx[:, :, :]))
                    st.sync()
                    st.do(dve.tensor_scalar(mxs[:, :, 0:H], mxh_r[:, :, :].bitcast(F32), -1.0, None, ALU.mult))
                    st.do(dve.tensor_tensor(mxs[:, :, H:2 * H], mxh_r[:, :, :].bitcast(F32), mx[:, :, :], ALU.subtract))
                    st.sync()
                    dve.sem_inc(s_ms, 1)

                def rows(count):
                    dve.wait_ge(s_mT, count)
                    for g in range(2):
                        last = dve.tensor_copy(mxT[64 * g:64 * g + 2 * H, :], ps[0:2 * H, 512 * 4:512 * 4 + N])
                    last.then_inc(s_mr, 1)

                def step(i, slot, last):
                    if not last:
                        for u in range(UNITS):
                            unit_max(u, after(i, slot, UNITS, UNITS + u + 1))
                        split_max(after(i, slot, UNITS, 2 * UNITS))
                    dve.wait_ge(s_pv, after(i, slot, CHUNKS, CHUNKS, CHUNKS * B))
                    dve.wait_ge(s_os[slot], i * 16 + (16 * (B // 2) + CR_OS))
                    dve.tensor_copy(osb[slot][:, :], ps[:, 512 * 6:512 * 8]).then_inc(s_ev, 1)
                    if not last:
                        rows(after(i, slot, 1, 2))

                dve.wait_ge(s_sel, 32)
                for g in range(2):
                    at = slice(64 * g, 64 * g + 2 * H)
                    st.do(dve.tensor_copy(selh_r[at, :], selh_f[at, :]))
                for u in range(UNITS):
                    unit_max(u, u + 1)
                split_max(UNITS)
                rows(1)
                with dve.Fori(0, B // 2 - 1) as i:
                    st.enter(i, 2 * 3)
                    step(i, 0, False)
                    step(i, 1, False)
                st.leave(B // 2 - 1)
                step(B // 2 - 1, 0, False)
                step(B // 2 - 1, 1, True)
                dve.wait_ge(s_ev, 2 * B + CR_EV)

            def attention_tail(f, i):
                dve.wait_ge(s_oP, lap(f, i) + CR_OP)
                if f == 0:
                    raw = ps[:, 0:4 * 512].rearrange("p (t h c) -> p t h c", h=H, c=VW)
                else:
                    raw = ps[:, 0:4 * 512].rearrange("p (l g c) -> p g l c", g=GTILES, c=VW)
                st.do(dve.reciprocal(rden[:, :, :], raw[:, :, :, HD]))
                st.sync()
                dve.tensor_tensor(otok[:, :, :].rearrange("p t (h c) -> p t h c", c=HD), raw[:, :, :, 0:HD],
                                  rden[:, :, :].unsqueeze(3).broadcast_to([P, GTILES, H, HD]),
                                  ALU.mult).then_inc(s_on, 1)
                dve.wait_ge(s_wo, lap(f, i))
                xg = X[:, bass.ds(i * GTILES, GTILES), :]
                st.do(dve.tensor_tensor(xg, xg, bank(5).rearrange("p (t d) -> p t d", d=P), ALU.add))
                st.sync()
                if f == 1:
                    st.do(dve.tensor_tensor(xg, xg, pb_s[:, :].unsqueeze(1).broadcast_to([P, GTILES, P]), ALU.add))
                    st.sync()

            def route(f, i):
                dve.wait_ge(s_sc, lap(f, i))
                st.do(dve.tensor_tensor(sfc[:, :, :], sc[:, :, :],
                                        eb_s[:, :].unsqueeze(1).broadcast_to([P, GTILES, E]), ALU.add))
                st.sync_apart(s_mark)
                for j in range(GTILES):
                    for g in range(8):
                        st.do(dve.max(m8[:, j, g, :], sfc[:, j, 8 * g:8 * g + 8]))
                st.sync()
                st.do(dve.tensor_tensor(gs[:, :, 0:8], m8[:, :, :, 0], m8[:, :, :, 1], ALU.add))
                st.sync_apart(s_mark)
                for j in range(GTILES):
                    st.do(dve.max(g8[:, j, :], gs[:, j, :]))
                st.sync_apart(s_mark)
                for j in range(GTILES):
                    st.do(dve.match_replace(gr[:, j, :], g8[:, j, :], gs[:, j, :], -BIG))
                st.sync()
                st.do(dve.tensor_scalar(gm[:, :, :], gr[:, :, 0:8], -BIG, None, ALU.is_equal))
                st.sync()
                mk3 = mk[:, :, :].rearrange("p t (g e) -> p (t g) e", e=8)
                st.do(dve.tensor_tensor(mk3, sfc[:, :, :].rearrange("p t (g e) -> p (t g) e", e=8),
                                        gm[:, :, :].rearrange("p t g -> p (t g)").unsqueeze(2)
                                        .broadcast_to([P, GTILES * 8, 8]), ALU.mult))
                st.sync()
                st.do(dve.tensor_scalar(mk[:, :, :], mk[:, :, :], 0.0, None, ALU.add))
                st.sync_apart(s_mark)
                for j in range(GTILES):
                    st.do(dve.max(k8[:, j, :], mk[:, j, :]))
                st.sync_apart(s_mark)
                for j in range(GTILES):
                    st.do(dve.match_replace(mr[:, j, :], k8[:, j, :], mk[:, j, :], -BIG))
                st.sync()
                st.do(dve.scalar_tensor_tensor(wsel[:, :, :], mr[:, :, :], -BIG, sc[:, :, :],
                                               ALU.is_equal, ALU.mult))
                st.sync()
                st.do(dve.tensor_reduce(wsum[:, :], wsel[:, :, :], AX_X, ALU.add))
                st.sync()
                st.do(dve.tensor_scalar(wsum[:, :], wsum[:, :], 1e-20, None, ALU.add))
                st.sync()
                st.do(dve.reciprocal(wrec[:, :], wsum[:, :]))
                st.sync()
                for j in range(GTILES):
                    last = dve.tensor_scalar(coef[:, j, :].rearrange("p (r e) -> p r e", r=2),
                                             wsel[:, j, :].unsqueeze(1).broadcast_to([P, 2, E]),
                                             wrec[:, j:j + 1], ROUTE_SCALE, ALU.mult, ALU.mult)
                last.then_inc(s_cf, 1)

            def prepare_f(f, i):
                attention_tail(f, i)
                norm(2 * f + 1, i, f_xn)
                at = bass.ds(i * GT, GT)
                dve.wait_ge(s_xT, lap(2 * f + 1, i))
                split(xh[:, at], xl[:, at], f_xT[:, :])
                route(f, i)
                dve.wait_ge(s_cT, lap(f, i))
                st.do(dve.tensor_copy(chi[:, :], bank(2)))
                st.do(dve.tensor_copy(cs[0:E, at], bank(2)[0:E, :]))
                st.sync()
                st.do(dve.tensor_tensor(cs[E:2 * E, at], bank(2)[E:2 * E, :], chi[E:2 * E, :], ALU.subtract))
                st.sync()
                dve.sem_inc(s_grp, 1)

            def experts(f):
                s0 = (PAIRS + 1) * FF_STEPS * f
                c0 = PAIRS * FF_STEPS * f - FF_STEPS * (f + 1) - PAIRS * FF_STEPS * f

                def gate_up(n, c, shared):
                    dve.wait_ge(s_sg, n + 1)
                    dve.wait_ge(s_u, n + 1)
                    dve.wait_ge(s_hl, n - 1 + CR_HL)
                    if shared:
                        dve.tensor_tensor(hf[c % 2][:, :], sg[c % 2][:, :], bank(5), ALU.mult).then_inc(s_h1, 1)
                        dve.wait_ge(s_h1, n + 1)
                        dve.sem_inc(s_h, 1)
                        return
                    dve.tensor_tensor(h1[c % 2][:, :], sg[c % 2][:, :], bank(5), ALU.mult).then_inc(s_h1, 1)
                    dve.wait_ge(s_h1, n + 1)
                    dve.wait_ge(s_c, n + (1 - FF_STEPS * (f + 1)))
                    dve.tensor_tensor(hf[c % 2][:, :], h1[c % 2][:, :], bank(6), ALU.mult).then_inc(s_h, 1)

                def low(n, c):
                    dve.wait_ge(s_hh, n)
                    dve.wait_ge(s_yd, n - FF_STEPS + CR_YD)
                    dve.tensor_tensor(hl[c][:, :], hf[c % 2][:, :], hh[c][:, :], ALU.subtract).then_inc(s_hl, 1)

                st.do(dve.memset(zr[:, :].bitcast(F32), 0.0))
                st.sync()
                dve.sem_inc(s_z, 1)
                for c in range(FF_STEPS):
                    gate_up(s0 + c, c, True)
                    if c >= 1:
                        low(s0 + c, c - 1)
                with dve.Fori(0, PAIRS // 2) as i:
                    for s in range(2):
                        for c in range(FF_STEPS):
                            n = i * (2 * FF_STEPS) + (s0 + (s + 1) * FF_STEPS + c)
                            gate_up(n, c, False)
                            low(n, (c - 1) % FF_STEPS)
                end = s0 + (PAIRS + 1) * FF_STEPS
                low(end, FF_STEPS - 1)
                for c in range(FF_STEPS):
                    dve.wait_ge(s_yP, FF_STEPS * f + c + 1)
                    xg = X[:, c * GTILES:(c + 1) * GTILES, :]
                    dve.tensor_tensor(xg, xg, bank(4 + c).rearrange("p (t d) -> p t d", d=P),
                                      ALU.add).then_inc(s_res, 1)
                dve.wait_ge(s_res, FF_STEPS * (f + 1))

            def groups(steps, body):
                with dve.Fori(0, GROUPS) as i:
                    st.enter(i, steps)
                    body(i)
                st.leave(GROUPS)

            dve.sem_inc(s_ev, CR_EV)
            dve.sem_inc(s_hl, CR_HL)
            dve.sem_inc(s_grp, CR_GRP)
            st.do(dve.memset(eps_s[:, :], 1e-5))
            st.sync()
            dve.sem_inc(s_eps, 1)
            dve.wait_ge(s_in, 16 * 9)
            init_v()
            groups(DVE_A, prepare_a)
            meet(dve, 1)
            samples_a()
            meet(dve, 2)
            st.do(dve.memset(gs[:, :, 8:12], BIG))
            groups(DVE_F0, lambda i: prepare_f(0, i))
            meet(dve, 3)
            experts(0)
            meet(dve, 4)
            init_v()
            groups(DVE_B, prepare_b)
            meet(dve, 5)
            samples_b()
            meet(dve, 6)
            st.do(dve.memset(gs[:, :, 8:12], BIG))
            groups(DVE_F0 + 1, lambda i: prepare_f(1, i))
            meet(dve, 7)
            experts(1)


_OUTS = [((8, 256, 128), "float32")]


def _constants():
    import numpy as np
    c = np.zeros((P, C_END), np.float32)
    c[:, C_ID:C_ID + P] = np.eye(P, dtype=np.float32)
    f = np.arange(P)
    c[f, C_HS + f // HD] = 1.0
    half = HD // 2
    for d in range(P):
        if d % HD < half:
            c[d + half, C_ROT + d] = -1.0
        else:
            c[d - half, C_ROT + d] = 1.0
    freq = (1.0 / 10000.0 ** (np.arange(0, HD, 2, dtype=np.float32) / HD)).astype(np.float32)
    pos = (np.arange(GT) % N).astype(np.float32)
    ang = (freq[f % half][:, None] * pos[None, :]).astype(np.float32)
    c[:, C_COS:C_COS + GT] = np.cos(ang)
    c[:, C_SIN:C_SIN + GT] = np.sin(ang)
    selh = np.zeros((2 * H, H * P), np.float32)
    for h in range(H):
        selh[h, h * P:(h + 1) * P] = 1.0
        selh[H + h, h * P:(h + 1) * P] = 1.0
    return c, selh


def _layout(w):
    import numpy as np
    w = {k.replace("L0_", ""): np.ascontiguousarray(v) for k, v in w.items()}
    consts, selh = _constants()
    wA = np.concatenate([w[f"attn_a_{n}"].T for n in ("Wq", "Wk", "Wv", "Wo")], axis=1)
    wB = np.concatenate([w["attn_b_qkv_w"].T, w["attn_b_proj_w"].T], axis=1)
    bqk = w["attn_b_qkv_b"][:2 * P].reshape(2, P).T
    brow = np.concatenate([w["attn_b_qkv_b"][2 * P:], w["attn_b_proj_b"], w["ffn_e_bias"]])[None]
    wexp = np.zeros((PAIRS + 1, P, 4 * P), np.float32)
    for k, n in enumerate(("ffn_Wg", "ffn_Wu")):
        wexp[:PAIRS, :, k * P:(k + 1) * P] = w[n].reshape(PAIRS, 2, P, I).transpose(0, 2, 1, 3).reshape(PAIRS, P, P)
    wexp[:PAIRS, :, 2 * P:3 * P] = w["ffn_Wd"].reshape(PAIRS, P, P)
    for k, n in enumerate(("ffn_SWg", "ffn_SWu", "ffn_SWd")):
        wexp[PAIRS, :, k * P:(k + 1) * P] = w[n]
    for p in range(PAIRS):
        for e in range(2):
            for half in range(2):
                wexp[p, half * E + 2 * p + e, 3 * P + e * I:3 * P + (e + 1) * I] = 1.0
    return {"x": w["attn_a_x"], "consts": consts, "selh": selh, "wA": wA, "wB": wB, "bqk": bqk,
            "brow": brow, "rwT": w["ffn_router_w"].T, "wexp": wexp}


def kernel(**inputs):
    import numpy as _np
    import concourse.bacc as _bacc
    from concourse import mybir as _mybir
    from concourse.bass_utils import run_bass_kernel_spmd as _run

    nc = _bacc.Bacc("TRN2", target_bir_lowering=False, num_devices=1)
    arrays, args = {}, []
    for name, a in _layout(inputs).items():
        a = _np.ascontiguousarray(a)
        arrays[f"in_{name}_dram"] = a
        args.append(nc.dram_tensor(f"in_{name}_dram", a.shape, _mybir.dt.from_np(a.dtype), kind="ExternalInput").ap())
    for i, (shape, dtype) in enumerate(_OUTS):
        dt = _mybir.dt.from_np(_np.dtype(dtype))
        args.append(nc.dram_tensor(f"out_{i}_dram", shape, dt, kind="ExternalOutput").ap())
    hybrid(nc, *args)
    r = _run(nc, [arrays], core_ids=[0])
    return r.results[0]["out_0_dram"]
```

```python
from contextlib import ExitStack

import concourse.bass as bass
from concourse import mybir

F32 = mybir.dt.float32
F32R = mybir.dt.float32r
ALU = mybir.AluOpType
ACT = mybir.ActivationFunctionType
AX_X = mybir.AxisListType.X

P = 128
B, N = 8, 256
T = B * N
TILES = T // P
H, HD = 16, 8
E, I = 64, 64
PAIRS = E // 2
GROUPS = 4
GT = T // GROUPS
GTILES = GT // P
UNITS = H // 2
CHUNKS = H // 4
MT = N // P
UC = 2 * MT * N
VW = 32
VB = H * VW + H
KQ = 4 * HD
KS = KQ + 4
SLOTS_B = 3
HALF = UNITS // 2
BIG = float(2 ** 100)
FF_TOK = 512
FF_STEPS = T // FF_TOK
SCALE_B = HD ** -0.5
STORES = (14, 9)
LOADS = (6, 5)
CR_YD, CR_WS, CR_EV, CR_OS, CR_OP, CR_GRP, CR_SCR, CR_SPL, CR_HL, CR_MX, CR_MT, CR_W, CR_PV = FF_STEPS, 1, 2, 16, 2, 2, 16, 2, 2, 2, 2, 4, 4
DVE_N = 2 * GTILES + 2
DVE_A = DVE_N + 2 * (2 + 3)
DVE_B = DVE_N + 2 * (2 + 2 + 2)
DVE_F = DVE_N + 2 * (1 + 1 + 1 + 14 + 1)
E_A = (H // 4) * B
ROUTE_SCALE = 2.5

C_ID, C_HS, C_ROT, C_COS, C_SIN, C_END = 0, 128, 144, 272, 784, 1296


class Steps:

    def __init__(self, eng, sem):
        self.eng, self.sem, self.n, self.off = eng, sem, 0, 0

    def do(self, ins):
        ins.then_inc(self.sem, 1)
        self.n += 1

    def sync(self):
        self.eng.wait_ge(self.sem, self.off + self.n)

    def sync_apart(self, mark):
        self.sync()
        self.eng.sem_inc(mark, 1)

    def enter(self, i, per):
        self.start, self.per, self.off = self.n, per, i * per

    def leave(self, trips):
        assert self.n - self.start == self.per, (self.n - self.start, self.per)
        self.n, self.off = self.start + trips * self.per, 0


def hybrid(nc, x, consts, wA, wB, bqk, brow, rwT, wexp, out):
    ctx = ExitStack()

    def sem(name):
        return ctx.enter_context(nc.semaphore(name))

    def dram(name, shape, dt):
        return nc.dram_tensor(name, shape, dt, kind="Internal").ap()

    q_d = dram("q_stack", [2, KS, UNITS, T], F32)
    k_d = dram("k_stack", [2, KS, UNITS, T], F32)
    a_d = dram("one_minus_q_norm", [H, T], F32)
    vb_d = dram("v_and_b", [T, VB], F32)
    o_d = dram("attn_unnormalised", [B, P, 4 * N], F32)

    with ctx:
        def keep(name, shape, dt=F32):
            return ctx.enter_context(nc.sbuf_tensor(name, shape, dt))

        X = keep("X", [P, TILES, P])
        cst = keep("cst", [P, C_END])
        wa = keep("wa", [P, 4 * P])
        wb = keep("wb", [P, 4 * P])
        bqk_s = keep("bqk_s", [P, 2])
        bv_s = keep("bv_s", [P, P])
        pb_s = keep("pb_s", [P, P])
        eb_s = keep("eb_s", [P, E])
        rw_s = keep("rw_s", [P, E])
        eps_s = keep("eps_s", [P, 1])
        stats = [keep(f"stats{g}", [P, GTILES, 6]) for g in range(2)]
        mv = [keep(f"mv{g}", [P, GTILES, 2]) for g in range(2)]
        std = [keep(f"std{g}", [P, GTILES]) for g in range(2)]
        rstd = [keep(f"rstd{g}", [P, GTILES]) for g in range(2)]
        ident = cst[:, C_ID:C_ID + P]
        HS = cst[:, C_HS:C_HS + H]
        ROT = cst[:, C_ROT:C_ROT + P]

        ps = ctx.enter_context(nc.psum_tensor("ps", [P, 8 * 512], F32))

        def bank(n, k=1):
            return ps[:, 512 * n:512 * (n + k)]

        with ExitStack() as pre:
            def sb(name, shape, dt=F32):
                return pre.enter_context(nc.sbuf_tensor(name, shape, dt))
            def two(name, shape, dt=F32):
                return [sb(f"{name}{g}", shape, dt) for g in range(2)]
            xn = two("xn", [P, GTILES, P])
            xT = two("xT", [P, GT])
            sqq = two("sqq", [P, GT])
            sqk = two("sqk", [P, GT])
            q2 = two("q2", [P, GT])
            k2 = two("k2", [P, GT])
            rt = two("rt", [P, 2, GT])
            qh = two("qh", [P, GT], F32R)
            ql = two("ql", [P, GT], F32R)
            kh = two("kh", [P, GT], F32R)
            kl = two("kl", [P, GT], F32R)
            nh = two("nh", [P, GT], F32R)
            nl = two("nl", [P, GT], F32R)
            arow = two("arow", [H, GT])
            vb = two("vb", [P, GTILES, VB])
            ones = sb("ones", [P, 2 * UNITS * T // P])
            zeros = sb("zeros", [P, 2 * UNITS * T // P])
        with ExitStack() as att:
            def sb(name, shape, dt=F32):
                return att.enter_context(nc.sbuf_tensor(name, shape, dt))
            qst = [sb(f"qst{s}", [P, UNITS, N], F32R) for s in range(2)]
            kst = [sb(f"kst{s}", [P, UNITS, N], F32R) for s in range(2)]
            vbs = [sb(f"vbs{s}", [P, MT, VB]) for s in range(2)]
            osb = [sb(f"osb{s}", [P, 4 * N]) for s in range(2)]
            with ExitStack() as a_only:
                abc = [a_only.enter_context(nc.sbuf_tensor(f"abc{s}", [P, H, N], F32)) for s in range(2)]
                Nt = a_only.enter_context(nc.sbuf_tensor("Nt", [P, CHUNKS, 2 * UC], F32))
                St = a_only.enter_context(nc.sbuf_tensor("St", [P, CHUNKS, 2 * UC], F32))
                Dt = a_only.enter_context(nc.sbuf_tensor("Dt", [P, CHUNKS, 2 * UC], F32))
            qst_b = qst + [sb("qst2", [P, UNITS, N], F32R)]
            kst_b = kst + [sb("kst2", [P, UNITS, N], F32R)]
            vbs_b = vbs + [sb("vbs2", [P, MT, VB])]
            osb_b = osb + [sb("osb2", [P, 4 * N])]
            Wt = sb("Wt", [P, CHUNKS, 2 * UC])
            mx = sb("mx", [P, 2, MT, 2 * HALF])
            mxh_r = sb("mxh_r", [P, 2, MT, 2 * HALF], F32R)
            mxs = sb("mxs", [P, 2, MT, 2, 2, HALF])
            mxT = [sb(f"mxT{f}", [4 * HALF, N], F32R) for f in range(2)]
        with ExitStack() as ffn:
            def sb(name, shape, dt=F32):
                return ffn.enter_context(nc.sbuf_tensor(name, shape, dt))
            xh = sb("xh", [P, T], F32R)
            xl = sb("xl", [P, T], F32R)
            cs = sb("cs", [P, T], F32R)
            with ExitStack() as rtr:
                def sr(name, shape, dt=F32):
                    return rtr.enter_context(nc.sbuf_tensor(name, shape, dt))
                def two(name, shape, dt=F32):
                    return [sr(f"{name}{g}", shape, dt) for g in range(2)]
                f_xn = two("f_xn", [P, GTILES, P])
                f_xT = two("f_xT", [P, GT])
                ou = two("ou", [P, 2, 4 * N])
                rden = two("rden", [P, GTILES, H])
                otok = two("otok", [P, GTILES, P])
                oT = two("oT", [P, GT])
                sc = two("sc", [P, GTILES, E])
                sfc = two("sfc", [P, GTILES, E])
                m8 = two("m8", [P, GTILES, 8, 8])
                gs = two("gs", [P, GTILES, 12])
                g8 = two("g8", [P, GTILES, 8])
                gr = two("gr", [P, GTILES, 12])
                gm = two("gm", [P, GTILES, 8])
                mk = two("mk", [P, GTILES, E])
                k8 = two("k8", [P, GTILES, 8])
                mr = two("mr", [P, GTILES, E])
                wsel = two("wsel", [P, GTILES, E])
                wsum = two("wsum", [P, GTILES])
                wrec = two("wrec", [P, GTILES])
                coef = two("coef", [P, GTILES, 2 * E])
                chi = two("chi", [P, GT], F32R)
            wraw = [sb(f"wraw{s}", [P, 4 * P]) for s in range(2)]
            whi = [sb(f"whi{s}", [P, 4 * P], F32R) for s in range(2)]
            wlo = [sb(f"wlo{s}", [P, 3 * P], F32R) for s in range(2)]
            sg = [sb(f"sg{s}", [P, FF_TOK]) for s in range(2)]
            h1 = [sb(f"h1{s}", [P, FF_TOK]) for s in range(2)]
            hf = [sb(f"hf{s}", [P, FF_TOK]) for s in range(2)]
            hh = [sb(f"hh{s}", [P, FF_TOK], F32R) for s in range(4)]
            hl = [sb(f"hl{s}", [P, FF_TOK], F32R) for s in range(4)]
            zr = sb("zr", [P, FF_TOK], F32R)
            yT = sb("yT", [P, T])

        s_in = sem("inputs_loaded")
        s_out = sem("output_stored")
        s_phase = sem("phase_done")
        s_mark = sem("wait_carrier")
        s_eps = sem("eps_ready")
        s_stat = sem("stats_ready")
        s_std = sem("std_ready")
        s_xn = sem("xn_ready")
        s_xnT = sem("xnT_in_psum")
        s_xT = sem("xT_ready")
        s_qkv = sem("qkv_in_psum")
        s_sq = sem("squares_ready")
        s_nrm = sem("norms_in_psum")
        s_rot = sem("rotated_in_psum")
        s_vc = sem("v_copied")
        s_nh = sem("norm_highs_ready")
        s_cos = sem("cosine_parts_ready")
        s_qk2 = sem("rotated_ready")
        s_qk2h = sem("rotated_highs_ready")
        s_xh = sem("x_high_ready")
        s_ch = sem("coef_highs_ready")
        s_spl = sem("splits_ready")
        s_scr = [sem(f"scratch_stored{g}") for g in range(2)]
        s_ou = [sem(f"unnormalised_loaded{g}") for g in range(2)]
        s_oP = sem("o_token_major_in_psum")
        s_on = sem("o_normalised")
        s_oT = sem("oT_in_psum")
        s_oTs = sem("oT_ready")
        s_wo = sem("projection_in_psum")
        s_lg = sem("logits_in_psum")
        s_sc = sem("scores_ready")
        s_cf = sem("coef_ready")
        s_cT = sem("coefT_in_psum")
        s_grp = sem("group_used")
        s_init = sem("ones_ready")
        s_one = sem("ones_stored")
        s_ldb = [sem(f"b_sample_loaded{s}") for s in range(SLOTS_B)]
        s_osb = [sem(f"b_o_stored{s}") for s in range(SLOTS_B)]
        s_mxl = [sem(f"b_max_rows_loaded{f}") for f in range(2)]
        s_ld = [sem(f"sample_loaded{s}") for s in range(2)]
        s_s = sem("diff_in_psum")
        s_fr = sem("diff_read")
        s_rt = sem("roots_ready")
        s_yp = sem("root_sum_of_even_chunk_ready")
        s_y = sem("root_sum_of_odd_chunk_ready")
        s_e = sem("inverse_square_ready")
        s_w = sem("weights_ready")
        s_pv = sem("pv_in_psum")
        s_ev = sem("pv_copied")
        s_os = [sem(f"o_stored{s}") for s in range(2)]
        s_s1 = sem("b_scores_in_psum")
        s_mx = sem("b_head_max_read")
        s_ms = sem("b_max_split_ready")
        s_mT = sem("b_maxT_in_psum")
        s_mr = sem("b_maxT_ready")
        s_s2 = sem("b_shifted_in_psum")
        s_wl = [sem(f"expert_weights_loaded{s}") for s in range(2)]
        s_ws = sem("expert_weights_split")
        s_z = sem("zero_ready")
        s_g = sem("gate_in_psum")
        s_u = sem("up_in_psum")
        s_c = sem("coef_in_psum")
        s_sg = sem("silu_ready")
        s_h1 = sem("gate_up_ready")
        s_h = sem("h_ready")
        s_hh = sem("h_hi_ready")
        s_hl = sem("h_lo_ready")
        s_yd = sem("down_done")
        s_yT = sem("yT_ready")
        s_yP = sem("y_token_major_in_psum")
        s_res = sem("residual_added")
        s_dve = sem("dve_steps")
        s_act = sem("act_steps")
        s_pool = sem("pool_steps")

        block = ctx.enter_context(nc.Block())

        def meet(eng, n):
            eng.sem_inc(s_phase, 1)
            eng.wait_ge(s_phase, 5 * n)

        def lap(stage, i, g):
            return i * 2 + (GROUPS * stage + g + 1)

        def group(i, g, width=GT):
            return bass.ds(i * (2 * width) + g * width, width)

        def groups(eng, body):
            with eng.Fori(0, GROUPS // 2) as i:
                body(i)

        def samples(eng, step):
            with eng.Fori(0, B // 2 - 1) as i:
                step(i, 0, False)
                step(i, 1, False)
            step(B // 2 - 1, 0, False)
            step(B // 2 - 1, 1, True)

        def after(i, slot, per, k, base=0):
            return i * (2 * per) + (slot * per + k + base)

        def samples_of_b(eng, step, enter=lambda i: None, leave=lambda: None):
            with eng.Fori(0, B // SLOTS_B) as i:
                enter(i)
                for slot in range(SLOTS_B):
                    step(i, slot, False)
            leave()
            for slot in range(B % SLOTS_B):
                step(B // SLOTS_B, slot, slot == B % SLOTS_B - 1)

        def after_b(i, slot, per, k, base=0):
            return i * (SLOTS_B * per) + (slot * per + k + base)

        @block.sync
        def _(sp):
            sp.dma_start(X[:, :, :], x.rearrange("b (m p) d -> p (b m) d", p=P)).then_inc(s_in, 16)
            sp.dma_start(cst[:, :], consts).then_inc(s_in, 16)
            sp.dma_start(wa[:, :], wA).then_inc(s_in, 16)
            sp.dma_start(wb[:, :], wB).then_inc(s_in, 16)
            sp.dma_start(bqk_s[:, :], bqk).then_inc(s_in, 16)
            sp.dma_start(bv_s[:, :], brow[0:1, 0:P].broadcast_to([P, P])).then_inc(s_in, 16)
            sp.dma_start(pb_s[:, :], brow[0:1, P:2 * P].broadcast_to([P, P])).then_inc(s_in, 16)
            sp.dma_start(eb_s[:, :], brow[0:1, 2 * P:2 * P + E].broadcast_to([P, E])).then_inc(s_in, 16)
            sp.dma_start(rw_s[:, :], rwT).then_inc(s_in, 16)
            sp.wait_ge(s_in, 16 * 9)

            def store_splits(stage, i):
                for g in range(2):
                    at = group(i, g)
                    sp.wait_ge(s_spl, lap(stage, i, g) + CR_SPL)
                    def rows(d, r):
                        return d[:, HD * r:HD * (r + 1), :, at].rearrange("g j t n -> g (j t) n")

                    todo = [(rows(q_d, r), (qh, qh, ql, ql)[r][g]) for r in range(4)]
                    todo += [(rows(k_d, r), (kh, kl, kh, kl)[r][g]) for r in range(4)]
                    todo = [(to, of[:, :].bitcast(F32)) for to, of in todo]
                    todo += [(vb_d[at, :].rearrange("(t p) c -> p t c", p=P), vb[g][:, :, :])]
                    if stage == 0:
                        todo += [(d[:, KQ + off + r, :, at].rearrange("g t n -> t g n"), t[g][row:row + H, :].bitcast(F32))
                                 for d, off, row in ((q_d, 0, 0), (k_d, 2, 32)) for r, t in enumerate((nh, nl))]
                        todo += [(a_d[:, at], arow[g][:, :])]
                    assert len(todo) == STORES[stage]
                    for to, of in todo:
                        sp.dma_start(to, of).then_inc(s_scr[g], 16)

            def load(at, q, k, v, loaded):
                for g in range(2):
                    for to, of in ((q, q_d), (k, k_d)):
                        sp.dma_start(to[64 * g:64 * g + KS, :, :].bitcast(F32), of[g, :, :, at]
                                     ).then_inc(loaded, 16)
                sp.dma_start(v[:, :, :], vb_d[at, :].rearrange("(m p) c -> p m c", p=P)).then_inc(loaded, 16)

            def samples_a():
                def load_sample(i, slot):
                    at = bass.ds(i * (2 * N) + slot * N, N)
                    load(at, qst[slot], kst[slot], vbs[slot], s_ld[slot])
                    sp.dma_start(abc[slot][:, :, :], a_d[:, at].partition_broadcast(P)).then_inc(s_ld[slot], 16)

                load_sample(0, 0)
                load_sample(0, 1)

                def step(i, slot, last):
                    if not (isinstance(i, int)):
                        sp.wait_ge(s_pv, after(i, slot, CHUNKS, CHUNKS, CR_PV))
                        load_sample(i + 1, slot)
                    sp.wait_ge(s_ev, after(i, slot, 1, 1, CR_EV))
                    sp.dma_start(o_d[bass.ds(i * 2 + slot, 1), :, :].rearrange("a p n -> p (a n)"),
                                 osb[slot][:, :]).then_inc(s_os[slot], 16)
                samples(sp, step)
                for s in range(2):
                    sp.wait_ge(s_os[s], 16 * (B // 2) + CR_OS)

            def samples_b():
                def load_sample(i, slot):
                    load(bass.ds(i * (SLOTS_B * N) + slot * N, N), qst_b[slot], kst_b[slot], vbs_b[slot],
                         s_ldb[slot])

                def max_rows(i, slot, half):
                    sp.wait_ge(s_mr, after_b(i, slot, 2, half + 1))
                    for g in range(2):
                        for part in range(2):
                            row = (2 * g + part) * HALF
                            to = 64 * g + KQ + part
                            sp.dma_start(qst_b[slot][to:to + 1, half * HALF:(half + 1) * HALF, :].bitcast(F32),
                                         mxT[half][row:row + HALF, :].bitcast(F32)).then_inc(s_mxl[half], 16)

                load_sample(0, 0)
                load_sample(0, 1)
                max_rows(0, 0, 0)
                max_rows(0, 0, 1)

                def step(i, slot, last):
                    if not isinstance(i, int):
                        sp.wait_ge(s_pv, after_b(i, slot, CHUNKS, 0, CHUNKS * B + CR_PV))
                        load_sample(i + (slot + 2) // SLOTS_B, (slot + 2) % SLOTS_B)
                    if not last:
                        for half in range(2):
                            max_rows(i + (slot + 1) // SLOTS_B, (slot + 1) % SLOTS_B, half)
                    sp.wait_ge(s_ev, after_b(i, slot, 1, 1, B + CR_EV))
                    sp.dma_start(o_d[bass.ds(i * SLOTS_B + slot, 1), :, :].rearrange("a p n -> p (a n)"),
                                 osb_b[slot][:, :]).then_inc(s_osb[slot], 16)
                samples_of_b(sp, step)
                for s in range(SLOTS_B):
                    sp.wait_ge(s_osb[s], 16 * ((B - s - 1) // SLOTS_B + 1) + CR_OS)

            def experts_phase(f):
                base = (PAIRS + 1) * f
                sp.dma_start(wraw[1][:, :], wexp[PAIRS]).then_inc(s_wl[1], 16)
                with sp.Fori(0, PAIRS // 2) as i:
                    for s in range(2):
                        sp.wait_ge(s_ws, i * 2 + (base + s + CR_WS))
                        sp.dma_start(wraw[s][:, :], wexp[bass.ds(i * 2 + s, 1), :, :].rearrange("a p n -> p (a n)")
                                     ).then_inc(s_wl[s], 16)

            def prepare_f(f):
                with sp.Fori(0, GROUPS // 2) as i:
                    for g in range(2):
                        sp.wait_ge(s_oP, i * 2 + (GROUPS * f + g - 1 + CR_OP))
                        if f == 0:
                            to = ou[g][:, :, :]
                            of = o_d[bass.ds(i * 4 + g * 2, 2), :, :].rearrange("a p n -> p a n")
                        else:
                            to = ou[g][:, :, :].rearrange("p a n -> p (a n)").rearrange("p (b n) -> p b n", n=N)
                            of = o_d[:, :, group(i, g, N)].rearrange("b p n -> p b n")
                        sp.dma_start(to, of).then_inc(s_ou[g], 16)

            for s in range(2):
                sp.sem_inc(s_scr[s], CR_SCR)
                sp.sem_inc(s_os[s], CR_OS)
            for s in range(SLOTS_B):
                sp.sem_inc(s_osb[s], CR_OS)
            for half in range(2):
                sp.sem_inc(s_mxl[half], CR_OS)
            def constant_rows(todo):
                for g in range(2):
                    for d, row, of in todo:
                        to = d[g, row:row + 2, :, :].rearrange("r t n -> (r t n)").rearrange("(p c) -> p c", p=P)
                        sp.dma_start(to, of[:, :]).then_inc(s_one, 16)

            sp.wait_ge(s_init, 1)
            constant_rows(((q_d, KQ + 2, ones), (k_d, KQ, ones)))
            groups(sp, lambda i: store_splits(0, i))
            for g in range(2):
                sp.wait_ge(s_scr[g], 2 * 16 * STORES[0] + CR_SCR)
            sp.wait_ge(s_one, 4 * 16)
            meet(sp, 1)
            samples_a()
            meet(sp, 2)
            prepare_f(0)
            meet(sp, 3)
            experts_phase(0)
            meet(sp, 4)
            sp.wait_ge(s_init, 2)
            constant_rows(((q_d, KQ, zeros), (q_d, KQ + 2, zeros), (k_d, KQ + 2, ones)))
            groups(sp, lambda i: store_splits(1, i))
            for g in range(2):
                sp.wait_ge(s_scr[g], 2 * 16 * (STORES[0] + STORES[1]) + CR_SCR)
            sp.wait_ge(s_one, (4 + 6) * 16)
            meet(sp, 5)
            samples_b()
            meet(sp, 6)
            prepare_f(1)
            meet(sp, 7)
            experts_phase(1)
            sp.wait_ge(s_res, 2 * FF_STEPS)
            sp.dma_start(out.rearrange("b (m p) d -> p (b m) d", p=P), X[:, :, :]).then_inc(s_out, 16)
            sp.wait_ge(s_out, 16)

        @block.tensor
        def _(pe):
            def mm(o, l, r, start=True, stop=True, **kw):
                return pe.matmul(o, l, r, start=start, stop=stop, **kw)

            def norm_transposed(stage, i, xn_, b):
                for g in range(2):
                    pe.wait_ge(s_xn, lap(stage, i, g))
                    for j in range(GTILES):
                        last = pe.transpose(bank(4 * g + b)[:, j * P:(j + 1) * P], xn_[g][:, j, :], ident)
                    last.then_inc(s_xnT, 1)

            def prepare_qkv(k, i):
                w = (wa, wb)[k]
                pe.wait_ge(s_spl, i * 2 + (GROUPS * k + CR_SPL))
                norm_transposed(2 * k, i, xn, 0)
                for g in range(2):
                    pe.wait_ge(s_xT, lap(2 * k, i, g))
                    mm(bank(4 * g + 1), w[:, 0:P], xT[g][:, :])
                    mm(bank(4 * g + 2), w[:, P:2 * P], xT[g][:, :])
                    for j in range(GTILES):
                        last = mm(bank(4 * g + 3)[:, j * P:(j + 1) * P], xT[g][:, j * P:(j + 1) * P],
                                  w[:, 2 * P:3 * P])
                    last.then_inc(s_qkv, 1)
                for g in range(2):
                    b = 512 * 4 * g
                    pe.wait_ge(s_sq, lap(k, i, g))
                    pe.wait_ge(s_vc, lap(k, i, g))
                    if k == 0:
                        mm(ps[0:H, b:b + GT], HS, sqq[g][:, :])
                        mm(ps[32:32 + H, b:b + GT], HS, sqk[g][:, :])
                        for j in range(GTILES):
                            last = mm(bank(4 * g + 3)[:, j * H:(j + 1) * H], sqk[g][:, j * P:(j + 1) * P], HS)
                        last.then_inc(s_nrm, 1)
                    else:
                        mm(bank(4 * g), ROT, sqq[g][:, :])
                        mm(bank(4 * g + 3), ROT, sqk[g][:, :]).then_inc(s_rot, 1)

            def pv(i, slot, c, wt, phase, min_rows=None):
                vs = (vbs, vbs_b)[phase][slot]
                if phase == 0:
                    b0 = 4 + 2 * slot
                    pe.wait_ge(s_w, after(i, slot, CHUNKS, c + 1, CR_W))
                    pe.wait_ge(s_ev, after(i, slot, 1, CR_EV - 1))
                else:
                    b0 = 6
                    pe.wait_ge(s_e, after_b(i, slot, UNITS, 2 * c + 2, E_A))
                    pe.wait_ge(s_ev, after_b(i, slot, 1, 0, B + CR_EV))
                    if c == 2:
                        pe.wait_ge(s_mr, min_rows)
                for mt in range(MT):
                    for g in range(4):
                        h = 4 * c + g
                        col = (g * MT + mt) * N
                        last = mm(ps[32 * g:32 * g + VW, 512 * b0 + c * N:512 * b0 + (c + 1) * N],
                                  vs[:, mt, h * VW:(h + 1) * VW], wt[:, c, col:col + N],
                                  start=(mt == 0), stop=(mt == MT - 1), tile_position=(0, 32 * g))
                last.then_inc(s_pv, 1)

            def a_scores(i, slot, u):
                b0 = 2 * (u % 2)
                for g in range(2):
                    for mt in range(MT):
                        col = 512 * b0 + (g * MT + mt) * N
                        last = mm(ps[:, col:col + N], kst[slot][64 * g:64 * g + KS, u, mt * P:(mt + 1) * P],
                                  qst[slot][64 * g:64 * g + KS, u, :])
                last.then_inc(s_s, 1)

            def samples_a():
                pe.wait_ge(s_ld[0], 16 * LOADS[0])
                for u in range(UNITS):
                    if u >= 2:
                        pe.wait_ge(s_fr, u - 1)
                    a_scores(0, 0, u)

                def step(i, slot, last):
                    ni, ns = (i, 1) if slot == 0 else (i + 1, 0)
                    if not last:
                        pe.wait_ge(s_ld[ns], ni * (16 * LOADS[0]) + 16 * LOADS[0])
                    for c in range(CHUNKS):
                        pv(i, slot, c, St, 0)
                        if not last:
                            for u in (2 * c, 2 * c + 1):
                                pe.wait_ge(s_fr, after(i, slot, UNITS, UNITS + u - 1))
                                a_scores(ni, ns, u)
                samples(pe, step)
                pe.wait_ge(s_pv, CHUNKS * B + CR_PV)

            def b_scores(i, slot, u):
                for g in range(2):
                    pe.wait_ge(s_mx, after_b(i, slot, H, 2 * u + g - 1, CR_MX))
                    for nt in range(MT):
                        col = 512 * (4 + g) + nt * N
                        last = mm(ps[:, col:col + N], qst_b[slot][64 * g:64 * g + KS, u, nt * P:(nt + 1) * P],
                                  kst_b[slot][64 * g:64 * g + KS, u, :])
                    last.then_inc(s_s1, 1)

            def b_max_rows(i, slot, half):
                pe.wait_ge(s_ms, after_b(i, slot, 2, half + 1))
                for nt in range(MT):
                    col = 512 * 7 + N + nt * P
                    tr = pe.transpose(ps[0:4 * HALF, col:col + P],
                                      mxs[:, half, nt, :, :, :].rearrange("p g r u -> p (g r u)"), ident)
                tr.then_inc(s_mT, 1)

            def b_shifted(i, slot, u):
                b0 = 2 * (u % 2)
                for g in range(2):
                    for mt in range(MT):
                        col = 512 * b0 + (g * MT + mt) * N
                        last = mm(ps[:, col:col + N], kst_b[slot][64 * g:64 * g + KS, u, mt * P:(mt + 1) * P],
                                  qst_b[slot][64 * g:64 * g + KS, u, :])
                last.then_inc(s_s2, 1)

            def samples_b():
                pe.wait_ge(s_ldb[0], 16 * LOADS[1])
                for u in range(UNITS):
                    b_scores(0, 0, u)
                    if u == HALF:
                        b_max_rows(0, 0, 0)

                def step(i, slot, last):
                    ni, ns = i + (slot + 1) // SLOTS_B, (slot + 1) % SLOTS_B
                    for u in range(UNITS):
                        if u % HALF == 0:
                            pe.wait_ge(s_mxl[u // HALF], after_b(i, slot, 4 * 16, 4 * 16, CR_OS))
                        pe.wait_ge(s_e, after_b(i, slot, UNITS, u - 1, E_A))
                        b_shifted(i, slot, u)
                        if u == 1:
                            pe.wait_ge(s_ev, after_b(i, slot, 1, 0, B + CR_EV))
                            b_max_rows(i, slot, 1)
                        if not last:
                            if u == 0:
                                pe.wait_ge(s_ldb[ns], ni * (16 * LOADS[1]) + 16 * LOADS[1])
                            b_scores(ni, ns, u)
                            if u == HALF + 1:
                                pe.wait_ge(s_mr, after_b(i, slot, 2, 2))
                                b_max_rows(ni, ns, 0)
                        if u % 2 == 1 and u >= 3:
                            pv(i, slot, u // 2 - 1, Wt, 1, after_b(i, slot, 2, 2 if last else 3))
                    pv(i, slot, CHUNKS - 1, Wt, 1)
                samples_of_b(pe, step)
                pe.wait_ge(s_pv, 2 * CHUNKS * B + CR_PV)

            def prepare_f(f, i):
                pe.wait_ge(s_grp, i * 2 + (GROUPS * f + CR_GRP))
                for g in range(2):
                    pe.wait_ge(s_ou[g], i * 16 + (16 * (GROUPS // 2) * f + 16))
                    b = 512 * 4 * g
                    if f == 0:
                        for b2 in range(2):
                            for nt in range(MT):
                                for hg in range(CHUNKS):
                                    col = b + 512 * (2 * b2 + nt) + hg * P
                                    last = pe.transpose(ps[:, col:col + P],
                                                        ou[g][:, b2, hg * N + nt * P:hg * N + (nt + 1) * P], ident)
                    else:
                        by16 = ou[g][:, :, :].rearrange("p a n -> p (a n)").rearrange("p (r l) -> p l r", l=P // HD)
                        for low in range(P // HD):
                            last = pe.transpose(ps[:, b + low * P:b + (low + 1) * P], by16[:, low, :], ident)
                    last.then_inc(s_oP, 1)
                for g in range(2):
                    pe.wait_ge(s_on, lap(f, i, g))
                    for j in range(GTILES):
                        last = pe.transpose(bank(4 * g)[:, j * P:(j + 1) * P], otok[g][:, j, :], ident)
                    last.then_inc(s_oT, 1)
                for g in range(2):
                    pe.wait_ge(s_oTs, lap(f, i, g))
                    for j in range(GTILES):
                        last = mm(bank(4 * g + 1)[:, j * P:(j + 1) * P], oT[g][:, j * P:(j + 1) * P],
                                  (wa, wb)[f][:, 3 * P:4 * P])
                    last.then_inc(s_wo, 1)
                norm_transposed(2 * f + 1, i, f_xn, 2)
                for g in range(2):
                    pe.wait_ge(s_xT, lap(2 * f + 1, i, g))
                    for j in range(GTILES):
                        last = mm(bank(4 * g + 3)[:, j * E:(j + 1) * E], f_xT[g][:, j * P:(j + 1) * P], rw_s[:, :])
                    last.then_inc(s_lg, 1)
                for g in range(2):
                    pe.wait_ge(s_cf, lap(f, i, g))
                    for j in range(GTILES):
                        last = pe.transpose(bank(4 * g)[:, j * P:(j + 1) * P], coef[g][:, j, :], ident)
                    last.then_inc(s_cT, 1)

            def experts(f):
                s0 = (PAIRS + 1) * FF_STEPS * f
                w0 = (PAIRS + 1) * f

                def y(n, slot, chunk):
                    pe.wait_ge(s_hl, n + CR_HL)
                    hi, lo = hh[chunk], hl[chunk]
                    for k, (l, r) in enumerate(((whi[slot], hi), (whi[slot], lo), (wlo[slot], hi))):
                        last = mm(bank(chunk), l[:, 2 * P:3 * P], r[:, :], start=False, stop=False,
                                  skip_group_check=True)
                    last.then_inc(s_yd, 1)

                def gate_up(n, slot, chunk, first, shared):
                    cols = slice(chunk * FF_TOK, (chunk + 1) * FF_TOK)
                    hi, lo = whi[slot], wlo[slot]
                    if not first:
                        pe.wait_ge(s_sg, n)
                    for k, (l, r) in enumerate(((hi, xh), (hi, xl), (lo, xh))):
                        last = mm(bank(4), l[:, 0:P], r[:, cols], start=(k == 0), stop=(k == 2))
                    last.then_inc(s_g, 1)
                    if not first:
                        pe.wait_ge(s_h1, n)
                    for k, (l, r) in enumerate(((hi, xh), (hi, xl), (lo, xh))):
                        last = mm(bank(5), l[:, P:2 * P], r[:, cols], start=(k == 0), stop=(k == 2))
                    last.then_inc(s_u, 1)
                    if not first:
                        pe.wait_ge(s_h, n)
                    if not shared:
                        mm(bank(6), hi[:, 3 * P:4 * P], cs[:, cols]).then_inc(s_c, 1)

                pe.wait_ge(s_z, f + 1)
                for c in range(FF_STEPS):
                    mm(bank(c), zr[:, 0:P], zr[:, :], start=True, stop=False, skip_group_check=True)
                pe.wait_ge(s_ws, w0 + 1 + CR_WS)
                for c in range(FF_STEPS):
                    gate_up(s0 + c, 1, c, c == 0, True)
                    if c >= 2:
                        y(s0 + c - 1, 1, c - 2)
                with pe.Fori(0, PAIRS // 2) as i:
                    for s in range(2):
                        pe.wait_ge(s_ws, i * 2 + (w0 + 2 + s + CR_WS))
                        for c in range(FF_STEPS):
                            n = i * (2 * FF_STEPS) + (s0 + (s + 1) * FF_STEPS + c)
                            gate_up(n, s, c, False, False)
                            y(n - 1, s if c >= 2 else 1 - s, (c - 2) % FF_STEPS)
                end = s0 + (PAIRS + 1) * FF_STEPS
                y(end - 1, 1, FF_STEPS - 2)
                y(end, 1, FF_STEPS - 1)
                for c in range(FF_STEPS):
                    pe.wait_ge(s_yT, FF_STEPS * f + c + 1)
                    for j in range(GTILES):
                        last = pe.transpose(bank(4 + c)[:, j * P:(j + 1) * P],
                                            yT[:, (c * GTILES + j) * P:(c * GTILES + j + 1) * P], ident)
                    last.then_inc(s_yP, 1)
                pe.wait_ge(s_yP, FF_STEPS * (f + 1))

            pe.sem_inc(s_yd, CR_YD)
            pe.sem_inc(s_oP, CR_OP)
            pe.sem_inc(s_mT, CR_MT)
            pe.sem_inc(s_pv, CR_PV)
            pe.wait_ge(s_in, 16 * 9)
            groups(pe, lambda i: prepare_qkv(0, i))
            pe.wait_ge(s_nrm, GROUPS)
            meet(pe, 1)
            samples_a()
            meet(pe, 2)
            groups(pe, lambda i: prepare_f(0, i))
            pe.wait_ge(s_cT, GROUPS)
            meet(pe, 3)
            experts(0)
            meet(pe, 4)
            groups(pe, lambda i: prepare_qkv(1, i))
            pe.wait_ge(s_rot, GROUPS)
            meet(pe, 5)
            samples_b()
            meet(pe, 6)
            groups(pe, lambda i: prepare_f(1, i))
            pe.wait_ge(s_cT, 2 * GROUPS)
            meet(pe, 7)
            experts(1)

        @block.scalar
        def _(act):
            st = Steps(act, s_act)

            def norm(stage, i, xT_, b, high=False):
                for g in range(2):
                    act.wait_ge(s_stat, lap(stage, i, g))
                    act.activation(std[g][:, :], mv[g][:, :, 1], ACT.Sqrt, bias=eps_s[:, 0:1]).then_inc(s_std, 1)
                for g in range(2):
                    act.wait_ge(s_xnT, lap(stage, i, g))
                    act.activation(xT_[g][:, :], bank(4 * g + b), ACT.Copy).then_inc(s_xT, 1)
                    if high:
                        act.activation(xh[:, group(i, g)], bank(4 * g + b), ACT.Copy).then_inc(s_xh, 1)

            def prepare_qkv(k, i):
                norm(2 * k, i, xT, 0)
                for g in range(2):
                    q, kk = bank(4 * g + 1), bank(4 * g + 2)
                    act.wait_ge(s_qkv, lap(k, i, g))
                    act.wait_ge(s_scr[g], i * (16 * STORES[k]) + (k * 2 * 16 * STORES[0] + CR_SCR))
                    if k == 0:
                        act.activation(sqq[g][:, :], q, ACT.Square)
                        act.activation(sqk[g][:, :], kk, ACT.Square)
                        act.activation(qh[g][:, :], q, ACT.Copy)
                        act.activation(kh[g][:, :], kk, ACT.Copy, scale=-2.0).then_inc(s_sq, 1)
                    else:
                        act.activation(sqq[g][:, :], q, ACT.Identity, bias=bqk_s[:, 0:1])
                        act.activation(sqk[g][:, :], kk, ACT.Identity, bias=bqk_s[:, 1:2]).then_inc(s_sq, 1)
                for g in range(2):
                    if k == 0:
                        b = 512 * 4 * g
                        act.wait_ge(s_nrm, lap(0, i, g))
                        act.activation(nh[g][0:H, :], ps[0:H, b:b + GT], ACT.Copy)
                        act.activation(arow[g][:, :], ps[0:H, b:b + GT], ACT.Copy, scale=-1.0, bias=1.0)
                        act.activation(nh[g][32:32 + H, :], ps[32:32 + H, b:b + GT], ACT.Copy).then_inc(s_nh, 1)
                    else:
                        act.wait_ge(s_qk2, lap(0, i, g))
                        act.activation(qh[g][:, :], q2[g][:, :], ACT.Copy)
                        act.activation(kh[g][:, :], k2[g][:, :], ACT.Copy).then_inc(s_qk2h, 1)

            def samples_a():
                def step(i, slot, last):
                    for half in range(2):
                        for c in (2 * half, 2 * half + 1):
                            act.wait_ge(s_fr, after(i, slot, UNITS, 2 * c + 2))
                            act.activation(Nt[:, c, :], Nt[:, c, :], ACT.Sqrt)
                            act.activation(St[:, c, :], St[:, c, :], ACT.Sqrt).then_inc(s_rt, 1)
                        act.preload_act_table_set("natural_log_exp_and_others")
                        for c, sums in ((2 * half, s_yp), (2 * half + 1, s_y)):
                            act.wait_ge(sums, after(i, slot, 2, half + 1))
                            st.do(act.activation(Nt[:, c, :], Nt[:, c, :], ACT.Ln))
                            st.sync()
                            act.activation(Nt[:, c, :], Nt[:, c, :], ACT.Exp, scale=-2.0).then_inc(s_e, 1)
                with act.Fori(0, B // 2 - 1) as i:
                    st.enter(i, 2 * CHUNKS)
                    step(i, 0, False)
                    step(i, 1, False)
                st.leave(B // 2 - 1)
                step(B // 2 - 1, 0, False)
                step(B // 2 - 1, 1, True)
                act.wait_ge(s_e, CHUNKS * B)

            def samples_b():
                def rows(i, slot, half):
                    act.wait_ge(s_mT, after_b(i, slot, 2, half + 1, CR_MT))
                    act.wait_ge(s_mxl[half], after_b(i, slot, 4 * 16, 0, CR_OS))
                    act.activation(mxT[half][:, :], ps[0:4 * HALF, 512 * 7 + N:512 * 8], ACT.Copy).then_inc(s_mr, 1)

                rows(0, 0, 0)

                def step(i, slot, last):
                    for u in range(UNITS):
                        b0 = 2 * (u % 2)
                        act.wait_ge(s_s2, after_b(i, slot, UNITS, u + 1))
                        act.wait_ge(s_pv, after_b(i, slot, CHUNKS, u // 2 + 1 - CHUNKS, CHUNKS * B + CR_PV))
                        act.activation(Wt[:, u // 2, (u % 2) * UC:(u % 2 + 1) * UC],
                                       ps[:, 512 * b0:512 * b0 + UC], ACT.Exp, scale=SCALE_B).then_inc(s_e, 1)
                        if u == 1:
                            rows(i, slot, 1)
                        if u == HALF + 1 and not last:
                            rows(i + (slot + 1) // SLOTS_B, (slot + 1) % SLOTS_B, 0)
                    act.wait_ge(s_pv, after_b(i, slot, CHUNKS, CHUNKS, CHUNKS * B + CR_PV))
                    act.wait_ge(s_osb[slot], i * 16 + CR_OS)
                    act.activation(osb_b[slot][:, :], ps[:, 512 * 6:512 * 8], ACT.Copy).then_inc(s_ev, 1)
                samples_of_b(act, step)
                act.wait_ge(s_e, E_A + UNITS * B)
                act.wait_ge(s_ev, 2 * B + CR_EV)

            def prepare_f(f, i):
                for g in range(2):
                    act.wait_ge(s_oT, lap(f, i, g))
                    act.activation(oT[g][:, :], bank(4 * g), ACT.Copy).then_inc(s_oTs, 1)
                norm(2 * f + 1, i, f_xT, 2, high=True)
                for g in range(2):
                    act.wait_ge(s_lg, lap(f, i, g))
                    act.activation(sc[g][:, :, :].rearrange("p t e -> p (t e)"), bank(4 * g + 3)[:, 0:GTILES * E],
                                   ACT.Sigmoid).then_inc(s_sc, 1)
                for g in range(2):
                    act.wait_ge(s_cT, lap(f, i, g))
                    act.activation(chi[g][E:2 * E, :], bank(4 * g)[E:2 * E, :], ACT.Copy)
                    act.activation(cs[0:E, group(i, g)], bank(4 * g)[0:E, :], ACT.Copy).then_inc(s_ch, 1)

            def experts(f):
                s0 = (PAIRS + 1) * FF_STEPS * f

                def silu(n, c, sg_used):
                    act.wait_ge(s_g, n + 1)
                    if sg_used is not None:
                        act.wait_ge(s_h1, sg_used)
                    act.activation(sg[c % 2][:, :], bank(4), ACT.Silu).then_inc(s_sg, 1)

                def high(n, c):
                    act.wait_ge(s_h, n)
                    act.wait_ge(s_yd, n - FF_STEPS + CR_YD)
                    act.activation(hh[c][:, :], hf[c % 2][:, :], ACT.Copy).then_inc(s_hh, 1)

                for c in range(FF_STEPS):
                    silu(s0 + c, c, s0 + c - 1 if s0 + c >= 2 else None)
                    if c >= 1:
                        high(s0 + c, c - 1)
                with act.Fori(0, PAIRS // 2) as i:
                    for s in range(2):
                        for c in range(FF_STEPS):
                            n = i * (2 * FF_STEPS) + (s0 + (s + 1) * FF_STEPS + c)
                            silu(n, c, n - 1)
                            high(n, (c - 1) % FF_STEPS)
                end = s0 + (PAIRS + 1) * FF_STEPS
                high(end, FF_STEPS - 1)
                for c in range(FF_STEPS):
                    act.wait_ge(s_yd, end - (FF_STEPS - 1 - c) + CR_YD)
                    act.activation(yT[:, c * FF_TOK:(c + 1) * FF_TOK], bank(c), ACT.Copy).then_inc(s_yT, 1)
                act.wait_ge(s_yT, FF_STEPS * (f + 1))

            act.wait_ge(s_in, 16 * 9)
            act.wait_ge(s_eps, 1)
            groups(act, lambda i: prepare_qkv(0, i))
            act.wait_ge(s_nh, GROUPS)
            meet(act, 1)
            samples_a()
            meet(act, 2)
            groups(act, lambda i: prepare_f(0, i))
            act.wait_ge(s_ch, GROUPS)
            meet(act, 3)
            experts(0)
            meet(act, 4)
            groups(act, lambda i: prepare_qkv(1, i))
            act.wait_ge(s_qk2h, GROUPS)
            meet(act, 5)
            samples_b()
            meet(act, 6)
            groups(act, lambda i: prepare_f(1, i))
            act.wait_ge(s_ch, 2 * GROUPS)
            meet(act, 7)
            experts(1)

        @block.gpsimd
        def _(pool):
            def samples_a():
                def step(i, slot, last):
                    for half in range(2):
                        c = 2 * half
                        pool.wait_ge(s_rt, after(i, slot, CHUNKS, c + 1))
                        pool.tensor_tensor(Nt[:, c, :], Nt[:, c, :], St[:, c, :], ALU.add).then_inc(s_yp, 1)
                        for c in (2 * half, 2 * half + 1):
                            pool.wait_ge(s_e, after(i, slot, CHUNKS, c + 1))
                            pool.tensor_tensor(St[:, c, :], Dt[:, c, :], Nt[:, c, :], ALU.mult).then_inc(s_w, 1)
                samples(pool, step)
                pool.wait_ge(s_w, CHUNKS * B + CR_W)

            def split(slot, n, loaded):
                pool.wait_ge(s_wl[slot], loaded)
                pool.sem_inc(s_mark, 1)
                pool.tensor_copy(whi[slot][:, :], wraw[slot][:, :]).then_inc(s_pool, 1)
                pool.wait_ge(s_pool, n)
                pool.tensor_tensor(wlo[slot][:, :], wraw[slot][:, 0:3 * P], whi[slot][:, 0:3 * P],
                                   ALU.subtract).then_inc(s_ws, 1)

            def experts(f):
                w0 = (PAIRS + 1) * f
                s0 = (PAIRS + 1) * FF_STEPS * f
                loads = ((PAIRS // 2) * f, (PAIRS // 2 + 1) * f + 1)
                split(1, w0 + 1, 16 * loads[1])
                with pool.Fori(0, PAIRS // 2) as i:
                    for s in range(2):
                        pool.wait_ge(s_yd, i * (2 * FF_STEPS) + (s0 + s * FF_STEPS + CR_YD))
                        split(s, i * 2 + (w0 + 2 + s), i * 16 + 16 * (loads[s] + 1))
                pool.wait_ge(s_ws, w0 + PAIRS + 1 + CR_WS)

            def cosines(i):
                for g in range(2):
                    pool.wait_ge(s_sq, lap(1, i, g))
                    pool.tensor_tensor(q2[g][:, :], sqq[g][:, :], cst[:, C_COS:C_COS + GT], ALU.mult)
                    pool.tensor_tensor(k2[g][:, :], sqk[g][:, :], cst[:, C_COS:C_COS + GT], ALU.mult
                                       ).then_inc(s_cos, 1)

            pool.sem_inc(s_ws, CR_WS)
            pool.sem_inc(s_w, CR_W)
            meet(pool, 1)
            samples_a()
            meet(pool, 2)
            meet(pool, 3)
            experts(0)
            meet(pool, 4)
            groups(pool, cosines)
            pool.wait_ge(s_cos, GROUPS)
            meet(pool, 5)
            meet(pool, 6)
            meet(pool, 7)
            experts(1)

        @block.vector
        def _(dve):
            st = Steps(dve, s_dve)

            def tile(i, g, j):
                return X[:, bass.ds(i * (2 * GTILES) + (g * GTILES + j), 1), :].rearrange("p a d -> p (a d)")

            def norm(stage, i, xn_):
                dve.sem_inc(s_mark, 1)
                for g in range(2):
                    for j in range(GTILES):
                        st.do(dve.bn_stats(stats[g][:, j, :], tile(i, g, j)))
                st.sync_apart(s_mark)
                for g in range(2):
                    for j in range(GTILES):
                        last = dve.bn_aggr(mv[g][:, j, :], stats[g][:, j, :])
                    last.then_inc(s_stat, 1)
                for g in range(2):
                    dve.wait_ge(s_std, lap(stage, i, g))
                    st.do(dve.reciprocal(rstd[g][:, :], std[g][:, :]))
                    st.sync()
                    for j in range(GTILES):
                        last = dve.tensor_scalar(xn_[g][:, j, :], tile(i, g, j), mv[g][:, j, 0:1],
                                                 rstd[g][:, j:j + 1], ALU.subtract, ALU.mult)
                    last.then_inc(s_xn, 1)

            def init_v():
                for g in range(2):
                    st.do(dve.memset(vb[g][:, :, :], 0.0))
                st.sync()
                for g in range(2):
                    heads = vb[g][:, :, 0:H * VW].rearrange("p t (h c) -> p t h c", c=VW)
                    st.do(dve.memset(heads[:, :, :, HD:HD + 1], 1.0))
                st.sync()

            def init_rows():
                st.do(dve.memset(ones[:, :], 1.0))
                st.do(dve.memset(zeros[:, :], 0.0))
                st.sync()
                dve.sem_inc(s_init, 1)

            def v_columns(k, i):
                for g in range(2):
                    dve.wait_ge(s_qkv, lap(k, i, g))
                    dve.wait_ge(s_scr[g], i * (16 * STORES[k]) + (k * 2 * 16 * STORES[0] + CR_SCR))
                    for j in range(GTILES):
                        o = vb[g][:, j, 0:H * VW].rearrange("p (h c) -> p h c", c=VW)[:, :, 0:HD]
                        v = bank(4 * g + 3)[:, j * P:(j + 1) * P].rearrange("p (h c) -> p h c", c=HD)
                        if k == 0:
                            last = dve.tensor_copy(o, v)
                        else:
                            last = dve.tensor_tensor(o, v, bv_s[:, :].rearrange("p (h c) -> p h c", c=HD), ALU.add)
                    last.then_inc(s_vc, 1)

            def prepare_a(i):
                norm(0, i, xn)
                v_columns(0, i)
                for g in range(2):
                    dve.wait_ge(s_sq, lap(0, i, g))
                    st.do(dve.tensor_tensor(ql[g][:, :], bank(4 * g + 1), qh[g][:, :], ALU.subtract))
                    st.do(dve.scalar_tensor_tensor(kl[g][:, :], bank(4 * g + 2), -2.0, kh[g][:, :],
                                                   ALU.mult, ALU.subtract))
                for g in range(2):
                    dve.wait_ge(s_nh, lap(0, i, g))
                    for row in (0, 32):
                        st.do(dve.tensor_tensor(nl[g][row:row + H, :], ps[row:row + H, 2048 * g:2048 * g + GT],
                                                nh[g][row:row + H, :], ALU.subtract))
                    st.do(dve.tensor_scalar(vb[g][:, :, H * VW:VB],
                                            bank(4 * g + 3)[:, 0:GTILES * H].rearrange("p (t h) -> p t h", h=H),
                                            -1.0, 1.0, ALU.mult, ALU.add))
                    st.sync()
                    dve.sem_inc(s_spl, 1)

            def prepare_b(i):
                norm(2, i, xn)
                v_columns(1, i)
                for g in range(2):
                    dve.wait_ge(s_rot, lap(0, i, g))
                    for r, b in ((0, 4 * g), (1, 4 * g + 3)):
                        st.do(dve.tensor_tensor(rt[g][:, r, :], bank(b), cst[:, C_SIN:C_SIN + GT], ALU.mult))
                    st.sync()
                    dve.wait_ge(s_cos, lap(0, i, g))
                    for r, o in ((0, q2), (1, k2)):
                        st.do(dve.tensor_tensor(o[g][:, :], o[g][:, :], rt[g][:, r, :], ALU.add))
                    st.sync()
                    dve.sem_inc(s_qk2, 1)
                for g in range(2):
                    dve.wait_ge(s_qk2h, lap(0, i, g))
                    for lo, o, hi in ((ql, q2, qh), (kl, k2, kh)):
                        st.do(dve.tensor_tensor(lo[g][:, :], o[g][:, :], hi[g][:, :], ALU.subtract))
                    st.sync()
                    dve.sem_inc(s_spl, 1)

            def samples_a():
                def front(i, n, c):
                    slot = n % 2
                    dve.wait_ge(s_w, after(i, n, CHUNKS, c + 1 - CHUNKS, CR_W))
                    if c == 0:
                        dve.wait_ge(s_ld[slot], (i + n // 2) * (16 * LOADS[0]) + 16 * LOADS[0])
                    for u in (2 * c, 2 * c + 1):
                        for g in range(2):
                            for mt in range(MT):
                                col = ((u % 2) * 2 * MT + g * MT + mt) * N
                                h = 2 * u + g
                                st.do(dve.tensor_scalar(Dt[:, c, col:col + N], abc[slot][:, h, :],
                                                        vbs[slot][:, mt, H * VW + h:H * VW + h + 1], 1e-6,
                                                        ALU.mult, ALU.max))
                    st.sync()
                    dve.wait_ge(s_pv, after(i, n, CHUNKS, c + 1 - CHUNKS, CR_PV))
                    for u in (2 * c, 2 * c + 1):
                        dve.wait_ge(s_s, after(i, n, UNITS, u + 1))
                        b0 = 512 * 2 * (u % 2)
                        at = slice((u % 2) * UC, (u % 2 + 1) * UC)
                        dve.tensor_scalar(Nt[:, c, at], ps[:, b0:b0 + UC], 0.0, None, ALU.max)
                        dve.scalar_tensor_tensor(St[:, c, at], ps[:, b0:b0 + UC], 0.0, Dt[:, c, at],
                                                 ALU.max, ALU.add).then_inc(s_fr, 1)

                def root_sum(i, n, half):
                    c = 2 * half + 1
                    dve.wait_ge(s_rt, after(i, n, CHUNKS, c + 1))
                    dve.tensor_tensor(Nt[:, c, :], Nt[:, c, :], St[:, c, :], ALU.add).then_inc(s_y, 1)

                def copy_out(i, n):
                    slot = n % 2
                    dve.wait_ge(s_pv, after(i, n, CHUNKS, CHUNKS, CR_PV))
                    dve.wait_ge(s_os[slot], (i + n // 2) * 16 + CR_OS)
                    b0 = 512 * (4 + 2 * slot)
                    dve.tensor_copy(osb[slot][:, :], ps[:, b0:b0 + 2 * 512]).then_inc(s_ev, 1)

                def step(i, n, first=False, last=False):
                    front(i, n, 2)
                    root_sum(i, n, 0)
                    front(i, n, 3)
                    if not first:
                        copy_out(i, n - 1)
                    if not last:
                        front(i, n + 1, 0)
                    root_sum(i, n, 1)
                    if not last:
                        front(i, n + 1, 1)

                front(0, 0, 0)
                front(0, 0, 1)
                step(0, 0, first=True)
                with dve.Fori(0, B // 2 - 1) as i:
                    st.enter(i, 2 * UNITS * 2 * MT)
                    step(i, 1)
                    step(i, 2)
                st.leave(B // 2 - 1)
                step(B // 2 - 1, 1, last=True)
                copy_out(B // 2 - 1, 1)
                dve.wait_ge(s_ev, B + CR_EV)

            def samples_b():
                def head_max(i, slot, u, g):
                    dve.wait_ge(s_s1, after_b(i, slot, H, 2 * u + g + 1))
                    dve.tensor_reduce(mx[:, u // HALF, :, g * HALF + u % HALF],
                                      bank(4 + g).rearrange("p (t m) -> p t m", t=MT), AX_X, ALU.max
                                      ).then_inc(s_mx, 1)

                def split_max(i, slot, half):
                    dve.wait_ge(s_mx, after_b(i, slot, H, 2 * HALF * (half + 1), CR_MX))
                    st.do(dve.tensor_copy(mxh_r[:, half, :, :], mx[:, half, :, :]))
                    st.sync()
                    whole = mx[:, half, :, :].rearrange("p t (g u) -> p t g u", g=2)
                    high = mxh_r[:, half, :, :].bitcast(F32).rearrange("p t (g u) -> p t g u", g=2)
                    dve.tensor_scalar(mxs[:, half, :, :, 0, :], high, -1.0, None, ALU.mult)
                    dve.tensor_tensor(mxs[:, half, :, :, 1, :], high, whole, ALU.subtract).then_inc(s_ms, 1)

                def maxima(i, slot):
                    for u in range(UNITS):
                        if u % HALF == 0:
                            dve.wait_ge(s_mT, after_b(i, slot, 2, u // HALF - 1, CR_MT))
                        for g in range(2):
                            head_max(i, slot, u, g)
                        if u % HALF == HALF - 1:
                            split_max(i, slot, u // HALF)

                def step(i, slot, last):
                    if not last:
                        maxima(i + (slot + 1) // SLOTS_B, (slot + 1) % SLOTS_B)

                maxima(0, 0)
                samples_of_b(dve, step, lambda i: st.enter(i, SLOTS_B * 2), lambda: st.leave(B // SLOTS_B))
                dve.wait_ge(s_ms, 2 * B)

            def attention_tail(f, i):
                for g in range(2):
                    dve.wait_ge(s_oP, lap(f, i, g) + CR_OP)
                    b = 2048 * g
                    if f == 0:
                        raw = ps[:, b:b + 2048].rearrange("p (t h c) -> p t h c", h=H, c=VW)
                    else:
                        raw = ps[:, b:b + 2048].rearrange("p (l g c) -> p g l c", g=GTILES, c=VW)
                    st.do(dve.reciprocal(rden[g][:, :, :], raw[:, :, :, HD]))
                    st.sync()
                    dve.tensor_tensor(otok[g][:, :, :].rearrange("p t (h c) -> p t h c", c=HD), raw[:, :, :, 0:HD],
                                      rden[g][:, :, :].unsqueeze(3).broadcast_to([P, GTILES, H, HD]),
                                      ALU.mult).then_inc(s_on, 1)
                for g in range(2):
                    dve.wait_ge(s_wo, lap(f, i, g))
                    xg = X[:, group(i, g, GTILES), :]
                    st.do(dve.tensor_tensor(xg, xg, bank(4 * g + 1).rearrange("p (t d) -> p t d", d=P), ALU.add))
                    st.sync()
                    if f == 1:
                        st.do(dve.tensor_tensor(xg, xg, pb_s[:, :].unsqueeze(1).broadcast_to([P, GTILES, P]),
                                                ALU.add))
                        st.sync()

            def route(f, i):
                def both(step, apart=False):
                    for g in range(2):
                        step(g)
                    if apart:
                        st.sync_apart(s_mark)
                    else:
                        st.sync()

                def biased(g):
                    dve.wait_ge(s_sc, lap(f, i, g))
                    st.do(dve.tensor_tensor(sfc[g][:, :, :], sc[g][:, :, :],
                                            eb_s[:, :].unsqueeze(1).broadcast_to([P, GTILES, E]), ALU.add))

                def best_of_group(g):
                    for j in range(GTILES):
                        for k in range(8):
                            last = dve.max(m8[g][:, j, k, :], sfc[g][:, j, 8 * k:8 * k + 8])
                    st.do(last)

                def group_scores(g):
                    st.do(dve.tensor_tensor(gs[g][:, :, 0:8], m8[g][:, :, :, 0], m8[g][:, :, :, 1], ALU.add))

                def best_groups(g):
                    for j in range(GTILES):
                        last = dve.max(g8[g][:, j, :], gs[g][:, j, :])
                    st.do(last)

                def mark_groups(g):
                    for j in range(GTILES):
                        last = dve.match_replace(gr[g][:, j, :], g8[g][:, j, :], gs[g][:, j, :], -BIG)
                    st.do(last)

                def group_mask(g):
                    st.do(dve.tensor_scalar(gm[g][:, :, :], gr[g][:, :, 0:8], -BIG, None, ALU.is_equal))

                def masked(g):
                    st.do(dve.tensor_tensor(mk[g][:, :, :].rearrange("p t (g e) -> p (t g) e", e=8),
                                            sfc[g][:, :, :].rearrange("p t (g e) -> p (t g) e", e=8),
                                            gm[g][:, :, :].rearrange("p t g -> p (t g)").unsqueeze(2)
                                            .broadcast_to([P, GTILES * 8, 8]), ALU.mult))

                def no_minus_zero(g):
                    st.do(dve.tensor_scalar(mk[g][:, :, :], mk[g][:, :, :], 0.0, None, ALU.add))

                def best_experts(g):
                    for j in range(GTILES):
                        last = dve.max(k8[g][:, j, :], mk[g][:, j, :])
                    st.do(last)

                def mark_experts(g):
                    for j in range(GTILES):
                        last = dve.match_replace(mr[g][:, j, :], k8[g][:, j, :], mk[g][:, j, :], -BIG)
                    st.do(last)

                def chosen(g):
                    st.do(dve.scalar_tensor_tensor(wsel[g][:, :, :], mr[g][:, :, :], -BIG, sc[g][:, :, :],
                                                   ALU.is_equal, ALU.mult))

                def total(g):
                    st.do(dve.tensor_reduce(wsum[g][:, :], wsel[g][:, :, :], AX_X, ALU.add))

                def guarded(g):
                    st.do(dve.tensor_scalar(wsum[g][:, :], wsum[g][:, :], 1e-20, None, ALU.add))

                def inverse(g):
                    st.do(dve.reciprocal(wrec[g][:, :], wsum[g][:, :]))

                both(biased, True)
                both(best_of_group)
                both(group_scores, True)
                both(best_groups, True)
                both(mark_groups)
                both(group_mask)
                both(masked)
                both(no_minus_zero, True)
                both(best_experts, True)
                both(mark_experts)
                both(chosen)
                both(total)
                both(guarded)
                both(inverse)
                for g in range(2):
                    for j in range(GTILES):
                        last = dve.tensor_scalar(coef[g][:, j, :].rearrange("p (r e) -> p r e", r=2),
                                                 wsel[g][:, j, :].unsqueeze(1).broadcast_to([P, 2, E]),
                                                 wrec[g][:, j:j + 1], ROUTE_SCALE, ALU.mult, ALU.mult)
                    last.then_inc(s_cf, 1)

            def marks():
                for g in range(2):
                    st.do(dve.memset(gs[g][:, :, 8:12], BIG))

            def prepare_f(f, i):
                attention_tail(f, i)
                norm(2 * f + 1, i, f_xn)
                for g in range(2):
                    dve.wait_ge(s_xh, lap(f, i, g))
                    st.do(dve.tensor_tensor(xl[:, group(i, g)], f_xT[g][:, :], xh[:, group(i, g)], ALU.subtract))
                route(f, i)
                for g in range(2):
                    dve.wait_ge(s_ch, lap(f, i, g))
                    st.do(dve.tensor_tensor(cs[E:2 * E, group(i, g)], bank(4 * g)[E:2 * E, :], chi[g][E:2 * E, :],
                                            ALU.subtract))
                    st.sync()
                    dve.sem_inc(s_grp, 1)

            def experts(f):
                s0 = (PAIRS + 1) * FF_STEPS * f
                c0 = PAIRS * FF_STEPS * f - FF_STEPS * (f + 1) - PAIRS * FF_STEPS * f

                def gate_up(n, c, shared):
                    dve.wait_ge(s_sg, n + 1)
                    dve.wait_ge(s_u, n + 1)
                    dve.wait_ge(s_hl, n - 1 + CR_HL)
                    if shared:
                        dve.tensor_tensor(hf[c % 2][:, :], sg[c % 2][:, :], bank(5), ALU.mult).then_inc(s_h1, 1)
                        dve.wait_ge(s_h1, n + 1)
                        dve.sem_inc(s_h, 1)
                        return
                    dve.tensor_tensor(h1[c % 2][:, :], sg[c % 2][:, :], bank(5), ALU.mult).then_inc(s_h1, 1)
                    dve.wait_ge(s_h1, n + 1)
                    dve.wait_ge(s_c, n + (1 - FF_STEPS * (f + 1)))
                    dve.tensor_tensor(hf[c % 2][:, :], h1[c % 2][:, :], bank(6), ALU.mult).then_inc(s_h, 1)

                def low(n, c):
                    dve.wait_ge(s_hh, n)
                    dve.wait_ge(s_yd, n - FF_STEPS + CR_YD)
                    dve.tensor_tensor(hl[c][:, :], hf[c % 2][:, :], hh[c][:, :], ALU.subtract).then_inc(s_hl, 1)

                st.do(dve.memset(zr[:, :].bitcast(F32), 0.0))
                st.sync()
                dve.sem_inc(s_z, 1)
                for c in range(FF_STEPS):
                    gate_up(s0 + c, c, True)
                    if c >= 1:
                        low(s0 + c, c - 1)
                with dve.Fori(0, PAIRS // 2) as i:
                    for s in range(2):
                        for c in range(FF_STEPS):
                            n = i * (2 * FF_STEPS) + (s0 + (s + 1) * FF_STEPS + c)
                            gate_up(n, c, False)
                            low(n, (c - 1) % FF_STEPS)
                end = s0 + (PAIRS + 1) * FF_STEPS
                low(end, FF_STEPS - 1)
                for c in range(FF_STEPS):
                    dve.wait_ge(s_yP, FF_STEPS * f + c + 1)
                    xg = X[:, c * GTILES:(c + 1) * GTILES, :]
                    dve.tensor_tensor(xg, xg, bank(4 + c).rearrange("p (t d) -> p t d", d=P),
                                      ALU.add).then_inc(s_res, 1)
                dve.wait_ge(s_res, FF_STEPS * (f + 1))

            def phase(steps, body):
                def counted(i):
                    st.enter(i, steps)
                    body(i)
                groups(dve, counted)
                st.leave(GROUPS // 2)

            dve.sem_inc(s_ev, CR_EV)
            dve.sem_inc(s_hl, CR_HL)
            dve.sem_inc(s_grp, CR_GRP)
            dve.sem_inc(s_spl, CR_SPL)
            dve.sem_inc(s_mx, CR_MX)
            st.do(dve.memset(eps_s[:, :], 1e-5))
            st.sync()
            dve.sem_inc(s_eps, 1)
            init_rows()
            dve.wait_ge(s_in, 16 * 9)
            init_v()
            phase(DVE_A, prepare_a)
            meet(dve, 1)
            samples_a()
            meet(dve, 2)
            marks()
            phase(DVE_F, lambda i: prepare_f(0, i))
            meet(dve, 3)
            experts(0)
            meet(dve, 4)
            init_rows()
            init_v()
            phase(DVE_B, prepare_b)
            meet(dve, 5)
            samples_b()
            meet(dve, 6)
            marks()
            phase(DVE_F + 2, lambda i: prepare_f(1, i))
            meet(dve, 7)
            experts(1)


_OUTS = [((8, 256, 128), "float32")]


def _feature_order():
    import numpy as np
    g, d, u = (a.ravel() for a in np.meshgrid(np.arange(2), np.arange(HD), np.arange(UNITS), indexing="ij"))
    head = 2 * u + g
    return head * HD + d, head, d


def _constants():
    import numpy as np
    c = np.zeros((P, C_END), np.float32)
    c[:, C_ID:C_ID + P] = np.eye(P, dtype=np.float32)
    _, head, d = _feature_order()
    c[np.arange(P), C_HS + head] = 1.0
    half = HD // 2
    for f in range(P):
        if d[f] < half:
            c[f + half * UNITS, C_ROT + f] = -1.0
        else:
            c[f - half * UNITS, C_ROT + f] = 1.0
    freq = (1.0 / 10000.0 ** (np.arange(0, HD, 2, dtype=np.float32) / HD)).astype(np.float32)
    pos = (np.arange(GT) % N).astype(np.float32)
    ang = (freq[d % half][:, None] * pos[None, :]).astype(np.float32)
    c[:, C_COS:C_COS + GT] = np.cos(ang)
    c[:, C_SIN:C_SIN + GT] = np.sin(ang)
    return c


def _layout(w):
    import numpy as np
    w = {k.replace("L0_", ""): np.ascontiguousarray(v) for k, v in w.items()}
    consts = _constants()
    order = _feature_order()[0]
    wA = np.concatenate([w["attn_a_Wq"][order].T, w["attn_a_Wk"][order].T, w["attn_a_Wv"].T, w["attn_a_Wo"].T], axis=1)
    qkv_w = w["attn_b_qkv_w"].reshape(3, P, P)
    wB = np.concatenate([qkv_w[0][order].T, qkv_w[1][order].T, qkv_w[2].T, w["attn_b_proj_w"].T], axis=1)
    bqk = w["attn_b_qkv_b"][:2 * P].reshape(2, P)[:, order].T
    brow = np.concatenate([w["attn_b_qkv_b"][2 * P:], w["attn_b_proj_b"], w["ffn_e_bias"]])[None]
    wexp = np.zeros((PAIRS + 1, P, 4 * P), np.float32)
    for k, n in enumerate(("ffn_Wg", "ffn_Wu")):
        wexp[:PAIRS, :, k * P:(k + 1) * P] = w[n].reshape(PAIRS, 2, P, I).transpose(0, 2, 1, 3).reshape(PAIRS, P, P)
    wexp[:PAIRS, :, 2 * P:3 * P] = w["ffn_Wd"].reshape(PAIRS, P, P)
    for k, n in enumerate(("ffn_SWg", "ffn_SWu", "ffn_SWd")):
        wexp[PAIRS, :, k * P:(k + 1) * P] = w[n]
    for p in range(PAIRS):
        for e in range(2):
            for half in range(2):
                wexp[p, half * E + 2 * p + e, 3 * P + e * I:3 * P + (e + 1) * I] = 1.0
    return {"x": w["attn_a_x"], "consts": consts, "wA": wA, "wB": wB, "bqk": bqk,
            "brow": brow, "rwT": w["ffn_router_w"].T, "wexp": wexp}


def kernel(**inputs):
    import numpy as _np
    import concourse.bacc as _bacc
    from concourse import mybir as _mybir
    from concourse.bass_utils import run_bass_kernel_spmd as _run

    nc = _bacc.Bacc("TRN2", target_bir_lowering=False, num_devices=1)
    arrays, args = {}, []
    for name, a in _layout(inputs).items():
        a = _np.ascontiguousarray(a)
        arrays[f"in_{name}_dram"] = a
        args.append(nc.dram_tensor(f"in_{name}_dram", a.shape, _mybir.dt.from_np(a.dtype), kind="ExternalInput").ap())
    for i, (shape, dtype) in enumerate(_OUTS):
        dt = _mybir.dt.from_np(_np.dtype(dtype))
        args.append(nc.dram_tensor(f"out_{i}_dram", shape, dt, kind="ExternalOutput").ap())
    hybrid(nc, *args)
    r = _run(nc, [arrays], core_ids=[0])
    return r.results[0]["out_0_dram"]
```

```python
from contextlib import ExitStack

import concourse.bass as bass
from concourse import mybir

F32 = mybir.dt.float32
F32R = mybir.dt.float32r
ALU = mybir.AluOpType
ACT = mybir.ActivationFunctionType
AX_X = mybir.AxisListType.X

P = 128
B, N = 8, 256
T = B * N
TILES = T // P
H, HD = 16, 8
E, I = 64, 64
PAIRS = E // 2
GROUPS = 4
GT = T // GROUPS
GTILES = GT // P
LT = 2 * GTILES
UNITS = H // 2
CHUNKS = H // 4
MT = N // P
UC = 2 * MT * N
VW = 32
VB = H * VW + H
KQ = 4 * HD
KS = KQ + 4
SLOTS_B = 3
HALF = UNITS // 2
BIG = float(2 ** 100)
FF_TOK = 512
FF_STEPS = T // FF_TOK
SCALE_B = HD ** -0.5
OR = 4 * (HD + 1)
OW0, OW1 = 256, 64
KD = 2 * HD + 4
STORES = (10, 5)
LOADS = (12, 11)
CR_OP, CR_SPL, CR_GRP, CR_SCR = 2, 2, 2, 16
CR_EV, CR_OS, CR_W, CR_PV, CR_MX, CR_MT = 2, 16, 4, 4, 2, 2
CR_WS, CR_HL, CR_H, CR_YD = 1, 2, 1, FF_STEPS
E_A = CHUNKS * B
ROUTE_SCALE = 2.5

C_ID, C_HS, C_ROT, C_COS, C_SIN, C_END = 0, 128, 144, 272, 784, 1296


class Steps:

    def __init__(self, eng, sem):
        self.eng, self.sem, self.n, self.off = eng, sem, 0, 0

    def do(self, ins):
        ins.then_inc(self.sem, 1)
        self.n += 1

    def sync(self):
        self.eng.wait_ge(self.sem, self.off + self.n)

    def sync_apart(self, mark):
        self.sync()
        self.eng.sem_inc(mark, 1)

    def enter(self, i, per):
        self.start, self.per, self.off = self.n, per, i * per

    def leave(self, trips):
        assert self.n - self.start == self.per, (self.n - self.start, self.per)
        self.n, self.off = self.start + trips * self.per, 0


def hybrid(nc, x, consts, wA, wB, bqk, brow, rwT, wexp, out):
    ctx = ExitStack()

    def sem(name):
        return ctx.enter_context(nc.semaphore(name))

    def dram(name, shape, dt):
        return nc.dram_tensor(name, shape, dt, kind="Internal").ap()

    q_d = dram("q_stack", [2, KD, UNITS, T], F32)
    k_d = dram("k_stack", [2, KD, UNITS, T], F32)
    a_d = dram("one_minus_q_norm", [H, T], F32)
    vb_d = dram("v_and_b", [T, VB], F32)
    c_d = dram("routing_coefficients", [E, T], F32)
    o_d = dram("attn_unnormalised", [B, OR, 4 * N], F32)

    with ctx:
        def keep(name, shape, dt=F32):
            return ctx.enter_context(nc.sbuf_tensor(name, shape, dt))

        X = keep("X", [P, TILES, P])
        cst = keep("cst", [P, C_END])
        wa = keep("wa", [P, 4 * P])
        wb = keep("wb", [P, 4 * P])
        bqk_s = keep("bqk_s", [P, 2])
        bv_s = keep("bv_s", [P, P])
        pb_s = keep("pb_s", [P, P])
        eb_s = keep("eb_s", [P, E])
        rw_s = keep("rw_s", [P, E])
        eps_s = keep("eps_s", [P, 1])
        stats = [keep(f"stats{g}", [P, GTILES, 6]) for g in range(2)]
        mv = [keep(f"mv{g}", [P, GTILES, 2]) for g in range(2)]
        std = [keep(f"std{g}", [P, GTILES]) for g in range(2)]
        rstd = [keep(f"rstd{g}", [P, GTILES]) for g in range(2)]
        ident = cst[:, C_ID:C_ID + P]
        HS = cst[:, C_HS:C_HS + H]
        ROT = cst[:, C_ROT:C_ROT + P]

        ps = ctx.enter_context(nc.psum_tensor("ps", [P, 8 * 512], F32))

        def bank(n, k=1):
            return ps[:, 512 * n:512 * (n + k)]

        with ExitStack() as att:
            def sb(name, shape, dt=F32):
                return att.enter_context(nc.sbuf_tensor(name, shape, dt))
            qst = [sb(f"qst{s}", [P, UNITS, N], F32R) for s in range(2)]
            kst = [sb(f"kst{s}", [P, UNITS, N], F32R) for s in range(2)]
            vbs = [sb(f"vbs{s}", [P, MT, VB]) for s in range(2)]
            osb = [sb(f"osb{s}", [P, 4 * N]) for s in range(2)]
            abc = [sb(f"abc{s}", [P, H, N]) for s in range(2)]
            with ExitStack() as pre:
                def pre_sb(name, shape, dt=F32):
                    return pre.enter_context(nc.sbuf_tensor(name, shape, dt))
                def two(name, shape, dt=F32):
                    return [pre_sb(f"{name}{g}", shape, dt) for g in range(2)]
                xn = two("xn", [P, GTILES, P])
                xT = two("xT", [P, GT])
                sqq = two("sqq", [P, GT])
                sqk = two("sqk", [P, GT])
                q2 = two("q2", [P, GT])
                k2 = two("k2", [P, GT])
                rt = two("rt", [P, 2, GT])
                ones = pre_sb("ones", [P, 2 * UNITS * T // P])
                zeros = pre_sb("zeros", [P, 2 * UNITS * T // P])
                used = 2 * (6 * GT + 2 * GT) + 2 * (2 * UNITS * T // P)
                pre_sb("to_second_half", [P, CHUNKS // 2 * 3 * 2 * UC - used])
                qh = two("qh", [P, GT], F32R)
                ql = two("ql", [P, GT], F32R)
                kh = two("kh", [P, GT], F32R)
                kl = two("kl", [P, GT], F32R)
                nh = two("nh", [P, GT], F32R)
                nl = two("nl", [P, GT], F32R)
                arow = two("arow", [H, GT])
                vb = two("vb", [P, GTILES, VB])
            with ExitStack() as a_only:
                work = a_only.enter_context(nc.sbuf_tensor("work", [P, CHUNKS, 3, 2 * UC], F32))
                Nt, St, Dt = (work[:, :, k, :] for k in range(3))
            with ExitStack() as b_only:
                def b_sb(name, shape, dt=F32):
                    return b_only.enter_context(nc.sbuf_tensor(name, shape, dt))
                Wt = b_sb("Wt", [P, CHUNKS, 2 * UC])
                osb_b = osb + [b_sb("osb2", [P, 4 * N])]
                mx = b_sb("mx", [P, 2, MT, 2 * HALF])
                mxh_r = b_sb("mxh_r", [P, 2, MT, 2 * HALF], F32R)
                mxs = b_sb("mxs", [P, 2, MT, 2, 2, HALF])
                mxT = [b_sb(f"mxT{f}", [4 * HALF, N], F32R) for f in range(2)]
                used = CHUNKS * 2 * UC + 4 * N + 2 * MT * 2 * HALF * 4 + 2 * N
                b_sb("to_second_half_b", [P, CHUNKS // 2 * 3 * 2 * UC - used])
                qst_b = qst + [b_sb("qst2", [P, UNITS, N], F32R)]
                kst_b = kst + [b_sb("kst2", [P, UNITS, N], F32R)]
                vbs_b = vbs + [b_sb("vbs2", [P, MT, VB])]
        with ExitStack() as ffn:
            def sb(name, shape, dt=F32):
                return ffn.enter_context(nc.sbuf_tensor(name, shape, dt))
            xh = sb("xh", [P, T], F32R)
            xl = sb("xl", [P, T], F32R)
            wraw = [sb(f"wraw{s}", [P, 3 * P]) for s in range(2)]
            whi = [sb(f"whi{s}", [P, 3 * P], F32R) for s in range(2)]
            wlo = [sb(f"wlo{s}", [P, 3 * P], F32R) for s in range(2)]
            zr = sb("zr", [P, FF_TOK], F32R)
            one_s = sb("one_s", [P, FF_TOK])
            with ExitStack() as rtr:
                def sr(name, shape, dt=F32):
                    return rtr.enter_context(nc.sbuf_tensor(name, shape, dt))
                def two(name, shape, dt=F32):
                    return [sr(f"{name}{g}", shape, dt) for g in range(2)]
                f_xn = two("f_xn", [P, GTILES, P])
                f_xT = two("f_xT", [P, GT])
                ou = two("ou", [OR, 2, 4 * N])
                rden = two("rden", [P, GTILES, H])
                otok = two("otok", [P, GTILES, P])
                oT = two("oT", [P, GT])
                sc = sr("sc", [P, LT, E])
                sfc = sr("sfc", [P, LT, E])
                top = [sr(f"top{k}", [P, LT * 8, w]) for k, w in enumerate((4, 2, 1))]
                second = [sr(f"second{k}", [P, LT * 8, w]) for k, w in enumerate((4, 2, 1))]
                lesser = [sr(f"lesser{k}", [P, LT * 8, w]) for k, w in enumerate((2, 1))]
                gs = sr("gs", [P, LT, 12])
                g8 = sr("g8", [P, LT, 8])
                gr = sr("gr", [P, LT, 12])
                gm = sr("gm", [P, LT, 8])
                mk = sr("mk", [P, LT, E])
                k8 = sr("k8", [P, LT, 8])
                mr = sr("mr", [P, LT, E])
                wsel = sr("wsel", [P, LT, E])
                wsum = sr("wsum", [P, LT])
                wrec = sr("wrec", [P, LT])
                coef = sr("coef", [P, LT, E])
                cT = two("cT", [E, GT])
            cbc = [sb(f"cbc{s}", [P, T]) for s in range(2)]
            sg = [sb(f"sg{s}", [P, FF_TOK]) for s in range(2)]
            h1 = [sb(f"h1{s}", [P, FF_TOK]) for s in range(2)]
            hf = [sb(f"hf{s}", [P, FF_TOK]) for s in range(2)]
            hh = [sb(f"hh{s}", [P, FF_TOK], F32R) for s in range(4)]
            hl = [sb(f"hl{s}", [P, FF_TOK], F32R) for s in range(4)]
            yT = sb("yT", [P, T])

        s_x = sem("first_tokens_loaded")
        s_in = sem("inputs_loaded")
        s_out = sem("output_stored")
        s_phase = sem("phase_done")
        s_mark = sem("wait_carrier")
        s_eps = sem("eps_ready")
        s_stat = sem("stats_ready")
        s_std = sem("std_ready")
        s_xn = sem("xn_ready")
        s_xnT = sem("xnT_in_psum")
        s_xT = sem("xT_ready")
        s_qkv = sem("qkv_in_psum")
        s_sq = sem("squares_ready")
        s_nrm = sem("norms_in_psum")
        s_rot = sem("rotated_in_psum")
        s_vc = sem("v_copied")
        s_nh = sem("norm_highs_ready")
        s_cos = sem("cosine_parts_ready")
        s_qk2 = sem("rotated_ready")
        s_qk2h = sem("rotated_highs_ready")
        s_xh = sem("x_high_ready")
        s_ch = sem("coefT_ready")
        s_spl = sem("splits_ready")
        s_scr = [sem(f"scratch_stored{g}") for g in range(2)]
        s_ou = [sem(f"unnormalised_loaded{g}") for g in range(2)]
        s_oP = sem("o_token_major_in_psum")
        s_on = sem("o_normalised")
        s_oT = sem("oT_in_psum")
        s_oTs = sem("oT_ready")
        s_wo = sem("projection_in_psum")
        s_lg = sem("logits_in_psum")
        s_sc = sem("scores_ready")
        s_cf = sem("coef_ready")
        s_cT = sem("coefT_in_psum")
        s_cst = [sem(f"coef_stored{g}") for g in range(2)]
        s_init = sem("ones_ready")
        s_one = sem("ones_stored")
        s_vz = sem("padded_v_zeroed")
        s_iv = sem("padded_v_ready")
        s_ldb = [sem(f"b_sample_loaded{s}") for s in range(SLOTS_B)]
        s_osb = [sem(f"b_o_stored{s}") for s in range(SLOTS_B)]
        s_mxl = [sem(f"b_max_rows_loaded{f}") for f in range(2)]
        s_ld = [sem(f"sample_loaded{s}") for s in range(2)]
        s_s = sem("diff_in_psum")
        s_fr = sem("diff_read")
        s_rt = sem("roots_ready")
        s_yp = sem("root_sum_of_even_chunk_ready")
        s_y = sem("root_sum_of_odd_chunk_ready")
        s_e = sem("inverse_square_ready")
        s_w = sem("weights_ready")
        s_pv = sem("pv_in_psum")
        s_ev = sem("pv_copied")
        s_os = [sem(f"o_stored{s}") for s in range(2)]
        s_s1 = sem("b_scores_in_psum")
        s_mx = sem("b_head_max_read")
        s_ms = sem("b_max_split_ready")
        s_mT = sem("b_maxT_in_psum")
        s_mr = sem("b_maxT_ready")
        s_s2 = sem("b_shifted_in_psum")
        s_wl = [sem(f"expert_weights_loaded{s}") for s in range(2)]
        s_ws = sem("expert_weights_split")
        s_z = sem("zero_ready")
        s_g = sem("gate_in_psum")
        s_u = sem("up_in_psum")
        s_cl = [sem(f"expert_coefs_loaded{s}") for s in range(2)]
        s_sg = sem("silu_ready")
        s_h1 = sem("gate_up_ready")
        s_h = sem("h_ready")
        s_hh = sem("h_hi_ready")
        s_hl = sem("h_lo_ready")
        s_yd = sem("down_done")
        s_yT = sem("yT_ready")
        s_yP = sem("y_token_major_in_psum")
        s_res = sem("residual_added")
        s_dve = sem("dve_steps")
        s_act = sem("act_steps")
        s_pool = sem("pool_steps")

        block = ctx.enter_context(nc.Block())

        def meet(eng, n):
            eng.sem_inc(s_phase, 1)
            eng.wait_ge(s_phase, 5 * n)

        def lap(stage, i, g):
            return i * 2 + (GROUPS * stage + g + 1)

        def group(i, g, width=GT):
            return bass.ds(i * (2 * width) + g * width, width)

        def groups(eng, body):
            with eng.Fori(0, GROUPS // 2) as i:
                body(i)

        def samples(eng, step):
            with eng.Fori(0, B // 2 - 1) as i:
                step(i, 0, False)
                step(i, 1, False)
            step(B // 2 - 1, 0, False)
            step(B // 2 - 1, 1, True)

        def after(i, slot, per, k, base=0):
            return i * (2 * per) + (slot * per + k + base)

        def samples_of_b(eng, step, enter=lambda i: None, leave=lambda: None):
            with eng.Fori(0, B // SLOTS_B) as i:
                enter(i)
                for slot in range(SLOTS_B):
                    step(i, slot, False)
            leave()
            for slot in range(B % SLOTS_B):
                step(B // SLOTS_B, slot, slot == B % SLOTS_B - 1)

        def after_b(i, slot, per, k, base=0):
            return i * (SLOTS_B * per) + (slot * per + k + base)

        @block.sync
        def _(sp):
            x_tiles = x.rearrange("b (m p) d -> p (b m) d", p=P)
            sp.dma_start(X[:, 0:LT, :], x_tiles[:, 0:LT, :]).then_inc(s_x, 16)
            sp.dma_start(cst[:, :], consts).then_inc(s_in, 16)
            sp.dma_start(wa[:, :], wA).then_inc(s_in, 16)
            sp.dma_start(X[:, LT:2 * LT, :], x_tiles[:, LT:2 * LT, :]).then_inc(s_in, 16)
            sp.dma_start(wb[:, :], wB).then_inc(s_in, 16)
            sp.dma_start(bqk_s[:, :], bqk).then_inc(s_in, 16)
            sp.dma_start(bv_s[:, :], brow[0:1, 0:P].broadcast_to([P, P])).then_inc(s_in, 16)
            sp.dma_start(pb_s[:, :], brow[0:1, P:2 * P].broadcast_to([P, P])).then_inc(s_in, 16)
            sp.dma_start(eb_s[:, :], brow[0:1, 2 * P:2 * P + E].broadcast_to([P, E])).then_inc(s_in, 16)
            sp.dma_start(rw_s[:, :], rwT).then_inc(s_in, 16)
            sp.wait_ge(s_in, 16 * 9)

            def store_splits(stage, i):
                for g in range(2):
                    at = group(i, g)
                    sp.wait_ge(s_spl, lap(stage, i, g) + CR_SPL)
                    def rows(d, r):
                        return d[:, HD * r:HD * (r + 1), :, at].rearrange("g j t n -> g (j t) n")

                    todo = [(rows(d, r), t[g]) for d, halves in ((q_d, (qh, ql)), (k_d, (kh, kl)))
                            for r, t in enumerate(halves)]
                    todo = [(to, of[:, :].bitcast(F32)) for to, of in todo]
                    todo += [(vb_d[at, :].rearrange("(t p) c -> p t c", p=P), vb[g][:, :, :])]
                    if stage == 0:
                        todo += [(d[:, 2 * HD + off + r, :, at].rearrange("g t n -> t g n"),
                                  t[g][row:row + H, :].bitcast(F32))
                                 for d, off, row in ((q_d, 0, 0), (k_d, 2, 32)) for r, t in enumerate((nh, nl))]
                        todo += [(a_d[:, at], arow[g][:, :])]
                    assert len(todo) == STORES[stage]
                    for to, of in todo:
                        sp.dma_start(to, of).then_inc(s_scr[g], 16)

            def load(at, q, k, v, loaded):
                parts = ((q, q_d, ((0, 0, HD), (HD, 0, 2 * HD), (3 * HD, HD, KD - HD))),
                         (k, k_d, ((0, 0, 2 * HD), (2 * HD, 0, KD))))
                for g in range(2):
                    for to, of, pieces in parts:
                        for row, src, rows in pieces:
                            sp.dma_start(to[64 * g + row:64 * g + row + rows, :, :].bitcast(F32),
                                         of[g, src:src + rows, :, at]).then_inc(loaded, 16)
                sp.dma_start(v[:, :, :], vb_d[at, :].rearrange("(m p) c -> p m c", p=P)).then_inc(loaded, 16)

            def load_a(i, slot):
                at = bass.ds(i * (2 * N) + slot * N, N)
                sp.dma_start(abc[slot][:, :, :], a_d[:, at].partition_broadcast(P)).then_inc(s_ld[slot], 16)
                load(at, qst[slot], kst[slot], vbs[slot], s_ld[slot])

            def load_b(i, slot):
                load(bass.ds(i * (SLOTS_B * N) + slot * N, N), qst_b[slot], kst_b[slot], vbs_b[slot], s_ldb[slot])

            def store_o(osb_, b, stored):
                for g in range(4):
                    sp.dma_start(o_d[b, g * (HD + 1):(g + 1) * (HD + 1), :].rearrange("a p n -> p (a n)"),
                                 osb_[VW * g:VW * g + HD + 1, :]).then_inc(stored, 16)

            def samples_a():
                def step(i, slot, last):
                    if not (isinstance(i, int)):
                        sp.wait_ge(s_pv, after(i, slot, CHUNKS, CHUNKS, CR_PV))
                        load_a(i + 1, slot)
                    sp.wait_ge(s_ev, after(i, slot, 1, 1, CR_EV))
                    store_o(osb[slot], bass.ds(i * 2 + slot, 1), s_os[slot])
                samples(sp, step)
                for s in range(2):
                    sp.wait_ge(s_os[s], 4 * 16 * (B // 2) + CR_OS)

            def samples_b():
                def max_rows(i, slot, half):
                    sp.wait_ge(s_mr, after_b(i, slot, 2, half + 1))
                    for g in range(2):
                        for part in range(2):
                            row = (2 * g + part) * HALF
                            to = 64 * g + KQ + part
                            sp.dma_start(qst_b[slot][to:to + 1, half * HALF:(half + 1) * HALF, :].bitcast(F32),
                                         mxT[half][row:row + HALF, :].bitcast(F32)).then_inc(s_mxl[half], 16)

                max_rows(0, 0, 0)
                for g in range(2):
                    sp.wait_ge(s_scr[g], 16 * 2 * (STORES[0] + STORES[1]) + CR_SCR)
                max_rows(0, 0, 1)

                def step(i, slot, last):
                    if not isinstance(i, int):
                        sp.wait_ge(s_pv, after_b(i, slot, CHUNKS, 0, CHUNKS * B + CR_PV))
                        load_b(i + (slot + 2) // SLOTS_B, (slot + 2) % SLOTS_B)
                    if not last:
                        for half in range(2):
                            max_rows(i + (slot + 1) // SLOTS_B, (slot + 1) % SLOTS_B, half)
                    sp.wait_ge(s_ev, after_b(i, slot, 1, 1, B + CR_EV))
                    store_o(osb_b[slot], bass.ds(i * SLOTS_B + slot, 1), s_osb[slot])
                samples_of_b(sp, step)
                for s in range(SLOTS_B):
                    sp.wait_ge(s_osb[s], 4 * 16 * ((B - s - 1) // SLOTS_B + 1) + CR_OS)

            def experts_phase(f):
                base = (PAIRS + 1) * f
                s0 = (PAIRS + 1) * FF_STEPS * f
                with sp.Fori(0, PAIRS // 2) as i:
                    for s in range(2):
                        sp.wait_ge(s_ws, i * 2 + (base + s + CR_WS))
                        sp.dma_start(wraw[s][:, :], wexp[bass.ds(i * 2 + s, 1), :, :].rearrange("a p n -> p (a n)")
                                     ).then_inc(s_wl[s], 16)
                        sp.wait_ge(s_h, i * (2 * FF_STEPS) + (s0 + s * FF_STEPS + CR_H))
                        for e in range(2):
                            row = c_d[bass.ds(i * 4 + (2 * s + e), 1), :]
                            sp.dma_start(cbc[s][e * I:(e + 1) * I, :],
                                         row.rearrange("a n -> (a n)").partition_broadcast(I)).then_inc(s_cl[s], 16)

            def store_coefs(f):
                with sp.Fori(0, GROUPS // 2) as i:
                    for g in range(2):
                        sp.wait_ge(s_ch, lap(f, i, g) + CR_GRP)
                        sp.dma_start(c_d[:, group(i, g)], cT[g][:, :]).then_inc(s_cst[g], 16)
                for g in range(2):
                    sp.wait_ge(s_cst[g], 2 * 16 * (f + 1) + CR_SCR)

            def prepare_f(f):
                sp.dma_start(wraw[1][:, :], wexp[PAIRS]).then_inc(s_wl[1], 16)
                with sp.Fori(0, GROUPS // 2) as i:
                    for g in range(2):
                        sp.wait_ge(s_oP, i * 2 + (GROUPS * f + g - 1 + CR_OP))
                        if f == 0:
                            to = ou[g][:, :, :]
                            of = o_d[bass.ds(i * 4 + g * 2, 2), :, :].rearrange("a p n -> p a n")
                        else:
                            to = ou[g][:, :, :].rearrange("p a n -> p (a n)").rearrange("p (b n) -> p b n", n=N)
                            of = o_d[:, :, group(i, g, N)].rearrange("b p n -> p b n")
                        sp.dma_start(to, of).then_inc(s_ou[g], 16)

            for s in range(2):
                sp.sem_inc(s_scr[s], CR_SCR)
                sp.sem_inc(s_cst[s], CR_SCR)
                sp.sem_inc(s_os[s], CR_OS)
            for s in range(SLOTS_B):
                sp.sem_inc(s_osb[s], CR_OS)
            for half in range(2):
                sp.sem_inc(s_mxl[half], CR_OS)
            def constant_rows(todo):
                for g in range(2):
                    for d, row, of in todo:
                        to = d[g, row:row + 2, :, :].rearrange("r t n -> (r t n)").rearrange("(p c) -> p c", p=P)
                        sp.dma_start(to, of[:, :]).then_inc(s_one, 16)

            sp.wait_ge(s_init, 1)
            constant_rows(((q_d, KD - 2, ones), (k_d, KD - 4, ones)))
            sp.wait_ge(s_one, 4 * 16)
            store_splits(0, 0)
            sp.wait_ge(s_scr[0], 16 * STORES[0] + CR_SCR)
            load_a(0, 0)
            sp.sem_inc(s_phase, 1)
            store_splits(0, 1)
            sp.wait_ge(s_phase, 5 * 1)
            load_a(0, 1)
            for g in range(2):
                sp.wait_ge(s_scr[g], 2 * 16 * STORES[0] + CR_SCR)
            samples_a()
            meet(sp, 2)
            prepare_f(0)
            sp.sem_inc(s_phase, 1)
            store_coefs(0)
            sp.wait_ge(s_phase, 5 * 3)
            experts_phase(0)
            meet(sp, 4)
            sp.wait_ge(s_init, 2)
            constant_rows(((q_d, KD - 4, zeros), (q_d, KD - 2, zeros), (k_d, KD - 2, ones)))
            sp.wait_ge(s_one, (4 + 6) * 16)
            store_splits(1, 0)
            sp.wait_ge(s_scr[0], 16 * (2 * STORES[0] + STORES[1]) + CR_SCR)
            load_b(0, 0)
            load_b(0, 1)
            sp.sem_inc(s_phase, 1)
            store_splits(1, 1)
            sp.wait_ge(s_phase, 5 * 5)
            samples_b()
            meet(sp, 6)
            prepare_f(1)
            sp.sem_inc(s_phase, 1)
            store_coefs(1)
            sp.wait_ge(s_phase, 5 * 7)
            experts_phase(1)
            out_tiles = out.rearrange("b (m p) d -> p (b m) d", p=P)
            for c in range(FF_STEPS):
                sp.wait_ge(s_res, FF_STEPS + c + 1)
                tiles = slice(c * GTILES, (c + 1) * GTILES)
                sp.dma_start(out_tiles[:, tiles, :], X[:, tiles, :]).then_inc(s_out, 16)
            sp.wait_ge(s_out, 16 * FF_STEPS)

        @block.tensor
        def _(pe):
            def mm(o, l, r, start=True, stop=True, **kw):
                return pe.matmul(o, l, r, start=start, stop=stop, **kw)

            def norm_transposed(stage, i, xn_, b):
                for g in range(2):
                    pe.wait_ge(s_xn, lap(stage, i, g))
                    for j in range(GTILES):
                        last = pe.transpose(bank(4 * g + b)[:, j * P:(j + 1) * P], xn_[g][:, j, :], ident)
                    last.then_inc(s_xnT, 1)

            def prepare_qkv(k, i):
                w = (wa, wb)[k]
                pe.wait_ge(s_spl, i * 2 + (GROUPS * k + CR_SPL))
                norm_transposed(2 * k, i, xn, 0)
                for g in range(2):
                    pe.wait_ge(s_xT, lap(2 * k, i, g))
                    mm(bank(4 * g + 1), w[:, 0:P], xT[g][:, :])
                    mm(bank(4 * g + 2), w[:, P:2 * P], xT[g][:, :])
                    for j in range(GTILES):
                        last = mm(bank(4 * g + 3)[:, j * P:(j + 1) * P], xT[g][:, j * P:(j + 1) * P],
                                  w[:, 2 * P:3 * P])
                    last.then_inc(s_qkv, 1)
                for g in range(2):
                    b = 512 * 4 * g
                    pe.wait_ge(s_sq, lap(k, i, g))
                    pe.wait_ge(s_vc, lap(k, i, g))
                    if k == 0:
                        mm(ps[0:H, b:b + GT], HS, sqq[g][:, :])
                        mm(ps[32:32 + H, b:b + GT], HS, sqk[g][:, :])
                        for j in range(GTILES):
                            last = mm(bank(4 * g + 3)[:, j * H:(j + 1) * H], sqk[g][:, j * P:(j + 1) * P], HS)
                        last.then_inc(s_nrm, 1)
                    else:
                        mm(bank(4 * g), ROT, sqq[g][:, :])
                        mm(bank(4 * g + 3), ROT, sqk[g][:, :]).then_inc(s_rot, 1)

            def pv(i, slot, c, wt, phase, min_rows=None):
                vs = (vbs, vbs_b)[phase][slot]
                if phase == 0:
                    b0 = 4 + 2 * slot
                    pe.wait_ge(s_w, after(i, slot, CHUNKS, c + 1, CR_W))
                    pe.wait_ge(s_ev, after(i, slot, 1, CR_EV - 1))
                else:
                    b0 = 6
                    pe.wait_ge(s_e, after_b(i, slot, UNITS, 2 * c + 2, E_A))
                    pe.wait_ge(s_ev, after_b(i, slot, 1, 0, B + CR_EV))
                    if c == 2:
                        pe.wait_ge(s_mr, min_rows)
                for mt in range(MT):
                    for g in range(4):
                        h = 4 * c + g
                        col = (g * MT + mt) * N
                        last = mm(ps[32 * g:32 * g + VW, 512 * b0 + c * N:512 * b0 + (c + 1) * N],
                                  vs[:, mt, h * VW:(h + 1) * VW], wt[:, c, col:col + N],
                                  start=(mt == 0), stop=(mt == MT - 1), tile_position=(0, 32 * g))
                last.then_inc(s_pv, 1)

            def a_scores(i, slot, u):
                b0 = 2 * (u % 2)
                for g in range(2):
                    for mt in range(MT):
                        col = 512 * b0 + (g * MT + mt) * N
                        last = mm(ps[:, col:col + N], kst[slot][64 * g:64 * g + KS, u, mt * P:(mt + 1) * P],
                                  qst[slot][64 * g:64 * g + KS, u, :])
                last.then_inc(s_s, 1)

            def samples_a():
                pe.wait_ge(s_ld[0], 16 * LOADS[0])
                for u in range(UNITS):
                    if u >= 2:
                        pe.wait_ge(s_fr, u - 1)
                    a_scores(0, 0, u)

                def step(i, slot, last):
                    ni, ns = (i, 1) if slot == 0 else (i + 1, 0)
                    if not last:
                        pe.wait_ge(s_ld[ns], ni * (16 * LOADS[0]) + 16 * LOADS[0])
                    for c in range(CHUNKS):
                        pv(i, slot, c, St, 0)
                        if not last:
                            for u in (2 * c, 2 * c + 1):
                                pe.wait_ge(s_fr, after(i, slot, UNITS, UNITS + u - 1))
                                a_scores(ni, ns, u)
                samples(pe, step)
                pe.wait_ge(s_pv, CHUNKS * B + CR_PV)

            def b_scores(i, slot, u):
                for g in range(2):
                    pe.wait_ge(s_mx, after_b(i, slot, H, 2 * u + g - 1, CR_MX))
                    for nt in range(MT):
                        col = 512 * (4 + g) + nt * N
                        last = mm(ps[:, col:col + N], qst_b[slot][64 * g:64 * g + KS, u, nt * P:(nt + 1) * P],
                                  kst_b[slot][64 * g:64 * g + KS, u, :])
                    last.then_inc(s_s1, 1)

            def b_max_rows(i, slot, half):
                pe.wait_ge(s_ms, after_b(i, slot, 2, half + 1))
                for nt in range(MT):
                    col = 512 * 7 + N + nt * P
                    tr = pe.transpose(ps[0:4 * HALF, col:col + P],
                                      mxs[:, half, nt, :, :, :].rearrange("p g r u -> p (g r u)"), ident)
                tr.then_inc(s_mT, 1)

            def b_shifted(i, slot, u):
                b0 = 2 * (u % 2)
                for g in range(2):
                    for mt in range(MT):
                        col = 512 * b0 + (g * MT + mt) * N
                        last = mm(ps[:, col:col + N], kst_b[slot][64 * g:64 * g + KS, u, mt * P:(mt + 1) * P],
                                  qst_b[slot][64 * g:64 * g + KS, u, :])
                last.then_inc(s_s2, 1)

            def samples_b():
                pe.wait_ge(s_ldb[0], 16 * LOADS[1])
                for u in range(UNITS):
                    b_scores(0, 0, u)
                    if u == HALF:
                        b_max_rows(0, 0, 0)

                def step(i, slot, last):
                    ni, ns = i + (slot + 1) // SLOTS_B, (slot + 1) % SLOTS_B
                    for u in range(UNITS):
                        if u % HALF == 0:
                            pe.wait_ge(s_mxl[u // HALF], after_b(i, slot, 4 * 16, 4 * 16, CR_OS))
                        pe.wait_ge(s_e, after_b(i, slot, UNITS, u - 1, E_A))
                        b_shifted(i, slot, u)
                        if u == 1:
                            pe.wait_ge(s_ev, after_b(i, slot, 1, 0, B + CR_EV))
                            b_max_rows(i, slot, 1)
                        if not last:
                            if u == 0:
                                pe.wait_ge(s_ldb[ns], ni * (16 * LOADS[1]) + 16 * LOADS[1])
                            b_scores(ni, ns, u)
                            if u == HALF + 1:
                                pe.wait_ge(s_mr, after_b(i, slot, 2, 2))
                                b_max_rows(ni, ns, 0)
                        if u % 2 == 1 and u >= 3:
                            pv(i, slot, u // 2 - 1, Wt, 1, after_b(i, slot, 2, 2 if last else 3))
                    pv(i, slot, CHUNKS - 1, Wt, 1)
                samples_of_b(pe, step)
                pe.wait_ge(s_pv, 2 * CHUNKS * B + CR_PV)

            def token_major(f, i):
                for g in range(2):
                    pe.wait_ge(s_ou[g], 16 * (GROUPS // 2 * f + i + 1))
                    b = 512 * 4 * g
                    if f == 0:
                        for b2 in range(2):
                            for nt in range(MT):
                                for hg in range(CHUNKS):
                                    col = b + OW0 * (2 * b2 + nt) + hg * OR
                                    last = pe.transpose(ps[:, col:col + OR],
                                                        ou[g][:, b2, hg * N + nt * P:hg * N + (nt + 1) * P],
                                                        ident[0:OR, 0:OR])
                    else:
                        by16 = ou[g][:, :, :].rearrange("p a n -> p (a n)").rearrange("p (r l) -> p l r", l=P // HD)
                        for low in range(P // HD):
                            col = b + OW1 * low
                            last = pe.transpose(ps[:, col:col + OR], by16[:, low, :], ident[0:OR, 0:OR])
                    last.then_inc(s_oP, 1)

            def projection(f, i):
                for g in range(2):
                    pe.wait_ge(s_on, lap(f, i, g))
                    for j in range(GTILES):
                        last = pe.transpose(bank(4 * g)[:, j * P:(j + 1) * P], otok[g][:, j, :], ident)
                    last.then_inc(s_oT, 1)
                for g in range(2):
                    pe.wait_ge(s_oTs, lap(f, i, g))
                    for j in range(GTILES):
                        last = mm(bank(4 * g + 1)[:, j * P:(j + 1) * P], oT[g][:, j * P:(j + 1) * P],
                                  (wa, wb)[f][:, 3 * P:4 * P])
                    last.then_inc(s_wo, 1)

            def logits(f, i):
                norm_transposed(2 * f + 1, i, f_xn, 2)
                for g in range(2):
                    pe.wait_ge(s_xT, lap(2 * f + 1, i, g))
                    pe.wait_ge(s_ch, lap(f, i, g) - 2 + CR_GRP)
                    for j in range(GTILES):
                        last = mm(bank(4 * g + 3)[:, j * E:(j + 1) * E], f_xT[g][:, j * P:(j + 1) * P], rw_s[:, :])
                    last.then_inc(s_lg, 1)

            def coefs_transposed(f, i):
                for g in range(2):
                    pe.wait_ge(s_cf, 2 * f + i + 1)
                    for j in range(GTILES):
                        last = pe.transpose(bank(4 * g + 3)[0:E, j * P:(j + 1) * P],
                                            coef[:, g * GTILES + j, :], ident)
                    last.then_inc(s_cT, 1)

            def prepare_f(f):
                token_major(f, 0)
                projection(f, 0)
                pe.wait_ge(s_stat, lap(2 * f + 1, 0, 1))
                token_major(f, 1)
                logits(f, 0)
                projection(f, 1)
                coefs_transposed(f, 0)
                logits(f, 1)
                coefs_transposed(f, 1)
                pe.wait_ge(s_z, f + 1)
                for c in range(FF_STEPS):
                    if c == 3:
                        pe.wait_ge(s_ch, lap(f, 1, 0) + CR_GRP)
                    mm(bank(c), zr[:, 0:P], zr[:, :], start=True, stop=False, skip_group_check=True)

            def experts(f):
                s0 = (PAIRS + 1) * FF_STEPS * f
                w0 = (PAIRS + 1) * f

                def y(n, slot, chunk):
                    pe.wait_ge(s_hl, n + CR_HL)
                    hi, lo = hh[chunk], hl[chunk]
                    for k, (l, r) in enumerate(((whi[slot], hi), (whi[slot], lo), (wlo[slot], hi))):
                        last = mm(bank(chunk), l[:, 2 * P:3 * P], r[:, :], start=False, stop=False,
                                  skip_group_check=True)
                    last.then_inc(s_yd, 1)

                def gate_up(n, slot, chunk, first):
                    cols = slice(chunk * FF_TOK, (chunk + 1) * FF_TOK)
                    hi, lo = whi[slot], wlo[slot]
                    for b, read, done in ((0, s_sg, s_g), (1, s_h1, s_u)):
                        if not first:
                            pe.wait_ge(read, n - 1)
                        for k, (l, r) in enumerate(((hi, xh), (hi, xl), (lo, xh))):
                            last = mm(bank(4 + 2 * (chunk % 2) + b), l[:, b * P:(b + 1) * P], r[:, cols],
                                      start=(k == 0), stop=(k == 2))
                        last.then_inc(done, 1)

                pe.wait_ge(s_ws, w0 + 1 + CR_WS)
                for c in range(FF_STEPS):
                    gate_up(s0 + c, 1, c, c < 2)
                    if c >= 2:
                        y(s0 + c - 1, 1, c - 2)
                with pe.Fori(0, PAIRS // 2) as i:
                    for s in range(2):
                        pe.wait_ge(s_ws, i * 2 + (w0 + 2 + s + CR_WS))
                        for c in range(FF_STEPS):
                            n = i * (2 * FF_STEPS) + (s0 + (s + 1) * FF_STEPS + c)
                            gate_up(n, s, c, False)
                            y(n - 1, s if c >= 2 else 1 - s, (c - 2) % FF_STEPS)
                end = s0 + (PAIRS + 1) * FF_STEPS
                y(end - 1, 1, FF_STEPS - 2)
                y(end, 1, FF_STEPS - 1)
                for c in range(FF_STEPS):
                    pe.wait_ge(s_yT, FF_STEPS * f + c + 1)
                    for j in range(GTILES):
                        last = pe.transpose(bank(4 + c)[:, j * P:(j + 1) * P],
                                            yT[:, (c * GTILES + j) * P:(c * GTILES + j + 1) * P], ident)
                    last.then_inc(s_yP, 1)
                pe.wait_ge(s_yP, FF_STEPS * (f + 1))

            pe.sem_inc(s_yd, CR_YD)
            pe.sem_inc(s_oP, CR_OP)
            pe.sem_inc(s_mT, CR_MT)
            pe.sem_inc(s_pv, CR_PV)
            pe.wait_ge(s_in, 16 * 9)
            groups(pe, lambda i: prepare_qkv(0, i))
            pe.wait_ge(s_nrm, GROUPS)
            meet(pe, 1)
            samples_a()
            meet(pe, 2)
            prepare_f(0)
            pe.wait_ge(s_cT, GROUPS)
            meet(pe, 3)
            experts(0)
            meet(pe, 4)
            groups(pe, lambda i: prepare_qkv(1, i))
            pe.wait_ge(s_rot, GROUPS)
            meet(pe, 5)
            samples_b()
            meet(pe, 6)
            prepare_f(1)
            pe.wait_ge(s_cT, 2 * GROUPS)
            meet(pe, 7)
            experts(1)

        @block.scalar
        def _(act):
            st = Steps(act, s_act)

            def norm_std(stage, i):
                for g in range(2):
                    act.wait_ge(s_stat, lap(stage, i, g))
                    act.activation(std[g][:, :], mv[g][:, :, 1], ACT.Sqrt, bias=eps_s[:, 0:1]).then_inc(s_std, 1)

            def norm_copy(stage, i, xT_, b, high=False):
                for g in range(2):
                    act.wait_ge(s_xnT, lap(stage, i, g))
                    act.activation(xT_[g][:, :], bank(4 * g + b), ACT.Copy).then_inc(s_xT, 1)
                    if high:
                        act.activation(xh[:, group(i, g)], bank(4 * g + b), ACT.Copy).then_inc(s_xh, 1)

            def q_and_k(k, i):
                for g in range(2):
                    q, kk = bank(4 * g + 1), bank(4 * g + 2)
                    act.wait_ge(s_qkv, lap(k, i, g))
                    act.wait_ge(s_scr[g], i * (16 * STORES[k]) + (k * 2 * 16 * STORES[0] + CR_SCR))
                    if k == 0:
                        act.activation(sqq[g][:, :], q, ACT.Square)
                        act.activation(sqk[g][:, :], kk, ACT.Square)
                        act.activation(qh[g][:, :], q, ACT.Copy)
                        act.activation(kh[g][:, :], kk, ACT.Copy, scale=-2.0).then_inc(s_sq, 1)
                    else:
                        act.activation(sqq[g][:, :], q, ACT.Identity, bias=bqk_s[:, 0:1])
                        act.activation(sqk[g][:, :], kk, ACT.Identity, bias=bqk_s[:, 1:2]).then_inc(s_sq, 1)

            def highs(k, i):
                for g in range(2):
                    if k == 0:
                        b = 512 * 4 * g
                        act.wait_ge(s_nrm, lap(0, i, g))
                        act.activation(nh[g][0:H, :], ps[0:H, b:b + GT], ACT.Copy)
                        act.activation(arow[g][:, :], ps[0:H, b:b + GT], ACT.Copy, scale=-1.0, bias=1.0)
                        act.activation(nh[g][32:32 + H, :], ps[32:32 + H, b:b + GT], ACT.Copy).then_inc(s_nh, 1)
                    else:
                        act.wait_ge(s_qk2, lap(0, i, g))
                        act.activation(qh[g][:, :], q2[g][:, :], ACT.Copy)
                        act.activation(kh[g][:, :], k2[g][:, :], ACT.Copy).then_inc(s_qk2h, 1)

            def prepare_qkv(k):
                norm_std(2 * k, 0)
                act.wait_ge(s_in, 16 * 9)
                norm_copy(2 * k, 0, xT, 0)
                q_and_k(k, 0)
                highs(k, 0)
                norm_std(2 * k, 1)
                norm_copy(2 * k, 1, xT, 0)
                q_and_k(k, 1)
                highs(k, 1)

            def samples_a():
                def step(i, slot, last):
                    for half in range(2):
                        for c in (2 * half, 2 * half + 1):
                            act.wait_ge(s_fr, after(i, slot, UNITS, 2 * c + 2))
                            act.activation(work[:, c, 0:2, :], work[:, c, 0:2, :], ACT.Sqrt).then_inc(s_rt, 1)
                        act.preload_act_table_set("natural_log_exp_and_others")
                        for c, sums in ((2 * half, s_yp), (2 * half + 1, s_y)):
                            act.wait_ge(sums, after(i, slot, 2, half + 1))
                            st.do(act.activation(Nt[:, c, :], Nt[:, c, :], ACT.Ln))
                            st.sync()
                            act.activation(Nt[:, c, :], Nt[:, c, :], ACT.Exp, scale=-2.0).then_inc(s_e, 1)
                with act.Fori(0, B // 2 - 1) as i:
                    st.enter(i, 2 * CHUNKS)
                    step(i, 0, False)
                    step(i, 1, False)
                st.leave(B // 2 - 1)
                step(B // 2 - 1, 0, False)
                step(B // 2 - 1, 1, True)
                act.wait_ge(s_e, CHUNKS * B)

            def samples_b():
                def rows(i, slot, half):
                    act.wait_ge(s_mT, after_b(i, slot, 2, half + 1, CR_MT))
                    act.wait_ge(s_mxl[half], after_b(i, slot, 4 * 16, 0, CR_OS))
                    act.activation(mxT[half][:, :], ps[0:4 * HALF, 512 * 7 + N:512 * 8], ACT.Copy).then_inc(s_mr, 1)

                rows(0, 0, 0)

                def step(i, slot, last):
                    for u in range(UNITS):
                        b0 = 2 * (u % 2)
                        act.wait_ge(s_s2, after_b(i, slot, UNITS, u + 1))
                        act.wait_ge(s_pv, after_b(i, slot, CHUNKS, u // 2 + 1 - CHUNKS, CHUNKS * B + CR_PV))
                        act.activation(Wt[:, u // 2, (u % 2) * UC:(u % 2 + 1) * UC],
                                       ps[:, 512 * b0:512 * b0 + UC], ACT.Exp, scale=SCALE_B).then_inc(s_e, 1)
                        if u == 1:
                            rows(i, slot, 1)
                        if u == HALF + 1 and not last:
                            rows(i + (slot + 1) // SLOTS_B, (slot + 1) % SLOTS_B, 0)
                    act.wait_ge(s_pv, after_b(i, slot, CHUNKS, CHUNKS, CHUNKS * B + CR_PV))
                    act.wait_ge(s_osb[slot], i * (4 * 16) + CR_OS)
                    act.activation(osb_b[slot][:, :], ps[:, 512 * 6:512 * 8], ACT.Copy).then_inc(s_ev, 1)
                samples_of_b(act, step)
                act.wait_ge(s_e, E_A + UNITS * B)
                act.wait_ge(s_ev, 2 * B + CR_EV)

            def o_copies(f, i):
                for g in range(2):
                    act.wait_ge(s_oT, lap(f, i, g))
                    act.activation(oT[g][:, :], bank(4 * g), ACT.Copy).then_inc(s_oTs, 1)

            def scores(f, i):
                for g in range(2):
                    act.wait_ge(s_lg, lap(f, i, g))
                    act.activation(sc[:, g * GTILES:(g + 1) * GTILES, :].rearrange("p t e -> p (t e)"),
                                   bank(4 * g + 3)[:, 0:GTILES * E], ACT.Sigmoid).then_inc(s_sc, 1)

            def coef_copies(f, i):
                for g in range(2):
                    act.wait_ge(s_cT, lap(f, i, g))
                    act.wait_ge(s_cst[g], 16 * (2 * f + i) + CR_SCR)
                    act.activation(cT[g][:, :], bank(4 * g + 3)[0:E, :], ACT.Copy).then_inc(s_ch, 1)

            def prepare_f(f):
                o_copies(f, 0)
                norm_std(2 * f + 1, 0)
                norm_copy(2 * f + 1, 0, f_xT, 2, high=True)
                scores(f, 0)
                o_copies(f, 1)
                norm_std(2 * f + 1, 1)
                coef_copies(f, 0)
                norm_copy(2 * f + 1, 1, f_xT, 2, high=True)
                scores(f, 1)
                coef_copies(f, 1)

            def experts(f):
                s0 = (PAIRS + 1) * FF_STEPS * f

                def silu(n, c, sg_used):
                    act.wait_ge(s_g, n + 1)
                    if sg_used is not None:
                        act.wait_ge(s_h1, sg_used)
                    act.activation(sg[c % 2][:, :], bank(4 + 2 * (c % 2)), ACT.Silu).then_inc(s_sg, 1)

                def high(n, c):
                    act.wait_ge(s_h, n + CR_H)
                    act.wait_ge(s_yd, n - FF_STEPS + CR_YD)
                    act.activation(hh[c][:, :], hf[c % 2][:, :], ACT.Copy).then_inc(s_hh, 1)

                for c in range(FF_STEPS):
                    silu(s0 + c, c, s0 + c - 1 if s0 + c >= 2 else None)
                    if c >= 1:
                        high(s0 + c, c - 1)
                with act.Fori(0, PAIRS // 2) as i:
                    for s in range(2):
                        for c in range(FF_STEPS):
                            n = i * (2 * FF_STEPS) + (s0 + (s + 1) * FF_STEPS + c)
                            silu(n, c, n - 1)
                            high(n, (c - 1) % FF_STEPS)
                end = s0 + (PAIRS + 1) * FF_STEPS
                high(end, FF_STEPS - 1)
                for c in range(FF_STEPS):
                    act.wait_ge(s_yd, end - (FF_STEPS - 1 - c) + CR_YD)
                    act.activation(yT[:, c * FF_TOK:(c + 1) * FF_TOK], bank(c), ACT.Copy).then_inc(s_yT, 1)
                act.wait_ge(s_yT, FF_STEPS * (f + 1))

            act.sem_inc(s_ch, CR_GRP)
            act.wait_ge(s_eps, 1)
            prepare_qkv(0)
            act.wait_ge(s_nh, GROUPS)
            meet(act, 1)
            samples_a()
            meet(act, 2)
            prepare_f(0)
            act.wait_ge(s_ch, GROUPS + CR_GRP)
            meet(act, 3)
            experts(0)
            meet(act, 4)
            prepare_qkv(1)
            act.wait_ge(s_qk2h, GROUPS)
            meet(act, 5)
            samples_b()
            meet(act, 6)
            prepare_f(1)
            act.wait_ge(s_ch, 2 * GROUPS + CR_GRP)
            meet(act, 7)
            experts(1)

        @block.gpsimd
        def _(pool):
            def samples_a():
                def step(i, slot, last):
                    for half in range(2):
                        c = 2 * half
                        pool.wait_ge(s_rt, after(i, slot, CHUNKS, c + 1))
                        pool.tensor_tensor(Nt[:, c, :], Nt[:, c, :], St[:, c, :], ALU.add).then_inc(s_yp, 1)
                        for c in (2 * half, 2 * half + 1):
                            pool.wait_ge(s_e, after(i, slot, CHUNKS, c + 1))
                            pool.tensor_tensor(St[:, c, :], Dt[:, c, :], Nt[:, c, :], ALU.mult).then_inc(s_w, 1)
                samples(pool, step)
                pool.wait_ge(s_w, CHUNKS * B + CR_W)

            def split(slot, n, loaded):
                pool.wait_ge(s_wl[slot], loaded)
                pool.sem_inc(s_mark, 1)
                pool.tensor_copy(whi[slot][:, :], wraw[slot][:, :]).then_inc(s_pool, 1)
                pool.wait_ge(s_pool, n)
                pool.tensor_tensor(wlo[slot][:, :], wraw[slot][:, :], whi[slot][:, :],
                                   ALU.subtract).then_inc(s_ws, 1)

            def experts(f):
                w0 = (PAIRS + 1) * f
                s0 = (PAIRS + 1) * FF_STEPS * f
                loads = ((PAIRS // 2) * f, (PAIRS // 2 + 1) * f + 1)
                with pool.Fori(0, PAIRS // 2) as i:
                    for s in range(2):
                        pool.wait_ge(s_yd, i * (2 * FF_STEPS) + (s0 + s * FF_STEPS + CR_YD))
                        split(s, i * 2 + (w0 + 2 + s), i * 16 + 16 * (loads[s] + 1))
                pool.wait_ge(s_ws, w0 + PAIRS + 1 + CR_WS)

            def constants(k):
                pool.memset(ones[:, :], 1.0)
                pool.memset(zeros[:, :], 0.0).then_inc(s_init, 1)
                for g in range(2):
                    pool.memset(vb[g][:, :, :], 0.0).then_inc(s_vz, 1)
                for g in range(2):
                    heads = vb[g][:, :, 0:H * VW].rearrange("p t (h c) -> p t h c", c=VW)
                    pool.wait_ge(s_vz, 2 * k + g + 1)
                    pool.memset(heads[:, :, :, HD:HD + 1], 1.0).then_inc(s_iv, 1)

            def prepare_experts(f):
                pool.memset(zr[:, :].bitcast(F32), 0.0)
                pool.memset(one_s[:, :], 1.0).then_inc(s_z, 1)
                split(1, (PAIRS + 1) * f + 1, 16 * ((PAIRS // 2 + 1) * f + 1))

            def cosines(i):
                for g in range(2):
                    pool.wait_ge(s_sq, lap(1, i, g))
                    pool.tensor_tensor(q2[g][:, :], sqq[g][:, :], cst[:, C_COS:C_COS + GT], ALU.mult)
                    pool.tensor_tensor(k2[g][:, :], sqk[g][:, :], cst[:, C_COS:C_COS + GT], ALU.mult
                                       ).then_inc(s_cos, 1)

            pool.sem_inc(s_ws, CR_WS)
            pool.sem_inc(s_w, CR_W)
            constants(0)
            pool.wait_ge(s_iv, 2)
            meet(pool, 1)
            samples_a()
            meet(pool, 2)
            prepare_experts(0)
            pool.wait_ge(s_ws, 1 + CR_WS)
            meet(pool, 3)
            experts(0)
            meet(pool, 4)
            constants(1)
            pool.wait_ge(s_iv, 4)
            groups(pool, cosines)
            pool.wait_ge(s_cos, GROUPS)
            meet(pool, 5)
            meet(pool, 6)
            prepare_experts(1)
            pool.wait_ge(s_ws, PAIRS + 2 + CR_WS)
            meet(pool, 7)
            experts(1)

        @block.vector
        def _(dve):
            st = Steps(dve, s_dve)

            def tile(i, g, j):
                return X[:, bass.ds(i * (2 * GTILES) + (g * GTILES + j), 1), :].rearrange("p a d -> p (a d)")

            def norm_stats(i):
                dve.sem_inc(s_mark, 1)
                for g in range(2):
                    for j in range(GTILES):
                        st.do(dve.bn_stats(stats[g][:, j, :], tile(i, g, j)))
                st.sync_apart(s_mark)
                for g in range(2):
                    for j in range(GTILES):
                        last = dve.bn_aggr(mv[g][:, j, :], stats[g][:, j, :])
                    last.then_inc(s_stat, 1)

            def norm_apply(stage, i, xn_):
                for g in range(2):
                    dve.wait_ge(s_std, lap(stage, i, g))
                    st.do(dve.reciprocal(rstd[g][:, :], std[g][:, :]))
                    st.sync()
                    for j in range(GTILES):
                        last = dve.tensor_scalar(xn_[g][:, j, :], tile(i, g, j), mv[g][:, j, 0:1],
                                                 rstd[g][:, j:j + 1], ALU.subtract, ALU.mult)
                    last.then_inc(s_xn, 1)

            def v_columns(k, i):
                dve.wait_ge(s_iv, 2 * (k + 1))
                for g in range(2):
                    dve.wait_ge(s_qkv, lap(k, i, g))
                    dve.wait_ge(s_scr[g], i * (16 * STORES[k]) + (k * 2 * 16 * STORES[0] + CR_SCR))
                    for j in range(GTILES):
                        o = vb[g][:, j, 0:H * VW].rearrange("p (h c) -> p h c", c=VW)[:, :, 0:HD]
                        v = bank(4 * g + 3)[:, j * P:(j + 1) * P].rearrange("p (h c) -> p h c", c=HD)
                        if k == 0:
                            last = dve.tensor_copy(o, v)
                        else:
                            last = dve.tensor_tensor(o, v, bv_s[:, :].rearrange("p (h c) -> p h c", c=HD), ALU.add)
                    last.then_inc(s_vc, 1)

            def splits_a(i):
                for g in range(2):
                    dve.wait_ge(s_sq, lap(0, i, g))
                    st.do(dve.tensor_tensor(ql[g][:, :], bank(4 * g + 1), qh[g][:, :], ALU.subtract))
                    st.do(dve.scalar_tensor_tensor(kl[g][:, :], bank(4 * g + 2), -2.0, kh[g][:, :],
                                                   ALU.mult, ALU.subtract))
                for g in range(2):
                    dve.wait_ge(s_nh, lap(0, i, g))
                    for row in (0, 32):
                        st.do(dve.tensor_tensor(nl[g][row:row + H, :], ps[row:row + H, 2048 * g:2048 * g + GT],
                                                nh[g][row:row + H, :], ALU.subtract))
                    st.do(dve.tensor_scalar(vb[g][:, :, H * VW:VB],
                                            bank(4 * g + 3)[:, 0:GTILES * H].rearrange("p (t h) -> p t h", h=H),
                                            -1.0, 1.0, ALU.mult, ALU.add))
                    st.sync()
                    dve.sem_inc(s_spl, 1)

            def splits_b(i):
                for g in range(2):
                    dve.wait_ge(s_rot, lap(0, i, g))
                    for r, b in ((0, 4 * g), (1, 4 * g + 3)):
                        st.do(dve.tensor_tensor(rt[g][:, r, :], bank(b), cst[:, C_SIN:C_SIN + GT], ALU.mult))
                    st.sync()
                    dve.wait_ge(s_cos, lap(0, i, g))
                    for r, o in ((0, q2), (1, k2)):
                        st.do(dve.tensor_tensor(o[g][:, :], o[g][:, :], rt[g][:, r, :], ALU.add))
                    st.sync()
                    dve.sem_inc(s_qk2, 1)
                for g in range(2):
                    dve.wait_ge(s_qk2h, lap(0, i, g))
                    for lo, o, hi in ((ql, q2, qh), (kl, k2, kh)):
                        st.do(dve.tensor_tensor(lo[g][:, :], o[g][:, :], hi[g][:, :], ALU.subtract))
                    st.sync()
                    dve.sem_inc(s_spl, 1)

            def prepare_qkv(k):
                splits = (splits_a, splits_b)[k]
                norm_stats(0)
                norm_apply(2 * k, 0, xn)
                v_columns(k, 0)
                if k == 0:
                    dve.wait_ge(s_in, 16 * 9)
                splits(0)
                norm_stats(1)
                norm_apply(2 * k, 1, xn)
                v_columns(k, 1)
                splits(1)

            def samples_a():
                def front(i, n, c):
                    slot = n % 2
                    dve.wait_ge(s_w, after(i, n, CHUNKS, c + 1 - CHUNKS, CR_W))
                    if c == 0:
                        dve.wait_ge(s_ld[slot], (i + n // 2) * (16 * LOADS[0]) + 16 * LOADS[0])
                    for u in (2 * c, 2 * c + 1):
                        for g in range(2):
                            for mt in range(MT):
                                col = ((u % 2) * 2 * MT + g * MT + mt) * N
                                h = 2 * u + g
                                st.do(dve.tensor_scalar(Dt[:, c, col:col + N], abc[slot][:, h, :],
                                                        vbs[slot][:, mt, H * VW + h:H * VW + h + 1], 1e-6,
                                                        ALU.mult, ALU.max))
                    st.sync()
                    dve.wait_ge(s_pv, after(i, n, CHUNKS, c + 1 - CHUNKS, CR_PV))
                    for u in (2 * c, 2 * c + 1):
                        dve.wait_ge(s_s, after(i, n, UNITS, u + 1))
                        b0 = 512 * 2 * (u % 2)
                        at = slice((u % 2) * UC, (u % 2 + 1) * UC)
                        dve.tensor_scalar(Nt[:, c, at], ps[:, b0:b0 + UC], 0.0, None, ALU.max)
                        dve.scalar_tensor_tensor(St[:, c, at], ps[:, b0:b0 + UC], 0.0, Dt[:, c, at],
                                                 ALU.max, ALU.add).then_inc(s_fr, 1)

                def root_sum(i, n, half):
                    c = 2 * half + 1
                    dve.wait_ge(s_rt, after(i, n, CHUNKS, c + 1))
                    dve.tensor_tensor(Nt[:, c, :], Nt[:, c, :], St[:, c, :], ALU.add).then_inc(s_y, 1)

                def copy_out(i, n):
                    slot = n % 2
                    dve.wait_ge(s_pv, after(i, n, CHUNKS, CHUNKS, CR_PV))
                    dve.wait_ge(s_os[slot], (i + n // 2) * (4 * 16) + CR_OS)
                    b0 = 512 * (4 + 2 * slot)
                    dve.tensor_copy(osb[slot][:, :], ps[:, b0:b0 + 2 * 512]).then_inc(s_ev, 1)

                def step(i, n, first=False, last=False):
                    front(i, n, 2)
                    root_sum(i, n, 0)
                    front(i, n, 3)
                    if not first:
                        copy_out(i, n - 1)
                    if not last:
                        front(i, n + 1, 0)
                    root_sum(i, n, 1)
                    if not last:
                        front(i, n + 1, 1)

                front(0, 0, 0)
                front(0, 0, 1)
                for g in range(2):
                    dve.wait_ge(s_scr[g], 2 * 16 * STORES[0] + CR_SCR)
                step(0, 0, first=True)
                with dve.Fori(0, B // 2 - 1) as i:
                    st.enter(i, 2 * UNITS * 2 * MT)
                    step(i, 1)
                    step(i, 2)
                st.leave(B // 2 - 1)
                step(B // 2 - 1, 1, last=True)
                copy_out(B // 2 - 1, 1)
                dve.wait_ge(s_ev, B + CR_EV)

            def samples_b():
                def head_max(i, slot, u, g):
                    dve.wait_ge(s_s1, after_b(i, slot, H, 2 * u + g + 1))
                    dve.tensor_reduce(mx[:, u // HALF, :, g * HALF + u % HALF],
                                      bank(4 + g).rearrange("p (t m) -> p t m", t=MT), AX_X, ALU.max
                                      ).then_inc(s_mx, 1)

                def split_max(i, slot, half):
                    dve.wait_ge(s_mx, after_b(i, slot, H, 2 * HALF * (half + 1), CR_MX))
                    st.do(dve.tensor_copy(mxh_r[:, half, :, :], mx[:, half, :, :]))
                    st.sync()
                    whole = mx[:, half, :, :].rearrange("p t (g u) -> p t g u", g=2)
                    high = mxh_r[:, half, :, :].bitcast(F32).rearrange("p t (g u) -> p t g u", g=2)
                    dve.tensor_scalar(mxs[:, half, :, :, 0, :], high, -1.0, None, ALU.mult)
                    dve.tensor_tensor(mxs[:, half, :, :, 1, :], high, whole, ALU.subtract).then_inc(s_ms, 1)

                def maxima(i, slot):
                    for u in range(UNITS):
                        if u % HALF == 0:
                            dve.wait_ge(s_mT, after_b(i, slot, 2, u // HALF - 1, CR_MT))
                        for g in range(2):
                            head_max(i, slot, u, g)
                        if u % HALF == HALF - 1:
                            split_max(i, slot, u // HALF)

                def step(i, slot, last):
                    if not last:
                        maxima(i + (slot + 1) // SLOTS_B, (slot + 1) % SLOTS_B)

                maxima(0, 0)
                samples_of_b(dve, step, lambda i: st.enter(i, SLOTS_B * 2), lambda: st.leave(B // SLOTS_B))
                dve.wait_ge(s_ms, 2 * B)

            def divide(f, i):
                for g in range(2):
                    dve.wait_ge(s_oP, lap(f, i, g) + CR_OP)
                    b = 2048 * g
                    if f == 0:
                        raw = ps[:, b:b + 1024].rearrange("p (t x) -> p t x", x=OW0)[:, :, 0:CHUNKS * OR]
                        raw = raw.rearrange("p t (h c) -> p t h c", h=H)
                    else:
                        raw = ps[:, b:b + 1024].rearrange("p (l x) -> p l x", x=OW1)[:, :, 0:OR]
                        raw = raw.rearrange("p l (g c) -> p g l c", g=GTILES)
                    st.do(dve.reciprocal(rden[g][:, :, :], raw[:, :, :, HD]))
                    st.sync()
                    dve.tensor_tensor(otok[g][:, :, :].rearrange("p t (h c) -> p t h c", c=HD), raw[:, :, :, 0:HD],
                                      rden[g][:, :, :].unsqueeze(3).broadcast_to([P, GTILES, H, HD]),
                                      ALU.mult).then_inc(s_on, 1)

            def residual(f, i):
                for g in range(2):
                    dve.wait_ge(s_wo, lap(f, i, g))
                    xg = X[:, group(i, g, GTILES), :]
                    st.do(dve.tensor_tensor(xg, xg, bank(4 * g + 1).rearrange("p (t d) -> p t d", d=P), ALU.add))
                    st.sync()
                    if f == 1:
                        st.do(dve.tensor_tensor(xg, xg, pb_s[:, :].unsqueeze(1).broadcast_to([P, GTILES, P]),
                                                ALU.add))
                        st.sync()

            def route(f, i):
                def step(*instructions):
                    st.do(instructions[-1])
                    st.sync()

                def tiles(op):
                    for j in range(LT):
                        last = op(j)
                    step(last)

                dve.wait_ge(s_sc, lap(f, i, 1))
                step(dve.tensor_tensor(sfc[:, :, :], sc[:, :, :],
                                       eb_s[:, :].unsqueeze(1).broadcast_to([P, LT, E]), ALU.add))
                v = sfc[:, :, :].rearrange("p t (k e) -> p (t k) e", e=8)
                step(dve.tensor_tensor(top[0][:, :, :], v[:, :, 0:4], v[:, :, 4:8], ALU.max),
                     dve.tensor_tensor(second[0][:, :, :], v[:, :, 0:4], v[:, :, 4:8], ALU.min))
                for k, w in ((0, 2), (1, 1)):
                    t, s2 = top[k], second[k]
                    step(dve.tensor_tensor(top[k + 1][:, :, :], t[:, :, 0:w], t[:, :, w:2 * w], ALU.max),
                         dve.tensor_tensor(lesser[k][:, :, :], t[:, :, 0:w], t[:, :, w:2 * w], ALU.min),
                         dve.tensor_tensor(second[k + 1][:, :, :], s2[:, :, 0:w], s2[:, :, w:2 * w], ALU.max))
                    step(dve.tensor_tensor(second[k + 1][:, :, :], second[k + 1][:, :, :], lesser[k][:, :, :], ALU.max))
                step(dve.tensor_tensor(gs[:, :, 0:8], top[2][:, :, :].rearrange("p (t k) e -> p t (k e)", k=8),
                                       second[2][:, :, :].rearrange("p (t k) e -> p t (k e)", k=8), ALU.add))
                tiles(lambda j: dve.max(g8[:, j, :], gs[:, j, :]))
                tiles(lambda j: dve.match_replace(gr[:, j, :], g8[:, j, :], gs[:, j, :], -BIG))
                step(dve.tensor_scalar(gm[:, :, :], gr[:, :, 0:8], -BIG, None, ALU.is_equal))
                step(dve.tensor_tensor(mk[:, :, :].rearrange("p t (g e) -> p (t g) e", e=8), v,
                                       gm[:, :, :].rearrange("p t g -> p (t g)").unsqueeze(2)
                                       .broadcast_to([P, LT * 8, 8]), ALU.mult))
                step(dve.tensor_scalar(mk[:, :, :], mk[:, :, :], 0.0, None, ALU.add))
                tiles(lambda j: dve.max(k8[:, j, :], mk[:, j, :]))
                tiles(lambda j: dve.match_replace(mr[:, j, :], k8[:, j, :], mk[:, j, :], -BIG))
                step(dve.scalar_tensor_tensor(wsel[:, :, :], mr[:, :, :], -BIG, sc[:, :, :], ALU.is_equal, ALU.mult))
                step(dve.tensor_reduce(wsum[:, :], wsel[:, :, :], AX_X, ALU.add))
                step(dve.tensor_scalar(wsum[:, :], wsum[:, :], 1e-20, None, ALU.add))
                step(dve.reciprocal(wrec[:, :], wsum[:, :]))
                dve.scalar_tensor_tensor(coef[:, :, :], wsel[:, :, :], ROUTE_SCALE,
                                         wrec[:, :].unsqueeze(2).broadcast_to([P, LT, E]),
                                         ALU.mult, ALU.mult).then_inc(s_cf, 1)

            def marks():
                st.do(dve.memset(gs[:, :, 8:12], BIG))

            def lows(f, i):
                for g in range(2):
                    dve.wait_ge(s_xh, lap(f, i, g))
                    st.do(dve.tensor_tensor(xl[:, group(i, g)], f_xT[g][:, :], xh[:, group(i, g)], ALU.subtract))

            def prepare_f(f):
                marks()
                divide(f, 0)
                residual(f, 0)
                norm_stats(0)
                norm_apply(2 * f + 1, 0, f_xn)
                divide(f, 1)
                lows(f, 0)
                residual(f, 1)
                norm_stats(1)
                route(f, 0)
                norm_apply(2 * f + 1, 1, f_xn)
                lows(f, 1)
                route(f, 1)

            def experts(f):
                s0 = (PAIRS + 1) * FF_STEPS * f
                def gate_up(n, c):
                    dve.wait_ge(s_sg, n + 1)
                    dve.wait_ge(s_u, n + 1)
                    dve.tensor_tensor(h1[c % 2][:, :], sg[c % 2][:, :], bank(5 + 2 * (c % 2)), ALU.mult
                                      ).then_inc(s_h1, 1)

                def low(n, c):
                    dve.wait_ge(s_hh, n)
                    dve.wait_ge(s_yd, n - FF_STEPS + CR_YD)
                    dve.tensor_tensor(hl[c][:, :], hf[c % 2][:, :], hh[c][:, :], ALU.subtract).then_inc(s_hl, 1)

                def weigh(n, c, coefs):
                    dve.wait_ge(s_h1, n + 1)
                    dve.wait_ge(s_hl, n - 1 + CR_HL)
                    dve.tensor_tensor(hf[c % 2][:, :], h1[c % 2][:, :], coefs, ALU.mult).then_inc(s_h, 1)

                dve.wait_ge(s_z, f + 1)
                for c in range(FF_STEPS):
                    gate_up(s0 + c, c)
                    if c >= 1:
                        low(s0 + c, c - 1)
                    weigh(s0 + c, c, one_s[:, :])
                with dve.Fori(0, PAIRS // 2) as i:
                    for s in range(2):
                        for c in range(FF_STEPS):
                            n = i * (2 * FF_STEPS) + (s0 + (s + 1) * FF_STEPS + c)
                            gate_up(n, c)
                            low(n, (c - 1) % FF_STEPS)
                            if c == 0:
                                dve.wait_ge(s_cl[s], i * 32 + (16 * PAIRS * f + 32))
                            weigh(n, c, cbc[s][:, c * FF_TOK:(c + 1) * FF_TOK])
                end = s0 + (PAIRS + 1) * FF_STEPS
                low(end, FF_STEPS - 1)
                for c in range(FF_STEPS):
                    dve.wait_ge(s_yP, FF_STEPS * f + c + 1)
                    xg = X[:, c * GTILES:(c + 1) * GTILES, :]
                    dve.tensor_tensor(xg, xg, bank(4 + c).rearrange("p (t d) -> p t d", d=P),
                                      ALU.add).then_inc(s_res, 1)
                dve.wait_ge(s_res, FF_STEPS * (f + 1))

            dve.sem_inc(s_ev, CR_EV)
            dve.sem_inc(s_hl, CR_HL)
            dve.sem_inc(s_h, CR_H)
            dve.sem_inc(s_spl, CR_SPL)
            dve.sem_inc(s_mx, CR_MX)
            st.do(dve.memset(eps_s[:, :], 1e-5))
            st.sync()
            dve.sem_inc(s_eps, 1)
            dve.wait_ge(s_x, 16)
            prepare_qkv(0)
            meet(dve, 1)
            samples_a()
            meet(dve, 2)
            prepare_f(0)
            meet(dve, 3)
            experts(0)
            meet(dve, 4)
            prepare_qkv(1)
            meet(dve, 5)
            samples_b()
            meet(dve, 6)
            prepare_f(1)
            meet(dve, 7)
            experts(1)


_OUTS = [((8, 256, 128), "float32")]


def _feature_order():
    import numpy as np
    g, d, u = (a.ravel() for a in np.meshgrid(np.arange(2), np.arange(HD), np.arange(UNITS), indexing="ij"))
    head = 2 * u + g
    return head * HD + d, head, d


def _constants():
    import numpy as np
    c = np.zeros((P, C_END), np.float32)
    c[:, C_ID:C_ID + P] = np.eye(P, dtype=np.float32)
    _, head, d = _feature_order()
    c[np.arange(P), C_HS + head] = 1.0
    half = HD // 2
    for f in range(P):
        if d[f] < half:
            c[f + half * UNITS, C_ROT + f] = -1.0
        else:
            c[f - half * UNITS, C_ROT + f] = 1.0
    freq = (1.0 / 10000.0 ** (np.arange(0, HD, 2, dtype=np.float32) / HD)).astype(np.float32)
    pos = (np.arange(GT) % N).astype(np.float32)
    ang = (freq[d % half][:, None] * pos[None, :]).astype(np.float32)
    c[:, C_COS:C_COS + GT] = np.cos(ang)
    c[:, C_SIN:C_SIN + GT] = np.sin(ang)
    return c


def _layout(w):
    import numpy as np
    w = {k.replace("L0_", ""): np.ascontiguousarray(v) for k, v in w.items()}
    consts = _constants()
    order = _feature_order()[0]
    wA = np.concatenate([w["attn_a_Wq"][order].T, w["attn_a_Wk"][order].T, w["attn_a_Wv"].T, w["attn_a_Wo"].T], axis=1)
    qkv_w = w["attn_b_qkv_w"].reshape(3, P, P)
    wB = np.concatenate([qkv_w[0][order].T, qkv_w[1][order].T, qkv_w[2].T, w["attn_b_proj_w"].T], axis=1)
    bqk = w["attn_b_qkv_b"][:2 * P].reshape(2, P)[:, order].T
    brow = np.concatenate([w["attn_b_qkv_b"][2 * P:], w["attn_b_proj_b"], w["ffn_e_bias"]])[None]
    wexp = np.zeros((PAIRS + 1, P, 3 * P), np.float32)
    for k, n in enumerate(("ffn_Wg", "ffn_Wu")):
        wexp[:PAIRS, :, k * P:(k + 1) * P] = w[n].reshape(PAIRS, 2, P, I).transpose(0, 2, 1, 3).reshape(PAIRS, P, P)
    wexp[:PAIRS, :, 2 * P:3 * P] = w["ffn_Wd"].reshape(PAIRS, P, P)
    for k, n in enumerate(("ffn_SWg", "ffn_SWu", "ffn_SWd")):
        wexp[PAIRS, :, k * P:(k + 1) * P] = w[n]
    return {"x": w["attn_a_x"], "consts": consts, "wA": wA, "wB": wB, "bqk": bqk,
            "brow": brow, "rwT": w["ffn_router_w"].T, "wexp": wexp}


def kernel(**inputs):
    import numpy as _np
    import concourse.bacc as _bacc
    from concourse import mybir as _mybir
    from concourse.bass_utils import run_bass_kernel_spmd as _run

    nc = _bacc.Bacc("TRN2", target_bir_lowering=False, num_devices=1)
    arrays, args = {}, []
    for name, a in _layout(inputs).items():
        a = _np.ascontiguousarray(a)
        arrays[f"in_{name}_dram"] = a
        args.append(nc.dram_tensor(f"in_{name}_dram", a.shape, _mybir.dt.from_np(a.dtype), kind="ExternalInput").ap())
    for i, (shape, dtype) in enumerate(_OUTS):
        dt = _mybir.dt.from_np(_np.dtype(dtype))
        args.append(nc.dram_tensor(f"out_{i}_dram", shape, dt, kind="ExternalOutput").ap())
    hybrid(nc, *args)
    r = _run(nc, [arrays], core_ids=[0])
    return r.results[0]["out_0_dram"]
```
